# Optimizing a Trainium2 kernel written in Bass

```python
import numpy as np
import jax
import jax.numpy as jnp

def _softmax(x, axis=-1):
    return jax.nn.softmax(x, axis=axis)

def _gelu(x):
    return jax.nn.gelu(x, approximate=True)

def _silu(x):
    return jax.nn.silu(x)

def _sigmoid(x):
    return jax.nn.sigmoid(x)

def _layernorm(x, axis=-1, eps=1e-05):
    m = jnp.mean(x, axis=axis, keepdims=True)
    v = jnp.var(x, axis=axis, keepdims=True)
    return (x - m) / jnp.sqrt(v + eps)

def _scatter_add(tgt, idx, src, axis=0):
    return tgt.at[idx].add(src)

def _segment_sum(src, seg, n):
    return jax.ops.segment_sum(src, seg, n)
kernel_name = 'mk_prb_d4_jaxref_r8_daffb6'

def setup_inputs(seed: int=0):
    np.random.seed(seed)
    _w = jnp.asarray

    def _L0_attn_setup():
        import jax, jax.numpy as jnp
        import numpy as np
        B, N, D = (4, 256, 128)
        H = 16
        HD = D // H
        SCALE = 1.0 / HD
        NEG = -10000.0
        THETA = 10000.0

        def _rope(t):
            d, n = (t.shape[-1], t.shape[-2])
            inv_freq = 1.0 / THETA ** (jnp.arange(0, d, 2, dtype=jnp.float32) / d)
            ang = jnp.arange(n, dtype=jnp.float32)[:, None] * inv_freq[None, :]
            cos = jnp.repeat(jnp.cos(ang), 2, axis=-1)
            sin = jnp.repeat(jnp.sin(ang), 2, axis=-1)
            x1, x2 = (t[..., ::2], t[..., 1::2])
            rot = jnp.stack([-x2, x1], axis=-1).reshape(t.shape)
            return t * cos + rot * sin
        key = jax.random.key(seed)
        ks = jax.random.split(key, 6)
        s = (1.0 / D) ** 0.5
        return {'x': jax.random.normal(ks[0], (B, N, D), jnp.float32), 'Wq': jax.random.normal(ks[1], (D, D), jnp.float32) * s, 'Wk': jax.random.normal(ks[2], (D, D), jnp.float32) * s, 'Wv': jax.random.normal(ks[3], (D, D), jnp.float32) * s, 'Wo': jax.random.normal(ks[4], (D, D), jnp.float32) * s, 'bo': jnp.zeros((D,), jnp.float32)}
    _L0_attn_in = _L0_attn_setup()

    def _L0_ffn_setup():
        import jax, jax.numpy as jnp
        import numpy as np
        B, S, IN, OUT = (4, 1024, 128, 128)
        EPS = 1e-06

        def _xla_quantized_matmul(x2d, weight_q, weight_scale):
            amax = jnp.max(jnp.abs(x2d), axis=-1, keepdims=True)
            x_scale = jnp.maximum(amax, EPS) / 127.0
            x_q = jnp.clip(jnp.round(x2d / x_scale), -128, 127).astype(jnp.int8)
            acc = jax.lax.dot_general(x_q, weight_q, (((1,), (1,)), ((), ())), preferred_element_type=jnp.int32)
            return acc.astype(jnp.float32) * x_scale * weight_scale[None, :]
        key = jax.random.key(seed)
        k1, k2, k3, k4 = jax.random.split(key, 4)
        x = jax.random.normal(k1, (B, S, IN), dtype=jnp.float32)
        weight_q = jax.random.randint(k2, (OUT, IN), -128, 128, dtype=jnp.int32).astype(jnp.int8)
        weight_scale = jax.random.uniform(k3, (OUT,), dtype=jnp.float32, minval=0.001, maxval=0.01)
        bias = jax.random.normal(k4, (OUT,), dtype=jnp.float32) * 0.01
        return {'x': x, 'weight_q': weight_q, 'weight_scale': weight_scale, 'bias': bias}
    _L0_ffn_in = _L0_ffn_setup()

    def _L1_attn_setup():
        import jax, jax.numpy as jnp
        import numpy as np
        B, S, D, H = (4, 256, 128, 16)
        HD = D // H

        def rope(x):
            d = x.shape[-1]
            inv_freq = 1.0 / 10000.0 ** (jnp.arange(0, d, 2, dtype=jnp.float32) / d)
            pos = jnp.arange(x.shape[1], dtype=jnp.float32)
            ang = pos[:, None] * inv_freq[None, :]
            cos, sin = (jnp.cos(ang), jnp.sin(ang))
            x1, x2 = (x[..., 0::2], x[..., 1::2])
            r1 = x1 * cos - x2 * sin
            r2 = x1 * sin + x2 * cos
            return jnp.stack([r1, r2], axis=-1).reshape(x.shape)
        key = jax.random.key(seed)
        ks = jax.random.split(key, 9)
        s = 1.0 / np.sqrt(D)

        def lin(k):
            kw, kb = jax.random.split(k)
            W = jax.random.uniform(kw, (D, D), jnp.float32, -s, s)
            b = jax.random.uniform(kb, (D,), jnp.float32, -s, s)
            return (W, b)
        Wq, bq = lin(ks[0])
        Wk, bk = lin(ks[1])
        Wv, bv = lin(ks[2])
        W0, b0 = lin(ks[3])
        x = jax.random.normal(ks[4], (B, S, D), jnp.float32)
        return {'x': x, 'Wq': Wq, 'bq': bq, 'Wk': Wk, 'bk': bk, 'Wv': Wv, 'bv': bv, 'W0': W0, 'b0': b0}
    _L1_attn_in = _L1_attn_setup()

    def _L1_ffn_setup():
        import jax, jax.numpy as jnp
        import numpy as np
        EMB = 128
        FF = 4 * EMB

        def _ternary(w):
            scale = jnp.maximum(jnp.mean(jnp.abs(w)), 1e-08)
            w_t = jnp.clip(jnp.round(w / scale), -1.0, 1.0)
            return w + jax.lax.stop_gradient(w_t - w)
        key = jax.random.key(seed)
        kx, k1, k2, kb1, kb2 = jax.random.split(key, 5)
        x = jax.random.normal(kx, (4, 256, EMB), dtype=jnp.float32)
        lim1 = 1.0 / np.sqrt(EMB)
        lim2 = 1.0 / np.sqrt(FF)
        W1 = jax.random.uniform(k1, (FF, EMB), jnp.float32, -lim1, lim1)
        b1 = jax.random.uniform(kb1, (FF,), jnp.float32, -lim1, lim1)
        W2 = jax.random.uniform(k2, (EMB, FF), jnp.float32, -lim2, lim2)
        b2 = jax.random.uniform(kb2, (EMB,), jnp.float32, -lim2, lim2)
        return {'x': x, 'W1': W1, 'b1': b1, 'W2': W2, 'b2': b2}
    _L1_ffn_in = _L1_ffn_setup()

    def _L2_attn_setup():
        import jax, jax.numpy as jnp
        import numpy as np
        B, S, E = (4, 512, 128)
        CHUNK = 32
        key = jax.random.key(seed)
        ks = jax.random.split(key, 9)
        sd = 1.0 / np.sqrt(E)
        x = jax.random.normal(ks[0], (B, S, E), dtype=jnp.float32)
        Wq = jax.random.normal(ks[1], (E, E), dtype=jnp.float32) * sd
        Wk = jax.random.normal(ks[2], (E, E), dtype=jnp.float32) * sd
        Wv = jax.random.normal(ks[3], (E, E), dtype=jnp.float32) * sd
        Wo = jax.random.normal(ks[4], (E, E), dtype=jnp.float32) * sd
        bq = jax.random.normal(ks[5], (E,), dtype=jnp.float32) * 0.01
        bk = jax.random.normal(ks[6], (E,), dtype=jnp.float32) * 0.01
        bv = jax.random.normal(ks[7], (E,), dtype=jnp.float32) * 0.01
        bo = jax.random.normal(ks[8], (E,), dtype=jnp.float32) * 0.01
        return {'x': x, 'Wq': Wq, 'bq': bq, 'Wk': Wk, 'bk': bk, 'Wv': Wv, 'bv': bv, 'Wo': Wo, 'bo': bo}
    _L2_attn_in = _L2_attn_setup()

    def _L2_ffn_setup():
        import jax, jax.numpy as jnp
        import numpy as np
        TOP_K = 4
        CAP_FACTOR = 4

        def swiglu(x, w1, w2, w3):
            return jax.nn.silu(x @ w1) * (x @ w3) @ w2
        key = jax.random.key(seed)
        ks = jax.random.split(key, 8)
        B, S, D, H, E = (2, 256, 128, 64, 32)
        Hs = 2 * H
        sd = lambda *sh: 1.0 / np.sqrt(sh[-2])
        x = jax.random.normal(ks[0], (B, S, D), dtype=jnp.float32)
        Wg = jax.random.normal(ks[1], (D, E), dtype=jnp.float32) * (1.0 / np.sqrt(D))
        W1 = jax.random.normal(ks[2], (E, D, H), dtype=jnp.float32) * (1.0 / np.sqrt(D))
        W3 = jax.random.normal(ks[3], (E, D, H), dtype=jnp.float32) * (1.0 / np.sqrt(D))
        W2 = jax.random.normal(ks[4], (E, H, D), dtype=jnp.float32) * (1.0 / np.sqrt(H))
        Ws1 = jax.random.normal(ks[5], (D, Hs), dtype=jnp.float32) * (1.0 / np.sqrt(D))
        Ws3 = jax.random.normal(ks[6], (D, Hs), dtype=jnp.float32) * (1.0 / np.sqrt(D))
        Ws2 = jax.random.normal(ks[7], (Hs, D), dtype=jnp.float32) * (1.0 / np.sqrt(Hs))
        return {'x': x, 'Wg': Wg, 'W1': W1, 'W2': W2, 'W3': W3, 'Ws1': Ws1, 'Ws2': Ws2, 'Ws3': Ws3}
    _L2_ffn_in = _L2_ffn_setup()

    def _L3_attn_setup():
        import jax, jax.numpy as jnp
        import numpy as np
        NUM_HEADS = 16
        KEY_DIM = 64
        UPDATE_STEPS_MAX = 3
        UPDATE_STEPS_EPS = 0.0001
        LN_EPS = 1e-05
        B, S, DIM = (4, 128, 128)
        INNER = NUM_HEADS * KEY_DIM

        def _glorot(key, shape):
            fan_in, fan_out = (shape[0], shape[1])
            lim = jnp.sqrt(6.0 / (fan_in + fan_out))
            return jax.random.uniform(key, shape, jnp.float32, -lim, lim)

        def _layernorm(t, gamma, beta):
            mu = jnp.mean(t, axis=-1, keepdims=True)
            var = jnp.mean(jnp.square(t - mu), axis=-1, keepdims=True)
            return (t - mu) * jax.lax.rsqrt(var + LN_EPS) * gamma + beta

        def _heads(t):
            b, s, _ = t.shape
            return t.reshape(b, s, NUM_HEADS, KEY_DIM).transpose(0, 2, 1, 3)
        key = jax.random.key(seed)
        ks = jax.random.split(key, 6)
        return {'x': jax.random.normal(ks[0], (B, S, DIM), jnp.float32), 'Wq': _glorot(ks[1], (DIM, INNER)), 'bq': jnp.zeros((INNER,), jnp.float32), 'Wk': _glorot(ks[2], (DIM, INNER)), 'bk': jnp.zeros((INNER,), jnp.float32), 'Wv': _glorot(ks[3], (DIM, INNER)), 'bv': jnp.zeros((INNER,), jnp.float32), 'Wo': _glorot(ks[4], (INNER, DIM)), 'bo': jnp.zeros((DIM,), jnp.float32), 'gamma': jnp.ones((KEY_DIM,), jnp.float32), 'beta': jnp.zeros((KEY_DIM,), jnp.float32)}
    _L3_attn_in = _L3_attn_setup()

    def _L3_ffn_setup():
        import jax, jax.numpy as jnp
        import numpy as np
        B, N, D = (4, 512, 128)
        E, S, F = (16, 64, 256)
        DO = 128
        EPS = 1e-05

        def _layernorm(x, g, b):
            mu = jnp.mean(x, axis=-1, keepdims=True)
            var = jnp.mean(jnp.square(x - mu), axis=-1, keepdims=True)
            return (x - mu) * jax.lax.rsqrt(var + EPS) * g + b
        key = jax.random.key(seed)
        ks = jax.random.split(key, 8)
        d = {'x': jax.random.normal(ks[0], (B, N, D), dtype=jnp.float32), 'norm_g': jnp.ones((D,), jnp.float32), 'norm_b': jnp.zeros((D,), jnp.float32), 'slot_g': jnp.ones((D,), jnp.float32), 'slot_b': jnp.zeros((D,), jnp.float32), 'scale': jnp.ones((1,), jnp.float32), 'slot_embeds': jax.random.normal(ks[1], (E, S, D), jnp.float32) / np.sqrt(D), 'Wg': jax.random.normal(ks[2], (E, D, F), jnp.float32) * np.sqrt(2.0 / (D + F)), 'bg': jnp.zeros((E, F), jnp.float32), 'Wu': jax.random.normal(ks[3], (E, D, F), jnp.float32) * np.sqrt(2.0 / (D + F)), 'bu': jnp.zeros((E, F), jnp.float32), 'Wd': jax.random.normal(ks[4], (E, F, DO), jnp.float32) * np.sqrt(2.0 / (F + DO)), 'bd': jnp.zeros((E, DO), jnp.float32)}
        return d
    _L3_ffn_in = _L3_ffn_setup()
    _d = {'L0_attn_x': _L0_attn_in['x'], 'L0_attn_Wq': _L0_attn_in['Wq'], 'L0_attn_Wk': _L0_attn_in['Wk'], 'L0_attn_Wv': _L0_attn_in['Wv'], 'L0_attn_Wo': _L0_attn_in['Wo'], 'L0_attn_bo': _L0_attn_in['bo'], 'L0_ffn_weight_q': _L0_ffn_in['weight_q'], 'L0_ffn_weight_scale': _L0_ffn_in['weight_scale'], 'L0_ffn_bias': _L0_ffn_in['bias'], 'L1_attn_Wq': _L1_attn_in['Wq'], 'L1_attn_bq': _L1_attn_in['bq'], 'L1_attn_Wk': _L1_attn_in['Wk'], 'L1_attn_bk': _L1_attn_in['bk'], 'L1_attn_Wv': _L1_attn_in['Wv'], 'L1_attn_bv': _L1_attn_in['bv'], 'L1_attn_W0': _L1_attn_in['W0'], 'L1_attn_b0': _L1_attn_in['b0'], 'L1_ffn_W1': _L1_ffn_in['W1'], 'L1_ffn_b1': _L1_ffn_in['b1'], 'L1_ffn_W2': _L1_ffn_in['W2'], 'L1_ffn_b2': _L1_ffn_in['b2'], 'L2_attn_Wq': _L2_attn_in['Wq'], 'L2_attn_bq': _L2_attn_in['bq'], 'L2_attn_Wk': _L2_attn_in['Wk'], 'L2_attn_bk': _L2_attn_in['bk'], 'L2_attn_Wv': _L2_attn_in['Wv'], 'L2_attn_bv': _L2_attn_in['bv'], 'L2_attn_Wo': _L2_attn_in['Wo'], 'L2_attn_bo': _L2_attn_in['bo'], 'L2_ffn_Wg': _L2_ffn_in['Wg'], 'L2_ffn_W1': _L2_ffn_in['W1'], 'L2_ffn_W2': _L2_ffn_in['W2'], 'L2_ffn_W3': _L2_ffn_in['W3'], 'L2_ffn_Ws1': _L2_ffn_in['Ws1'], 'L2_ffn_Ws2': _L2_ffn_in['Ws2'], 'L2_ffn_Ws3': _L2_ffn_in['Ws3'], 'L3_attn_Wq': _L3_attn_in['Wq'], 'L3_attn_bq': _L3_attn_in['bq'], 'L3_attn_Wk': _L3_attn_in['Wk'], 'L3_attn_bk': _L3_attn_in['bk'], 'L3_attn_Wv': _L3_attn_in['Wv'], 'L3_attn_bv': _L3_attn_in['bv'], 'L3_attn_Wo': _L3_attn_in['Wo'], 'L3_attn_bo': _L3_attn_in['bo'], 'L3_attn_gamma': _L3_attn_in['gamma'], 'L3_attn_beta': _L3_attn_in['beta'], 'L3_ffn_norm_g': _L3_ffn_in['norm_g'], 'L3_ffn_norm_b': _L3_ffn_in['norm_b'], 'L3_ffn_slot_g': _L3_ffn_in['slot_g'], 'L3_ffn_slot_b': _L3_ffn_in['slot_b'], 'L3_ffn_scale': _L3_ffn_in['scale'], 'L3_ffn_slot_embeds': _L3_ffn_in['slot_embeds'], 'L3_ffn_Wg': _L3_ffn_in['Wg'], 'L3_ffn_bg': _L3_ffn_in['bg'], 'L3_ffn_Wu': _L3_ffn_in['Wu'], 'L3_ffn_bu': _L3_ffn_in['bu'], 'L3_ffn_Wd': _L3_ffn_in['Wd'], 'L3_ffn_bd': _L3_ffn_in['bd']}
    _x0 = _d['L0_attn_x']
    _d['L0_attn_x'] = jax.random.normal(jax.random.fold_in(jax.random.key(seed), 1), (16, 256, 128), dtype=_x0.dtype)
    del _x0
    return _d

def reference(L0_attn_x, L0_attn_Wq, L0_attn_Wk, L0_attn_Wv, L0_attn_Wo, L0_attn_bo, L0_ffn_weight_q, L0_ffn_weight_scale, L0_ffn_bias, L1_attn_Wq, L1_attn_bq, L1_attn_Wk, L1_attn_bk, L1_attn_Wv, L1_attn_bv, L1_attn_W0, L1_attn_b0, L1_ffn_W1, L1_ffn_b1, L1_ffn_W2, L1_ffn_b2, L2_attn_Wq, L2_attn_bq, L2_attn_Wk, L2_attn_bk, L2_attn_Wv, L2_attn_bv, L2_attn_Wo, L2_attn_bo, L2_ffn_Wg, L2_ffn_W1, L2_ffn_W2, L2_ffn_W3, L2_ffn_Ws1, L2_ffn_Ws2, L2_ffn_Ws3, L3_attn_Wq, L3_attn_bq, L3_attn_Wk, L3_attn_bk, L3_attn_Wv, L3_attn_bv, L3_attn_Wo, L3_attn_bo, L3_attn_gamma, L3_attn_beta, L3_ffn_norm_g, L3_ffn_norm_b, L3_ffn_slot_g, L3_ffn_slot_b, L3_ffn_scale, L3_ffn_slot_embeds, L3_ffn_Wg, L3_ffn_bg, L3_ffn_Wu, L3_ffn_bu, L3_ffn_Wd, L3_ffn_bd):

    def _L0_attn_ref(x, Wq, Wk, Wv, Wo, bo):
        import jax, jax.numpy as jnp
        import numpy as np
        B, N, D = (4, 256, 128)
        H = 16
        HD = D // H
        SCALE = 1.0 / HD
        NEG = -10000.0
        THETA = 10000.0

        def _rope(t):
            d, n = (t.shape[-1], t.shape[-2])
            inv_freq = 1.0 / THETA ** (jnp.arange(0, d, 2, dtype=jnp.float32) / d)
            ang = jnp.arange(n, dtype=jnp.float32)[:, None] * inv_freq[None, :]
            cos = jnp.repeat(jnp.cos(ang), 2, axis=-1)
            sin = jnp.repeat(jnp.sin(ang), 2, axis=-1)
            x1, x2 = (t[..., ::2], t[..., 1::2])
            rot = jnp.stack([-x2, x1], axis=-1).reshape(t.shape)
            return t * cos + rot * sin
        b, n, _ = x.shape
        q = (x @ Wq.T).reshape(b, n, H, HD).transpose(0, 2, 1, 3)
        k = (x @ Wk.T).reshape(b, n, H, HD).transpose(0, 2, 1, 3)
        v = (x @ Wv.T).reshape(b, n, H, HD).transpose(0, 2, 1, 3)
        q = _rope(q)
        k = _rope(k)
        i = jnp.arange(n)
        add_mask = jnp.where(i[:, None] >= i[None, :], 0.0, NEG).astype(x.dtype)
        scores = jnp.einsum('bhqd,bhkd->bhqk', q, k) * SCALE + add_mask
        attn = jax.nn.softmax(scores, axis=-1)
        out = jnp.einsum('bhqk,bhkd->bhqd', attn, v)
        out = out.transpose(0, 2, 1, 3).reshape(b, n, H * HD)
        return out @ Wo.T + bo

    def _L0_ffn_ref(x, weight_q, weight_scale, bias):
        import jax, jax.numpy as jnp
        import numpy as np
        B, S, IN, OUT = (4, 1024, 128, 128)
        EPS = 1e-06

        def _xla_quantized_matmul(x2d, weight_q, weight_scale):
            amax = jnp.max(jnp.abs(x2d), axis=-1, keepdims=True)
            x_scale = jnp.maximum(amax, EPS) / 127.0
            x_q = jnp.clip(jnp.round(x2d / x_scale), -128, 127).astype(jnp.int8)
            acc = jax.lax.dot_general(x_q, weight_q, (((1,), (1,)), ((), ())), preferred_element_type=jnp.int32)
            return acc.astype(jnp.float32) * x_scale * weight_scale[None, :]
        orig_shape = x.shape
        x2d = x.reshape(-1, orig_shape[-1])
        out = _xla_quantized_matmul(x2d, weight_q, weight_scale)
        out = out.reshape(*orig_shape[:-1], out.shape[-1])
        out = out + bias
        return out

    def _L1_attn_ref(x, Wq, bq, Wk, bk, Wv, bv, W0, b0):
        import jax, jax.numpy as jnp
        import numpy as np
        B, S, D, H = (4, 256, 128, 16)
        HD = D // H

        def rope(x):
            d = x.shape[-1]
            inv_freq = 1.0 / 10000.0 ** (jnp.arange(0, d, 2, dtype=jnp.float32) / d)
            pos = jnp.arange(x.shape[1], dtype=jnp.float32)
            ang = pos[:, None] * inv_freq[None, :]
            cos, sin = (jnp.cos(ang), jnp.sin(ang))
            x1, x2 = (x[..., 0::2], x[..., 1::2])
            r1 = x1 * cos - x2 * sin
            r2 = x1 * sin + x2 * cos
            return jnp.stack([r1, r2], axis=-1).reshape(x.shape)
        q = x @ Wq + bq
        k = x @ Wk + bk
        v = x @ Wv + bv
        q = rope(q)
        k = rope(k)
        b, s, _ = x.shape
        qh = q.reshape(b, s, H, HD).transpose(0, 2, 1, 3)
        kh = k.reshape(b, s, H, HD).transpose(0, 2, 1, 3)
        vh = v.reshape(b, s, H, HD).transpose(0, 2, 1, 3)
        scores = jnp.einsum('bhqd,bhkd->bhqk', qh, kh) / jnp.sqrt(jnp.float32(HD))
        attn = jax.nn.softmax(scores, axis=-1)
        out = jnp.einsum('bhqk,bhkd->bhqd', attn, vh)
        out = out.transpose(0, 2, 1, 3).reshape(b, s, D)
        return out @ W0 + b0

    def _L1_ffn_ref(x, W1, b1, W2, b2):
        import jax, jax.numpy as jnp
        import numpy as np
        EMB = 128
        FF = 4 * EMB

        def _ternary(w):
            scale = jnp.maximum(jnp.mean(jnp.abs(w)), 1e-08)
            w_t = jnp.clip(jnp.round(w / scale), -1.0, 1.0)
            return w + jax.lax.stop_gradient(w_t - w)
        h = jnp.einsum('bsd,fd->bsf', x, _ternary(W1)) + b1
        h = jax.nn.gelu(h, approximate=False)
        out = jnp.einsum('bsf,df->bsd', h, _ternary(W2)) + b2
        return out

    def _L2_attn_ref(x, Wq, bq, Wk, bk, Wv, bv, Wo, bo):
        import jax, jax.numpy as jnp
        import numpy as np
        B, S, E = (4, 512, 128)
        CHUNK = 32
        b, s, e = x.shape
        nc = s // CHUNK
        scale = 1.0 / jnp.sqrt(jnp.asarray(e, x.dtype))
        Q = (x @ Wq + bq).reshape(b, nc, CHUNK, e)
        K = (x @ Wk + bk).reshape(b, nc, CHUNK, e)
        V = (x @ Wv + bv).reshape(b, nc, CHUNK, e)
        local_scores = jnp.einsum('bnqe,bnke->bnqk', Q, K) * scale
        local = jnp.einsum('bnqk,bnke->bnqe', jax.nn.softmax(local_scores, axis=-1), V)
        cross_scores = jnp.einsum('bnqe,bmke->bnmqk', Q, K) * scale
        cross = jnp.einsum('bnmqk,bnke->bnqe', jax.nn.softmax(cross_scores, axis=-1), V)
        combined = (local + cross).reshape(b, s, e)
        return combined @ Wo + bo

    def _L2_ffn_ref(x, Wg, W1, W2, W3, Ws1, Ws2, Ws3):
        import jax, jax.numpy as jnp
        import numpy as np
        TOP_K = 4
        CAP_FACTOR = 4

        def swiglu(x, w1, w2, w3):
            return jax.nn.silu(x @ w1) * (x @ w3) @ w2
        B, S, D = x.shape
        E = Wg.shape[1]
        T = B * S
        xf = x.reshape(T, D)
        scores = jax.nn.softmax(xf @ Wg, axis=-1)
        weights, indices = jax.lax.top_k(scores, TOP_K)
        P = T * TOP_K
        pair_expert = indices.reshape(-1)
        pair_token = jnp.repeat(jnp.arange(T), TOP_K)
        pair_weight = weights.reshape(-1).astype(xf.dtype)
        C = CAP_FACTOR * P // E
        y = jnp.zeros_like(xf)
        for e in range(E):
            pos = jnp.nonzero(pair_expert == e, size=C, fill_value=P)[0]
            valid = pos < P
            safe = jnp.minimum(pos, P - 1)
            tok = jnp.where(valid, pair_token[safe], 0)
            w = jnp.where(valid, pair_weight[safe], 0.0)
            xg = xf[tok]
            out = swiglu(xg, W1[e], W2[e], W3[e]) * w[:, None]
            y = y.at[tok].add(out)
        z = swiglu(xf, Ws1, Ws2, Ws3)
        return (y + z).reshape(B, S, D)

    def _L3_attn_ref(x, Wq, bq, Wk, bk, Wv, bv, Wo, bo, gamma, beta):
        import jax, jax.numpy as jnp
        import numpy as np
        NUM_HEADS = 16
        KEY_DIM = 64
        UPDATE_STEPS_MAX = 3
        UPDATE_STEPS_EPS = 0.0001
        LN_EPS = 1e-05
        B, S, DIM = (4, 128, 128)
        INNER = NUM_HEADS * KEY_DIM

        def _glorot(key, shape):
            fan_in, fan_out = (shape[0], shape[1])
            lim = jnp.sqrt(6.0 / (fan_in + fan_out))
            return jax.random.uniform(key, shape, jnp.float32, -lim, lim)

        def _layernorm(t, gamma, beta):
            mu = jnp.mean(t, axis=-1, keepdims=True)
            var = jnp.mean(jnp.square(t - mu), axis=-1, keepdims=True)
            return (t - mu) * jax.lax.rsqrt(var + LN_EPS) * gamma + beta

        def _heads(t):
            b, s, _ = t.shape
            return t.reshape(b, s, NUM_HEADS, KEY_DIM).transpose(0, 2, 1, 3)
        q = x @ Wq + bq
        k = x @ Wk + bk
        v = x @ Wv + bv
        q = _heads(q)
        k = _heads(k)
        v = _heads(v)
        q = _layernorm(q, gamma, beta)
        k = _layernorm(k, gamma, beta)
        scale = jnp.sqrt(jnp.asarray(KEY_DIM, q.dtype))

        def step(carry, _):
            q_cur, converged = carry
            scores = jnp.einsum('bhqd,bhkd->bhqk', q_cur, k) / scale
            attn = jax.nn.softmax(scores, axis=-1)
            out = jnp.einsum('bhqk,bhkd->bhqd', attn, v)
            diff = jnp.linalg.norm(out - q_cur)
            q_new = jnp.where(converged, q_cur, out)
            return ((q_new, converged | (diff < UPDATE_STEPS_EPS)), None)
        (q_final, _), _ = jax.lax.scan(step, (q, jnp.asarray(False)), None, length=UPDATE_STEPS_MAX)
        merged = q_final.transpose(0, 2, 1, 3).reshape(x.shape[0], x.shape[1], INNER)
        return merged @ Wo + bo

    def _L3_ffn_ref(x, norm_g, norm_b, slot_g, slot_b, scale, slot_embeds, Wg, bg, Wu, bu, Wd, bd):
        import jax, jax.numpy as jnp
        import numpy as np
        B, N, D = (4, 512, 128)
        E, S, F = (16, 64, 256)
        DO = 128
        EPS = 1e-05

        def _layernorm(x, g, b):
            mu = jnp.mean(x, axis=-1, keepdims=True)
            var = jnp.mean(jnp.square(x - mu), axis=-1, keepdims=True)
            return (x - mu) * jax.lax.rsqrt(var + EPS) * g + b
        x = _layernorm(x, norm_g, norm_b)
        se = _layernorm(slot_embeds, slot_g, slot_b) * scale
        logits = jnp.einsum('bnd,esd->bnes', x, se)
        dispatch = jax.nn.softmax(logits, axis=1)
        combine = jax.nn.softmax(logits.reshape(x.shape[0], x.shape[1], -1), axis=-1)
        slots = jnp.einsum('bnd,bnes->besd', x, dispatch)
        gate = jax.nn.gelu(jnp.einsum('besd,edf->besf', slots, Wg) + bg[None, :, None, :], approximate=False)
        up = jnp.einsum('besd,edf->besf', slots, Wu) + bu[None, :, None, :]
        eout = jnp.einsum('besf,efo->beso', gate * up, Wd) + bd[None, :, None, :]
        eout = eout.reshape(eout.shape[0], -1, eout.shape[-1])
        return jnp.einsum('bns,bso->bno', combine, eout)
    x = L0_attn_x
    xn = _layernorm(x, axis=-1)
    x = x + _L0_attn_ref(xn, L0_attn_Wq, L0_attn_Wk, L0_attn_Wv, L0_attn_Wo, L0_attn_bo) + _L0_ffn_ref(xn, L0_ffn_weight_q, L0_ffn_weight_scale, L0_ffn_bias)
    xn = _layernorm(x, axis=-1)
    x = x + _L1_attn_ref(xn, L1_attn_Wq, L1_attn_bq, L1_attn_Wk, L1_attn_bk, L1_attn_Wv, L1_attn_bv, L1_attn_W0, L1_attn_b0) + _L1_ffn_ref(xn, L1_ffn_W1, L1_ffn_b1, L1_ffn_W2, L1_ffn_b2)
    xn = _layernorm(x, axis=-1)
    x = x + _L2_attn_ref(xn, L2_attn_Wq, L2_attn_bq, L2_attn_Wk, L2_attn_bk, L2_attn_Wv, L2_attn_bv, L2_attn_Wo, L2_attn_bo) + _L2_ffn_ref(xn, L2_ffn_Wg, L2_ffn_W1, L2_ffn_W2, L2_ffn_W3, L2_ffn_Ws1, L2_ffn_Ws2, L2_ffn_Ws3)
    xn = _layernorm(x, axis=-1)
    x = x + _L3_attn_ref(xn, L3_attn_Wq, L3_attn_bq, L3_attn_Wk, L3_attn_bk, L3_attn_Wv, L3_attn_bv, L3_attn_Wo, L3_attn_bo, L3_attn_gamma, L3_attn_beta) + _L3_ffn_ref(xn, L3_ffn_norm_g, L3_ffn_norm_b, L3_ffn_slot_g, L3_ffn_slot_b, L3_ffn_scale, L3_ffn_slot_embeds, L3_ffn_Wg, L3_ffn_bg, L3_ffn_Wu, L3_ffn_bu, L3_ffn_Wd, L3_ffn_bd)
    return x

_drawn_inputs = setup_inputs


def setup_inputs(seed=0):
    import zlib

    import numpy as np

    out = dict(_drawn_inputs(seed))
    spreads = {'L0_attn_bo': (0.0, 0.458),
     'L3_attn_bq': (0.0, 2.0),
     'L3_attn_bk': (0.0, 2.0),
     'L3_attn_bv': (0.0, 2.0),
     'L3_attn_bo': (0.0, 2.0),
     'L3_attn_gamma': (1.0, 0.6),
     'L3_attn_beta': (0.0, 2.0),
     'L3_ffn_norm_g': (1.0, 0.6),
     'L3_ffn_norm_b': (0.0, 0.8),
     'L3_ffn_slot_g': (1.0, 0.6),
     'L3_ffn_slot_b': (0.0, 0.8),
     'L3_ffn_bg': (0.0, 0.8),
     'L3_ffn_bu': (0.0, 0.8),
     'L3_ffn_bd': (0.0, 2.0)}
    factors = {'L0_attn_Wq': 5.642,
     'L0_attn_Wk': 5.547,
     'L0_ffn_bias': 8.0,
     'L1_attn_Wq': 8.0,
     'L1_attn_bq': 8.0,
     'L1_attn_Wk': 8.0,
     'L1_attn_bk': 8.0,
     'L1_attn_Wv': 8.0,
     'L1_attn_bv': 8.0,
     'L1_attn_W0': 8.0,
     'L1_attn_b0': 8.0,
     'L1_ffn_b1': 8.0,
     'L1_ffn_b2': 30.059,
     'L2_attn_Wq': 8.0,
     'L2_attn_bq': 200.0,
     'L2_attn_Wk': 8.0,
     'L2_attn_bk': 200.0,
     'L2_attn_bv': 58.5,
     'L2_attn_bo': 200.0,
     'L2_ffn_Wg': 8.0,
     'L2_ffn_W1': 8.0,
     'L2_ffn_W2': 8.0,
     'L2_ffn_W3': 8.0,
     'L2_ffn_Ws1': 8.0,
     'L2_ffn_Ws2': 8.0,
     'L2_ffn_Ws3': 8.0,
     'L3_attn_Wq': 88.113,
     'L3_attn_Wk': 21.988,
     'L3_attn_Wv': 8.0,
     'L3_attn_Wo': 8.0,
     'L3_ffn_slot_embeds': 8.0,
     'L3_ffn_Wg': 8.0,
     'L3_ffn_Wu': 8.0,
     'L3_ffn_Wd': 8.0}
    for name, (base, spread) in spreads.items():
        noise = np.random.default_rng([zlib.crc32(name.encode()), seed]).standard_normal(out[name].shape)
        drawn = base * np.exp(spread * noise) if base else spread * noise
        out[name] = jnp.asarray(drawn.astype(out[name].dtype))
    for name, factor in factors.items():
        out[name] = (out[name] * factor).astype(out[name].dtype)
    return out
```

```python
from contextlib import ExitStack

import numpy as np

import concourse.bass as bass
from concourse import mybir

F32 = mybir.dt.float32
BF16 = mybir.dt.bfloat16
I8 = mybir.dt.int8
U32 = mybir.dt.uint32
ALU = mybir.AluOpType
ACT = mybir.ActivationFunctionType
AX = mybir.AxisListType

P = 128
D = 128
B, N = 16, 256
T = B * N
NT = T // P
TB = N // P
CH = 512
NCH = T // CH
H8, HD8 = 16, 8
BANK = 512


def rope_tables():
    pos = np.arange(N, dtype=np.float32)[:, None]
    out = []
    for d in (HD8, D):
        inv = (np.float32(1.0) / np.power(np.float32(10000.0), np.arange(0, d, 2, dtype=np.float32) / np.float32(d)))
        ang = pos * inv.astype(np.float32)[None, :]
        for f in (np.cos, np.sin):
            t = np.repeat(f(ang).astype(np.float32), 2, axis=1)
            out.append(np.tile(t, (1, D // d)).T)
    return out


def const_columns():
    p = np.arange(P)
    c = {"ident": np.eye(P)}
    turn = np.zeros((P, P))
    turn[p ^ 1, p] = np.where(p % 2 == 0, -1.0, 1.0)
    c["turn"] = turn
    c["cos0"], c["sin0"], c["cos1"], c["sin1"] = rope_tables()
    quarter = (p[:, None] // HD8) % 4 == np.arange(4)[None, :]
    c["head0"] = quarter * np.float32(1.0 / HD8)
    c["head1"] = quarter * np.float32(1.0 / np.sqrt(np.float32(HD8)))
    c["ones"] = np.ones((P, P))
    c["before"] = p[:, None] < p[None, :]
    k = np.arange(N)
    c["future0"] = np.where(k[None, :] > p[:, None], -25.0, 0.0)
    c["future1"] = np.where(p[None, :] > p[:, None], -25.0, 0.0)
    own = np.zeros((P, TB, 8))
    for t in range(TB):
        own[p, t, (t * P + p) // 32] = 1.0
    c["own1"] = (1.0 + own).reshape(P, TB * 8)
    c["block"] = (p[:, None] // 32) == np.arange(4)[None, :]
    c["expert"] = np.tile(np.arange(32), (P, 1))
    sel = np.zeros((P, 16, P))
    for pair in range(16):
        for m in range(P):
            sel[2 * pair + m // 64, pair, m] = 1.0
    c["sel"] = sel.reshape(P, 16 * P)
    return {k: np.ascontiguousarray(v, dtype=np.float32) for k, v in c.items()}


def const_layout():
    at, where = 0, {}
    for k, v in const_columns().items():
        where[k] = (at, v.shape[1])
        at += v.shape[1]
    return where, at


class Lane:

    def __init__(self, nc, eng, name):
        self.nc, self.eng, self.name = nc, eng, name
        self.seen = {}
        self.sem, self.count = None, 0

    def stage(self, name):
        self.sem, self.count = self.nc.alloc_semaphore(f"{name}_{self.name}"), 0

    def done(self, ins):
        ins.then_inc(self.sem, 1)
        self.count += 1
        return (self.sem, self.count)

    def need(self, *steps):
        for s in steps:
            if s is None:
                continue
            sem, v = s
            if self.seen.get(sem.name, 0) < v:
                self.eng.wait_ge(sem, v)
                self.seen[sem.name] = v

    def chain(self, ins):
        s = self.done(ins)
        self.need(s)
        return s


class Core:
    def __init__(self, nc, a):
        self.nc, self.a = nc, a
        self.pe = Lane(nc, nc.tensor, "pe")
        self.act = Lane(nc, nc.scalar, "act")
        self.dve = Lane(nc, nc.vector, "dve")
        self.pool = Lane(nc, nc.gpsimd, "pool")
        self.sp = Lane(nc, nc.sync, "sp")
        self.lanes = [self.pe, self.act, self.dve, self.pool]
        self.ps = nc.alloc_psum_tensor("psum", [P, 8, BANK], F32)
        self.banks = [self.ps[:, i, :] for i in range(8)]

    def stage(self, name):
        last = [(l.sem, l.count) for l in self.lanes if l.sem is not None and l.count]
        for l in self.lanes + [self.sp]:
            l.need(*last)
        for l in self.lanes:
            l.stage(name)

    def load(self, name, *pairs, eng=None):
        sem = self.nc.alloc_semaphore(f"{name}_landed")
        for dst, src in pairs:
            (eng or self.nc.sync).dma_start(dst, src).then_inc(sem, 16)
        return (sem, 16 * len(pairs))


def row(v):
    return v.partition_broadcast(P)


def col(v):
    return v.rearrange("(p o) -> p o", o=1)


def per_row(t):
    return t[:, :]


def per_tile(v, n):
    return v.unsqueeze(1).to_broadcast((v.shape[0], n, v.shape[1]))


def spread(v, n):
    return v.unsqueeze(2).to_broadcast((v.shape[0], v.shape[1], n))


def rsqrt_into(c, out, var, tmp, scale, eps):
    nc, act, dve = c.nc, c.act, c.dve
    v, t = tmp
    act.need(dve.chain(nc.vector.tensor_scalar(v, var, scale, eps, ALU.mult, ALU.add)))
    act.chain(nc.scalar.activation(out, v, ACT.Ln))
    dve.need(act.done(nc.scalar.activation(out, out, ACT.Exp, scale=-0.5)))
    dve.chain(nc.vector.tensor_tensor(t, out, out, ALU.mult))
    dve.chain(nc.vector.tensor_tensor(t, t, v, ALU.mult))
    dve.chain(nc.vector.tensor_scalar(t, t, -0.5, 1.5, ALU.mult, ALU.add))
    dve.chain(nc.vector.tensor_tensor(out, out, t, ALU.mult))


def norm_tiles(c, name, src, dst, n, dstT=None, affine=None, groups=4):
    nc, pe, act, dve, pool = c.nc, c.pe, c.act, c.dve, c.pool
    with ExitStack() as ctx:
        sb = lambda k, s: ctx.enter_context(nc.sbuf_tensor(f"{name}_{k}", s, F32))
        stats, mv = sb("stats", [P, n, 6]), sb("mv", [P, n, 2])
        rs, v, t = sb("rstd", [P, n]), sb("var", [P, n]), sb("newton", [P, n])
        g = n // groups
        ring = dst if dst is not None else sb("normed", [P, 2 * g, D])
        banks, read = c.banks, {}
        turned = {}
        for i in range(groups + 1):
            if i < groups:
                for k in range(i * g, i * g + g):
                    s = dve.done(nc.vector.bn_stats(stats[:, k, :], src[:, k, :]))
                dve.need(s)
                for k in range(i * g, i * g + g):
                    s = dve.done(nc.vector.bn_aggr(mv[:, k, :], stats[:, k, :]))
                dve.need(s)
                w = slice(i * g, i * g + g)
                rsqrt_into(c, rs[:, w], mv[:, w, 1], (v[:, w], t[:, w]), 1.0, 1e-5)
            if i >= 1:
                j = i - 1
                for k in range(j * g, j * g + g):
                    r = k if dst is not None else k % (2 * g)
                    if dst is None and k >= 2 * g:
                        dve.need(turned[(k - 2 * g) // 4])
                    s = dve.done(nc.vector.tensor_scalar(ring[:, r, :], src[:, k, :], mv[:, k, 0:1],
                                                         rs[:, k:k + 1], ALU.subtract, ALU.mult))
                    if affine is not None:
                        gamma, beta = affine
                        pool.need(s)
                        pool.chain(nc.gpsimd.tensor_tensor(ring[:, r, :], ring[:, r, :], gamma, ALU.mult))
                        s = pool.done(nc.gpsimd.tensor_tensor(ring[:, r, :], ring[:, r, :], beta, ALU.add))
                    if dstT is not None and k % 4 == 3:
                        q = k // 4
                        pe.need(s, read.get(q - 4))
                        for m in range(4):
                            rr = (k - 3 + m) if dst is not None else (k - 3 + m) % (2 * g)
                            mm = nc.tensor.transpose(banks[q % 4][:, m * P:(m + 1) * P], ring[:, rr, :], c.ident)
                        turned[q] = pe.done(mm)
                        act.need(turned[q])
                        read[q] = act.done(nc.scalar.copy(dstT[:, q * CH:(q + 1) * CH], banks[q % 4][:, :]))
        c.stage(f"{name}_end")


def transpose_into(c, dst, src, bank, before=()):
    c.pe.need(*before)
    s = c.pe.done(c.nc.tensor.transpose(bank[:, 0:P], src, c.ident))
    c.dve.need(s)
    return c.dve.done(c.nc.vector.tensor_copy(dst, bank[:, 0:P]))


def attention8(c, name, x, xnT, w, rope, head_scale, bias, causal, w_is_out_in):
    nc, pe, act, dve, pool = c.nc, c.pe, c.act, c.dve, c.pool
    cos, sin = rope
    S, PT, O, M = c.banks[0:3], c.banks[3:5], c.banks[5], c.banks[6:8]
    NH = B * H8
    with ExitStack() as ctx:
        sb = lambda k, s, dt=F32: ctx.enter_context(nc.sbuf_tensor(f"{name}_{k}", s, dt))
        wt = {k: sb(f"w{k}", [P, D]) for k in ("q", "k", "v", "o", "qr", "kr")}
        bcol = {k: sb(f"b{k}", [P, 1]) for k in ("qr", "kr")}
        qm = [sb(f"q{i}", [P, 4, CH]) for i in range(2)]
        kT = [sb(f"k{i}", [P, CH]) for i in range(2)]
        V = [sb(f"v{i}", [P, CH // P, D]) for i in range(2)]
        t1, t2, qf = sb("t1", [P, CH]), sb("t2", [P, CH]), sb("qf", [P, CH])
        Pr = [sb(f"p{i}", [P, TB, N]) for i in range(3)]
        PTs = [sb(f"pt{i}", [P, TB, N]) for i in range(2)]
        nm = sb("nm", [P, 4, TB])
        rsum = sb("rsum", [P, 2, TB, H8])
        rinv = sb("rinv", [P, 2, TB, H8])
        on, oT = sb("on", [P, TB, D]), sb("oT", [P, TB, D])

        steps = {}
        s = None
        for k in ("q", "k", "v", "o"):
            src = w[k]
            if w_is_out_in:
                s = transpose_into(c, wt[k][:, :], src, M[0], (s,))
            else:
                s = dve.done(nc.vector.tensor_copy(wt[k][:, :], src))
            steps[k] = s
        for k in ("q", "k"):
            if w_is_out_in:
                lhs = w[k]
            else:
                s = transpose_into(c, t1[:, 0:P], w[k], M[0], (s,))
                lhs = t1[:, 0:P]
            pe.need(s)
            s = pe.done(nc.tensor.matmul(M[0][:, 0:P], lhs, c.turn, start=True, stop=True))
            dve.need(s)
            s = dve.done(nc.vector.tensor_copy(wt[k + "r"][:, :], M[0][:, 0:P]))
            if bias is not None:
                pe.need(s)
                s = pe.done(nc.tensor.matmul(M[0][:, 0:1], c.turn, bias[k], start=True, stop=True))
                dve.need(s)
                s = dve.done(nc.vector.tensor_copy(bcol[k + "r"][:, :], M[0][:, 0:1]))
        weights_ready = s
        bias_of = {k: (0.0 if bias is None else (bias[k] if k in ("q", "k") else bcol[k][:, 0:1]))
                   for k in ("q", "qr", "k", "kr")}

        mread = [weights_ready, weights_ready]
        head_done = {}
        pv_done = {}
        ready = {}
        st = {}

        def project(ch, k):
            def pe_part():
                for m, kk in ((0, k), (1, k + "r")):
                    pe.need(weights_ready, mread[m])
                    st[m] = pe.done(nc.tensor.matmul(M[m][:, :], wt[kk][:, :], xnT[:, ch * CH:(ch + 1) * CH],
                                                     start=True, stop=True))
            def rest():
                two = CH // N
                for m, kk, tab, dst in ((0, k, cos, t1), (1, k + "r", sin, t2)):
                    dve.need(st[m], st.get("tfree"))
                    mread[m] = dve.done(nc.vector.scalar_tensor_tensor(
                        out=dst[:, :].rearrange("p (b n) -> p b n", b=two),
                        in0=M[m][:, :].rearrange("p (b n) -> p b n", b=two), scalar=bias_of[kk],
                        in1=per_tile(tab, two), op0=ALU.add, op1=ALU.mult))
                last = (ch - 1) * 2 * H8 - 1
                pool.need(mread[1], head_done.get(last))
                if k == "k":
                    s = pool.done(nc.gpsimd.tensor_tensor(kT[ch % 2][:, :], t1[:, :], t2[:, :], ALU.add))
                    st["tfree"] = s
                else:
                    s = pool.chain(nc.gpsimd.tensor_tensor(qf[:, :], t1[:, :], t2[:, :], ALU.add))
                    st["tfree"] = s
                    for j in range(4):
                        s = pool.done(nc.gpsimd.tensor_scalar(qm[ch % 2][:, j, :], qf[:, :],
                                                              head_scale[:, j:j + 1], None, ALU.mult))
                ready.setdefault(ch, []).append(s)
            return [pe_part, rest]

        def project_v(ch):
            def pe_part():
                pe.need(mread[0])
                for t in range(CH // P):
                    mm = nc.tensor.matmul(M[0][:, t * P:(t + 1) * P], xnT[:, ch * CH + t * P:ch * CH + (t + 1) * P],
                                          wt["v"][:, :], start=True, stop=True)
                st["v"] = pe.done(mm)
            def rest():
                dve.need(st["v"], pv_done.get((ch - 1) * 2 * H8 - 1))
                out, src = V[ch % 2][:, :, :], M[0][:, :].rearrange("p (t d) -> p t d", d=D)
                if bias is None:
                    mread[0] = dve.done(nc.vector.tensor_copy(out, src))
                else:
                    mread[0] = dve.done(nc.vector.tensor_tensor(out, src, per_tile(bias["v"], CH // P), ALU.add))
                ready.setdefault(ch, []).append(mread[0])
            return [pe_part, rest]

        def pieces(ch):
            return project(ch, "q") + project(ch, "k") + project_v(ch)

        for f in pieces(0):
            f()

        scored, exped, turned, moved = {}, {}, {}, {}
        out_read = {}

        def scores(i):
            b, h = divmod(i, H8)
            ch, off = b // 2, (b % 2) * N
            g, j = h // 4, h % 4
            rows = slice(32 * g, 32 * g + 32)
            pe.need(*ready[ch], exped.get(i - 3))
            bank = S[i % 3]
            for t in range(TB):
                o = bank[:, t * N:(t + 1) * N]
                mm = nc.tensor.matmul(o, qm[ch % 2][rows, j, off + t * P:off + (t + 1) * P],
                                      kT[ch % 2][rows, off:off + N], start=True, stop=not causal)
                if causal:
                    if t == 0:
                        mm = nc.tensor.matmul(o, c.mask400, c.future0, start=False, stop=True)
                    else:
                        mm = nc.tensor.matmul(o[:, P:N], c.mask400, c.future1, start=False, stop=True)
            scored[i] = head_done[i] = pe.done(mm)
            dve.need(scored[i], exped.get(i - 4))
            s = dve.done(nc.vector.tensor_reduce(nm[:, i % 4, :], bank[:, :].rearrange("p (t n) -> p t n", t=TB),
                                                 AX.X, ALU.max, negate=True))
            act.need(s, turned.get(i - 3), out_read.get(b - 2))
            for t in range(TB):
                e = nc.scalar.activation(Pr[i % 3][:, t, :], bank[:, t * N:(t + 1) * N], ACT.Exp,
                                         bias=nm[:, i % 4, t:t + 1], accum_out=rsum[:, b % 2, t, h:h + 1])
            exped[i] = act.done(e)

        def turn(i):
            pe.need(exped[i], moved.get(i - 2))
            for kt in range(TB):
                for t in range(TB):
                    mm = nc.tensor.transpose(PT[i % 2][:, kt * N + t * P:kt * N + (t + 1) * P],
                                             Pr[i % 3][:, t, kt * P:(kt + 1) * P], c.ident)
            turned[i] = pe.done(mm)
            dst, src = PTs[i % 2][:, :, :], PT[i % 2][:, :].rearrange("p (k n) -> p k n", k=TB)
            if i % 3 == 0:
                act.need(turned[i], pv_done.get(i - 2))
                moved[i] = act.done(nc.scalar.copy(dst, src))
            else:
                dve.need(turned[i], pv_done.get(i - 2))
                moved[i] = dve.done(nc.vector.tensor_copy(dst, src))

        def weigh(i):
            b, h = divmod(i, H8)
            ch = b // 2
            pe.need(moved[i], out_read.get(b - 2))
            at = (b % 2) * N
            for t in range(TB):
                for kt in range(TB):
                    mm = nc.tensor.matmul(O[:, at + t * P + HD8 * h:at + t * P + HD8 * (h + 1)],
                                          PTs[i % 2][:, kt, t * P:(t + 1) * P],
                                          V[ch % 2][:, (b % 2) * TB + kt, HD8 * h:HD8 * (h + 1)],
                                          start=(kt == 0), stop=(kt == TB - 1))
            pv_done[i] = pe.done(mm)

        def finish_a(b):
            dve.need(pv_done[(b + 1) * H8 - 1], exped[(b + 1) * H8 - 1])
            dve.chain(nc.vector.reciprocal(rinv[:, b % 2, :, :], rsum[:, b % 2, :, :]))
            dve.need(st.get("on_read"))
            for t in range(TB):
                s = dve.done(nc.vector.tensor_tensor(
                    on[:, t, :].rearrange("p (h d) -> p h d", d=HD8),
                    O[:, (b % 2) * N + t * P:(b % 2) * N + (t + 1) * P].rearrange("p (h d) -> p h d", d=HD8),
                    spread(rinv[:, b % 2, t, :], HD8), ALU.mult))
            out_read[b] = s
            pe.need(s, mread[0])
            for t in range(TB):
                mm = nc.tensor.transpose(M[0][:, t * P:(t + 1) * P], on[:, t, :], c.ident)
            st["on_read"] = pe.done(mm)

        def finish_b(b):
            act.need(st["on_read"], st.get("oT_read"))
            mread[0] = act.done(nc.scalar.copy(oT[:, :, :], M[0][:, 0:N].rearrange("p (t q) -> p t q", t=TB)))
            pe.need(mread[0], mread[1])
            for t in range(TB):
                mm = nc.tensor.matmul(M[1][:, t * P:(t + 1) * P], oT[:, t, :], wt["o"][:, :], start=True, stop=True)
            st["oT_read"] = pe.done(mm)
            dve.need(st["oT_read"])
            xs = x[:, b * TB:(b + 1) * TB, :]
            mread[1] = dve.done(nc.vector.tensor_tensor(xs, xs, M[1][:, 0:N].rearrange("p (t d) -> p t d", d=D), ALU.add))

        todo = []
        for i in range(NH + 4):
            if i < NH and i % (2 * H8) == 4 and i // (2 * H8) + 1 < NCH:
                todo = pieces(i // (2 * H8) + 1)
            if i < NH:
                scores(i)
            if 1 <= i <= NH:
                turn(i - 1)
            if 2 <= i < NH + 2:
                weigh(i - 2)
                if (i - 2) % H8 == H8 - 1:
                    finish_a((i - 2) // H8)
            if i >= 4 and (i - 4) % H8 == H8 - 1:
                finish_b((i - 4) // H8)
            if todo and i % H8 not in (0, 1, 2, 3) and i % 2 == 0:
                todo.pop(0)()
        c.stage(f"{name}_end")


def ffn_int8(c, name, x, xn, wq8, wscale):
    nc, pe, act, dve, pool = c.nc, c.pe, c.act, c.dve, c.pool
    G = 4
    with ExitStack() as ctx:
        sb = lambda k, s, dt=F32: ctx.enter_context(nc.sbuf_tensor(f"{name}_{k}", s, dt))
        wf, wT = sb("wf", [P, D]), sb("wT", [P, D], BF16)
        amax, xs, xi = sb("amax", [P, NT]), sb("xscale", [P, NT]), sb("xinv", [P, NT])
        xq = [sb(f"xq{i}", [P, G, D]) for i in range(2)]
        xqT = [sb(f"xqT{i}", [P, G, P], BF16) for i in range(2)]
        ys = [sb(f"y{i}", [P, G, D]) for i in range(2)]
        s = dve.done(nc.vector.tensor_copy(wf[:, :], wq8))
        pe.need(s)
        s = pe.done(nc.tensor.transpose(c.banks[7][:, 0:P], wf[:, :], c.ident))
        dve.need(s)
        w_ready = dve.done(nc.vector.tensor_copy(wT[:, :], c.banks[7][:, 0:P]))
        dve.chain(nc.vector.tensor_reduce(amax[:, :], xn[:, :, :], AX.X, ALU.max, apply_absolute_value=True))
        dve.chain(nc.vector.tensor_scalar(xs[:, :], amax[:, :], 1e-6, float(np.float32(1.0) / np.float32(127.0)),
                                          ALU.max, ALU.mult))
        dve.chain(nc.vector.reciprocal(xi[:, :], xs[:, :]))
        q_done, turned, moved, made, read, added = {}, {}, {}, {}, {}, {}
        ROUND = 12582912.0
        for g in range(NT // G + 2):
            if g < NT // G:
                dve.need(turned.get(g - 2))
                for t in range(G):
                    k = g * G + t
                    s = dve.done(nc.vector.tensor_scalar(xq[g % 2][:, t, :], xn[:, k, :], xi[:, k:k + 1], ROUND,
                                                         ALU.mult, ALU.add))
                dve.need(s)
                dve.chain(nc.vector.tensor_scalar(xq[g % 2][:, :, :], xq[g % 2][:, :, :], ROUND, -128.0,
                                                  ALU.subtract, ALU.max))
                q_done[g] = dve.done(nc.vector.tensor_scalar(xq[g % 2][:, :, :], xq[g % 2][:, :, :], 127.0, None, ALU.min))
            if 1 <= g <= NT // G:
                j = g - 1
                pe.need(q_done[j], moved.get(j - 2))
                for t in range(G):
                    mm = nc.tensor.transpose(c.banks[j % 2][:, t * P:(t + 1) * P], xq[j % 2][:, t, :], c.ident)
                turned[j] = pe.done(mm)
                act.need(turned[j], made.get(j - 2))
                moved[j] = act.done(nc.scalar.copy(xqT[j % 2][:, :, :],
                                                   c.banks[j % 2][:, :].rearrange("p (t q) -> p t q", t=G)))
            if g >= 2:
                j = g - 2
                bank = c.banks[2 + j % 2]
                pe.need(moved[j], w_ready, read.get(j - 2))
                for t in range(G):
                    mm = nc.tensor.matmul(bank[:, t * P:(t + 1) * P], xqT[j % 2][:, t, :], wT[:, :], start=True, stop=True)
                made[j] = pe.done(mm)
                dve.need(made[j], added.get(j - 2))
                for t in range(G):
                    k = j * G + t
                    s = dve.done(nc.vector.scalar_tensor_tensor(out=ys[j % 2][:, t, :], in0=bank[:, t * P:(t + 1) * P],
                                                                scalar=xs[:, k:k + 1], in1=wscale,
                                                                op0=ALU.mult, op1=ALU.mult))
                read[j] = s
                pool.need(s)
                xk = x[:, j * G:(j + 1) * G, :]
                added[j] = pool.done(nc.gpsimd.tensor_tensor(xk, xk, ys[j % 2][:, :, :], ALU.add))
        c.stage(f"{name}_end")


def ffn_ternary(c, name, x, xnT, w1, b1, w2):
    nc, pe, act, dve, pool = c.nc, c.pe, c.act, c.dve, c.pool
    F = w2.shape[1]
    FT = F // P
    with ExitStack() as ctx:
        sb = lambda k, s, dt=F32: ctx.enter_context(nc.sbuf_tensor(f"{name}_{k}", s, dt))
        tern = sb("tern", [P, F])
        w1T, w2T = sb("w1T", [P, FT, P]), sb("w2T", [P, FT, P])
        part, tot, inv = sb("part", [P, 1]), sb("tot", [P, 1]), sb("inv", [P, 1])
        h = [sb(f"h{i}", [P, FT, CH]) for i in range(2)]
        ROUND = 12582912.0
        s = None
        for wsrc, wdst in ((w1.rearrange("p t d -> p (t d)"), w1T), (w2, w2T)):
            dve.chain(nc.vector.tensor_reduce(part[:, :], wsrc, AX.X, ALU.add, apply_absolute_value=True))
            pe.need((dve.sem, dve.count))
            s = pe.done(nc.tensor.matmul(c.banks[7][:, 0:1], c.ones, part[:, :], start=True, stop=True))
            dve.need(s)
            dve.chain(nc.vector.tensor_scalar(tot[:, :], c.banks[7][:, 0:1], 1.0 / (F * D), 1e-8, ALU.mult, ALU.max))
            dve.chain(nc.vector.reciprocal(inv[:, :], tot[:, :]))
            dve.chain(nc.vector.tensor_scalar(tern[:, :], wsrc, inv[:, 0:1], ROUND, ALU.mult, ALU.add))
            dve.chain(nc.vector.tensor_scalar(tern[:, :], tern[:, :], ROUND, -1.0, ALU.subtract, ALU.max))
            dve.chain(nc.vector.tensor_scalar(tern[:, :], tern[:, :], 1.0, None, ALU.min))
            dve.chain(nc.vector.tensor_tensor(tern[:, :], tern[:, :], wsrc, ALU.subtract))
            pe.need(dve.chain(nc.vector.tensor_tensor(tern[:, :], tern[:, :], wsrc, ALU.add)))
            for t in range(FT):
                mm = nc.tensor.transpose(c.banks[6][:, t * P:(t + 1) * P], tern[:, t * P:(t + 1) * P], c.ident)
            s = pe.done(mm)
            dve.need(s)
            s = dve.done(nc.vector.tensor_copy(wdst[:, :, :], c.banks[6][:, :].rearrange("p (t d) -> p t d", t=FT)))
        w_ready = s
        made, gelued, out, read = {}, {}, {}, {}
        NG = NCH * FT
        for i in range(NG + 2):
            if i < NG:
                ch, f = divmod(i, FT)
                pe.need(w_ready, gelued.get(i - 4))
                made[i] = pe.done(nc.tensor.matmul(c.banks[i % 4], w1T[:, f, :], xnT[:, ch * CH:(ch + 1) * CH],
                                                   start=True, stop=True))
                act.need(made[i], out.get(ch - 2))
                gelued[i] = act.done(nc.scalar.activation(h[ch % 2][:, f, :], c.banks[i % 4], ACT.Gelu,
                                                          bias=b1[:, f:f + 1]))
            if i >= FT + 1 and (i - 1) % FT == 0:
                ch = (i - 1) // FT - 1
                bank = c.banks[4 + ch % 2]
                pe.need(gelued[ch * FT + FT - 1], read.get(ch - 2))
                for t in range(CH // P):
                    for f in range(FT):
                        mm = nc.tensor.matmul(bank[:, t * P:(t + 1) * P], h[ch % 2][:, f, t * P:(t + 1) * P],
                                              w2T[:, f, :], start=(f == 0), stop=(f == FT - 1))
                out[ch] = pe.done(mm)
                dve.need(out[ch])
                xs = x[:, ch * 4:(ch + 1) * 4, :]
                read[ch] = dve.done(nc.vector.tensor_tensor(xs, xs, bank[:, :].rearrange("p (t d) -> p t d", d=D), ALU.add))
        assert len(out) == NCH
        c.stage(f"{name}_end")


def chunk_attention(c, name, x, xnT, w, bcol, bv, own1, block):
    nc, pe, act, dve, pool = c.nc, c.pe, c.act, c.dve, c.pool
    NK, CK = N // 32, 32
    scale = float(np.float32(1.0) / np.sqrt(np.float32(D)))
    with ExitStack() as ctx:
        sb = lambda k, s, dt=F32: ctx.enter_context(nc.sbuf_tensor(f"{name}_{k}", s, dt))
        q, k = [sb(f"q{i}", [P, CH]) for i in range(2)], [sb(f"k{i}", [P, CH]) for i in range(2)]
        V = [sb(f"v{i}", [P, CH // P, D]) for i in range(2)]
        mx, z, zi = (sb(n, [P, 2, NK]) for n in ("mx", "z", "zi"))
        E = [sb(f"e{i}", [P, NK, CK]) for i in range(2)]
        W = sb("w", [P, 2, CK])
        Wb = [sb(f"wb{i}", [P, 4, CK]) for i in range(2)]
        WT = [sb(f"wt{i}", [P, P]) for i in range(2)]
        cT = [sb(f"ct{i}", [P, P]) for i in range(2)]
        scored, spread_, wide, mixed, comb, out = {}, {}, {}, {}, {}, {}
        ready = {}
        st = {}

        def project(ch):
            bank = c.banks[0]
            for dst, kk, last in ((q, "q", "r0"), (k, "k", "r1"), (V, "v", "r2")):
                bank = c.banks[{"q": 5, "k": 6, "v": 7}[kk]]
                pe.need(st.get(last))
                if kk == "v":
                    for t in range(CH // P):
                        mm = nc.tensor.matmul(bank[:, t * P:(t + 1) * P], xnT[:, ch * CH + t * P:ch * CH + (t + 1) * P],
                                              w["v"], start=True, stop=True)
                    s = pe.done(mm)
                    dve.need(s, mixed.get((ch - 1) * 4 - 1))
                    st[last] = dve.done(nc.vector.tensor_tensor(
                        V[ch % 2][:, :, :], bank[:, :].rearrange("p (t d) -> p t d", d=D), per_tile(bv, CH // P), ALU.add))
                else:
                    s = pe.done(nc.tensor.matmul(bank[:, :], w[kk], xnT[:, ch * CH:(ch + 1) * CH], start=True, stop=True))
                    act.need(s, scored.get((ch - 1) * 4 - 1))
                    st[last] = act.done(nc.scalar.activation(dst[ch % 2][:, :], bank[:, :], ACT.Identity, bias=bcol[kk]))
            ready[ch] = (st["r0"], st["r1"], st["r2"])

        def softmax(i):
            ch, off, t = i // 4, (i % 4) * P, i % TB
            boff = (i % 4) // TB * N
            bank = c.banks[i % 2]
            pe.need(*ready[ch], spread_.get(i - 2))
            scored[i] = pe.done(nc.tensor.matmul(bank[:, 0:N], q[ch % 2][:, off:off + P], k[ch % 2][:, boff:boff + N],
                                                 start=True, stop=True))
            sc = bank[:, 0:N].rearrange("p (m k) -> p m k", m=NK)
            j = i % 2
            dve.need(scored[i])
            dve.chain(nc.vector.tensor_reduce(mx[:, j, :], sc, AX.X, ALU.max))
            dve.need(wide.get(i - 2))
            spread_[i] = dve.done(nc.vector.tensor_tensor(E[j][:, :, :], sc, spread(mx[:, j, :], CK), ALU.subtract))
            act.need(spread_[i])
            st["exp", i] = act.done(nc.scalar.activation(E[j][:, :, :], E[j][:, :, :], ACT.Exp, scale=scale))

        def combine(i):
            j, t = i % 2, i % TB
            dve.need(st["exp", i])
            dve.chain(nc.vector.tensor_reduce(z[:, j, :], E[j][:, :, :], AX.X, ALU.add))
            dve.chain(nc.vector.reciprocal(zi[:, j, :], z[:, j, :]))
            s = dve.chain(nc.vector.tensor_tensor(zi[:, j, :], zi[:, j, :], own1[:, t * NK:(t + 1) * NK], ALU.mult))
            pool.need(s)
            s = pool.done(nc.gpsimd.tensor_tensor(E[j][:, :, :], E[j][:, :, :], spread(zi[:, j, :], CK), ALU.mult))
            dve.need(s)
            wide[i] = dve.chain(nc.vector.tensor_reduce(W[:, j, :], E[j][:, :, :].rearrange("p m k -> p k m"), AX.X, ALU.add))
            pool.need(wide[i], st.get(("turned", i - 2)))
            s = pool.done(nc.gpsimd.tensor_tensor(Wb[j][:, :, :], per_tile(W[:, j, :], 4), spread(block, CK), ALU.mult))
            pe.need(s, st.get(("t_read", i - 1)))
            s = pe.done(nc.tensor.transpose(c.banks[2][:, j * P:(j + 1) * P], Wb[j][:, :, :].rearrange("p m k -> p (m k)"), c.ident))
            st["turned", i] = s
            act.need(s, mixed.get(i - 2))
            st["t_read", i] = act.done(nc.scalar.copy(WT[j][:, :], c.banks[2][:, j * P:(j + 1) * P]))

        def mix(i):
            j, ch = i % 2, i // 4
            pe.need(st["t_read", i], comb.get(i - 1))
            mixed[i] = pe.done(nc.tensor.matmul(c.banks[3][:, j * P:(j + 1) * P], V[ch % 2][:, i % 4, :], WT[j][:, :],
                                                start=True, stop=True))
            act.need(mixed[i], st.get(("proj", i - 2)))
            comb[i] = act.done(nc.scalar.copy(cT[j][:, :], c.banks[3][:, j * P:(j + 1) * P]))
            pe.need(comb[i], out.get(i - 1))
            st["proj", i] = pe.done(nc.tensor.matmul(c.banks[4][:, j * P:(j + 1) * P], cT[j][:, :], w["o"], start=True, stop=True))
            dve.need(st["proj", i])
            out[i] = dve.done(nc.vector.tensor_tensor(x[:, i, :], x[:, i, :], c.banks[4][:, j * P:(j + 1) * P], ALU.add))

        project(0)
        for i in range(NT + 2):
            if i < NT:
                if i % 4 == 2 and i // 4 + 1 < NCH:
                    project(i // 4 + 1)
                softmax(i)
            if 1 <= i <= NT:
                combine(i - 1)
            if i >= 2:
                mix(i - 2)
        c.stage(f"{name}_end")


NE2, TOPK, HID = 32, 4, 64
CAP = 4 * (T * TOPK) // NE2


def route(c, name, xnT, wg, iota, before, weightT):
    nc, pe, act, dve, pool = c.nc, c.pe, c.act, c.dve, c.pool
    with ExitStack() as ctx:
        sb = lambda k, s, dt=F32: ctx.enter_context(nc.sbuf_tensor(f"{name}_{k}", s, dt))
        sc, wt, chosen, hit, rank = (sb(k, [P, NT, NE2]) for k in ("scores", "wt", "chosen", "hit", "rank"))
        m, z = sb("m", [P, NT]), sb("z", [P, NT])
        top, idx, idf = sb("top", [P, NT, 8]), sb("idx", [P, NT, 8], U32), sb("idf", [P, NT, TOPK])
        tot, run = sb("tot", [P, NT, NE2]), sb("run", [P, NT, NE2])
        half = NT // 2
        for t in range(NT):
            mm = nc.tensor.matmul(c.banks[t // half][:, (t % half) * NE2:(t % half + 1) * NE2],
                                  xnT[:, t * P:(t + 1) * P], wg, start=True, stop=True)
        dve.need(pe.done(mm))
        for b in range(2):
            s = dve.done(nc.vector.tensor_copy(sc[:, b * half:(b + 1) * half, :],
                                               c.banks[b][:, :].rearrange("p (t e) -> p t e", e=NE2)))
        dve.need(s)
        dve.chain(nc.vector.tensor_reduce(m[:, :], sc[:, :, :], AX.X, ALU.max))
        act.need(dve.done(nc.vector.tensor_tensor(sc[:, :, :], sc[:, :, :], spread(m[:, :], NE2), ALU.subtract)))
        dve.need(act.done(nc.scalar.activation(sc[:, :, :], sc[:, :, :], ACT.Exp)))
        dve.chain(nc.vector.tensor_reduce(z[:, :], sc[:, :, :], AX.X, ALU.add))
        dve.chain(nc.vector.reciprocal(z[:, :], z[:, :]))
        dve.chain(nc.vector.tensor_tensor(sc[:, :, :], sc[:, :, :], spread(z[:, :], NE2), ALU.mult))
        for t in range(NT):
            s = dve.done(nc.vector.max(top[:, t, :], sc[:, t, :]))
        dve.need(s)
        for t in range(NT):
            s = dve.done(nc.vector.max_index(idx[:, t, :], top[:, t, :], sc[:, t, :]))
        dve.need(s)
        dve.chain(nc.vector.tensor_copy(idf[:, :, :], idx[:, :, 0:TOPK]))
        for k in range(TOPK):
            s = dve.chain(nc.vector.tensor_tensor(hit[:, :, :], per_tile(iota, NT), spread(idf[:, :, k], NE2), ALU.is_equal))
            if k == 0:
                dve.chain(nc.vector.tensor_copy(chosen[:, :, :], hit[:, :, :]))
                dve.chain(nc.vector.tensor_tensor(wt[:, :, :], hit[:, :, :], spread(top[:, :, k], NE2), ALU.mult))
            else:
                dve.chain(nc.vector.tensor_tensor(chosen[:, :, :], chosen[:, :, :], hit[:, :, :], ALU.add))
                dve.chain(nc.vector.tensor_tensor(hit[:, :, :], hit[:, :, :], spread(top[:, :, k], NE2), ALU.mult))
                dve.chain(nc.vector.tensor_tensor(wt[:, :, :], wt[:, :, :], hit[:, :, :], ALU.add))
        pe.need((dve.sem, dve.count))
        for b in range(2):
            src = chosen[:, b * half:(b + 1) * half, :].rearrange("p t e -> p (t e)")
            nc.tensor.matmul(c.banks[2 + b][:, :], before, src, start=True, stop=True)
            s = pe.done(nc.tensor.matmul(c.banks[4 + b][:, :], c.ones, src, start=True, stop=True))
        dve.need(s)
        for b in range(2):
            w = slice(b * half, (b + 1) * half)
            nc.vector.tensor_copy(rank[:, w, :], c.banks[2 + b][:, :].rearrange("p (t e) -> p t e", e=NE2))
            dve.chain(nc.vector.tensor_copy(tot[:, w, :], c.banks[4 + b][:, :].rearrange("p (t e) -> p t e", e=NE2)))
        dve.chain(nc.vector.memset(run[:, 0, :], 0.0))
        for t in range(1, NT):
            dve.chain(nc.vector.tensor_tensor(run[:, t, :], run[:, t - 1, :], tot[:, t - 1, :], ALU.add))
        dve.chain(nc.vector.tensor_tensor(rank[:, :, :], rank[:, :, :], run[:, :, :], ALU.add))
        dve.chain(nc.vector.tensor_scalar(rank[:, :, :], rank[:, :, :], float(CAP), None, ALU.is_lt))
        pe.need(dve.chain(nc.vector.tensor_tensor(wt[:, :, :], wt[:, :, :], rank[:, :, :], ALU.mult)))
        read = {}
        for q in range(NT // 4):
            pe.need(read.get(q - 2))
            for k in range(4):
                mm = nc.tensor.transpose(c.banks[6 + q % 2][0:NE2, k * P:(k + 1) * P], wt[:, q * 4 + k, :], c.ident)
            act.need(pe.done(mm))
            read[q] = act.done(nc.scalar.copy(weightT[:, q * CH:(q + 1) * CH], c.banks[6 + q % 2][0:NE2, :]))
        c.stage(f"{name}_end")


def experts(c, name, x, xnT, weightT, w1, w3, w2, ws, sel):
    nc, pe, act, dve = c.nc, c.pe, c.act, c.dve
    NP2 = NE2 // 2
    R = NP2 + 1
    with ExitStack() as ctx:
        sb = lambda k, s, dt=F32: ctx.enter_context(nc.sbuf_tensor(f"{name}_{k}", s, dt))
        sg = [sb(f"sg{i}", [P, CH]) for i in range(2)]
        hh = [sb(f"h{i}", [P, CH]) for i in range(3)]
        G, U, Wb, Y = c.banks[0:2], c.banks[2:4], c.banks[4:6], c.banks[6:8]
        made, silu, half, hid, down, added = {}, {}, {}, {}, {}, {}

        def up(i):
            ch, p = divmod(i, R)
            xs = xnT[:, ch * CH:(ch + 1) * CH]
            if p < NP2:
                l1 = w1[:, 2 * p:2 * p + 2, :].rearrange("d e h -> d (e h)")
                l3 = w3[:, 2 * p:2 * p + 2, :].rearrange("d e h -> d (e h)")
            else:
                l1, l3 = ws[0], ws[1]
            pe.need(hid.get(i - 2))
            nc.tensor.matmul(G[i % 2][:, :], l1, xs, start=True, stop=True)
            mm = nc.tensor.matmul(U[i % 2][:, :], l3, xs, start=True, stop=True)
            if p < NP2:
                mm = nc.tensor.matmul(Wb[i % 2][:, :], sel[0:NE2, p * P:(p + 1) * P], weightT[:, ch * CH:(ch + 1) * CH],
                                      start=True, stop=True)
            made[i] = pe.done(mm)
            act.need(made[i], half.get(i - 2))
            silu[i] = act.done(nc.scalar.activation(sg[i % 2][:, :], G[i % 2][:, :], ACT.Silu))
            dve.need(silu[i], down.get(i - 3))
            half[i] = dve.chain(nc.vector.tensor_tensor(hh[i % 3][:, :], sg[i % 2][:, :], U[i % 2][:, :], ALU.mult))
            hid[i] = half[i]
            if p < NP2:
                hid[i] = dve.done(nc.vector.tensor_tensor(hh[i % 3][:, :], hh[i % 3][:, :], Wb[i % 2][:, :], ALU.mult))

        def low(i):
            ch, p = divmod(i, R)
            l2 = w2[:, p, :] if p < NP2 else ws[2]
            bank = Y[ch % 2]
            pe.need(hid[i], added.get(ch - 2))
            for t in range(CH // P):
                mm = nc.tensor.matmul(bank[:, t * P:(t + 1) * P], hh[i % 3][:, t * P:(t + 1) * P], l2,
                                      start=(p == 0 and t == 0), stop=(p == R - 1), skip_group_check=True)
            down[i] = pe.done(mm)
            if p == R - 1:
                dve.need(down[i])
                xs = x[:, ch * 4:(ch + 1) * 4, :]
                added[ch] = dve.done(nc.vector.tensor_tensor(xs, xs, bank[:, :].rearrange("p (t d) -> p t d", d=D), ALU.add))

        for i in range(NCH * R + 2):
            if i < NCH * R:
                up(i)
            if i >= 2:
                low(i - 2)
        c.stage(f"{name}_end")


E3, SL, F3 = 16, 64, 256
ES = E3 * SL
FK = F3 // P
HB = B // 2


def slot_experts(c, name, x, xl, xlT, seT, wg, wu, wd, bgT, buT, bd):
    nc, pe, act, dve, pool = c.nc, c.pe, c.act, c.dve, c.pool
    UT = ES // N
    with ExitStack() as ctx:
        sb = lambda k, s, dt=F32: ctx.enter_context(nc.sbuf_tensor(f"{name}_{k}", s, dt))
        slots = sb("slots", [P, E3, HB * SL])
        eout = lambda ep: slots[:, 2 * ep:2 * ep + 2, :].rearrange("p e r -> p (e r)").rearrange("p (b o) -> p b o", o=D)
        nm, z, zi = sb("nm", [P, 4, 2]), sb("z", [P, 4, 2]), sb("zi", [P, 4, 2])
        scratch = sb("scratch", [P, 4 * ES])
        cut = lambda at, n: scratch[:, at:at + n]
        Ex = [cut(i * 2 * N, 2 * N).rearrange("p (s n) -> p s n", s=2) for i in range(3)]
        Dn = [cut((3 + i) * 2 * N, 2 * N).rearrange("p (t n) -> p t n", t=TB) for i in range(2)]
        g = [cut(i * CH, CH) for i in range(2)]
        h = [cut((2 + i * FK) * CH, FK * CH).rearrange("p (f n) -> p f n", f=FK) for i in range(2)]
        Cx = [cut(i * ES, ES) for i in range(2)]
        CT = [cut((2 + i) * ES, ES).rearrange("p (s n) -> p s n", n=P) for i in range(2)]
        for half in range(2):
            n = HB * UT
            lg, ex, nd, tr, mv, sl, ev = {}, {}, {}, {}, {}, {}, {}
            L, TR, X = c.banks[0:3], c.banks[3:5], c.banks[5:7]

            def logits(i):
                b, u = half * HB + i // UT, i % UT
                pe.need(ex.get(i - 3))
                for s in range(2):
                    mm = nc.tensor.matmul(L[i % 3][:, s * N:(s + 1) * N], seT[:, (2 * u + s) * P:(2 * u + s + 1) * P],
                                          xlT[:, b * N:(b + 1) * N], start=True, stop=True)
                lg[i] = pe.done(mm)
                dve.need(lg[i], ex.get(i - 4))
                s_ = dve.done(nc.vector.tensor_reduce(nm[:, i % 4, :], L[i % 3].rearrange("p (s n) -> p s n", s=2),
                                                      AX.X, ALU.max, negate=True))
                act.need(s_, tr.get(i - 3), nd.get(i - 4))
                for s in range(2):
                    e = nc.scalar.activation(Ex[i % 3][:, s, :], L[i % 3][:, s * N:(s + 1) * N], ACT.Exp,
                                             bias=nm[:, i % 4, s:s + 1], accum_out=z[:, i % 4, s:s + 1])
                ex[i] = act.done(e)
                dve.need(ex[i], nd.get(i - 4))
                pool.need(dve.done(nc.vector.reciprocal(zi[:, i % 4, :], z[:, i % 4, :])))
                nd[i] = pool.done(nc.gpsimd.tensor_tensor(Ex[i % 3][:, :, :], Ex[i % 3][:, :, :],
                                                          spread(zi[:, i % 4, :], N), ALU.mult))

            def turn(i):
                pe.need(nd[i], mv.get(i - 2))
                for s in range(2):
                    for t in range(TB):
                        mm = nc.tensor.transpose(TR[i % 2][:, t * N + s * P:t * N + (s + 1) * P],
                                                 Ex[i % 3][:, s, t * P:(t + 1) * P], c.ident)
                tr[i] = pe.done(mm)
                e = act if i % 2 else dve
                e.need(tr[i], sl.get(i - 2))
                src = TR[i % 2].rearrange("p (t n) -> p t n", t=TB)
                mv[i] = e.done(nc.scalar.copy(Dn[i % 2][:, :, :], src) if i % 2 else
                               nc.vector.tensor_copy(Dn[i % 2][:, :, :], src))

            def gather(i):
                b, u = i // UT, i % UT
                pe.need(mv[i], ev.get(i - 2))
                for t in range(TB):
                    mm = nc.tensor.matmul(X[i % 2][:, 0:N], xl[:, (half * HB + b) * TB + t, :], Dn[i % 2][:, t, :],
                                          start=(t == 0), stop=(t == TB - 1))
                sl[i] = pe.done(mm)
                act.need(sl[i])
                ev[i] = act.done(nc.scalar.copy(slots[:, 4 * u:4 * u + 4, b * SL:(b + 1) * SL],
                                                X[i % 2][:, 0:N].rearrange("p (e s) -> p e s", s=SL)))

            for i in range(n + 3):
                if i < n:
                    logits(i)
                if 2 <= i < n + 2:
                    turn(i - 2)
                if i >= 3:
                    gather(i - 3)
            c.stage(f"{name}_experts{half}")

            made, gel, hid, down, wr = {}, {}, {}, {}, {}

            def up(j):
                e, f = divmod(j, FK)
                pe.need(hid.get(j - 2))
                for m, w in ((0, wg), (2, wu)):
                    mm = nc.tensor.matmul(c.banks[m + j % 2], w[:, e, f * P:(f + 1) * P], slots[:, e, :], start=True, stop=True)
                made[j] = pe.done(mm)
                act.need(made[j], hid.get(j - 2))
                gel[j] = act.done(nc.scalar.activation(g[j % 2], c.banks[j % 2], ACT.Gelu,
                                                       bias=bgT[:, j:j + 1]))
                dve.need(gel[j], down.get(e - 2))
                hid[j] = dve.done(nc.vector.scalar_tensor_tensor(out=h[e % 2][:, f, :], in0=c.banks[2 + j % 2],
                                                                 scalar=buT[:, j:j + 1], in1=g[j % 2],
                                                                 op0=ALU.add, op1=ALU.mult))

            def low(e):
                ep, rows = e // 2, slice((e % 2) * SL, (e % 2) * SL + SL)
                pe.need(hid[e * FK + FK - 1], wr.get(ep - 2))
                for b in range(HB):
                    bank = c.banks[4 + 2 * (ep % 2) + b // 4]
                    for f in range(FK):
                        mm = nc.tensor.matmul(bank[rows, (b % 4) * D:(b % 4 + 1) * D], h[e % 2][:, f, b * SL:(b + 1) * SL],
                                              wd[:, e, f, :], start=(f == 0), stop=(f == FK - 1))
                down[e] = pe.done(mm)
                if e % 2:
                    dve.need(down[e])
                    for q in range(2):
                        s = dve.done(nc.vector.tensor_tensor(
                            eout(ep)[:, 4 * q:4 * q + 4, :], c.banks[4 + 2 * (ep % 2) + q].rearrange("p (b o) -> p b o", o=D),
                            per_tile(bd[:, ep, :], 4), ALU.add))
                    wr[ep] = s

            for e in range(E3 + 1):
                if e < E3:
                    up(e * FK)
                    up(e * FK + 1)
                if e >= 1:
                    low(e - 1)
            c.stage(f"{name}_combine{half}")

            n = HB * TB
            lg, ex, tr, mv, mx, ad = {}, {}, {}, {}, {}, {}

            def logits2(i):
                t = half * n + i
                two = c.ps[:, 2 * (i % 2):2 * (i % 2) + 2, :]
                pe.need(ex.get(i - 2))
                for q in range(2):
                    mm = nc.tensor.matmul(two[:, q, :], xlT[:, t * P:(t + 1) * P], seT[:, q * BANK:(q + 1) * BANK],
                                          start=True, stop=True)
                lg[i] = pe.done(mm)
                dve.need(lg[i], ex.get(i - 4))
                s = dve.done(nc.vector.tensor_reduce(nm[:, i % 4, 0:1], two, AX.XY, ALU.max, negate=True))
                act.need(s, tr.get(i - 2), ad.get(i - 4))
                ex[i] = act.done(nc.scalar.activation(Cx[i % 2].rearrange("p (q n) -> p q n", q=2), two, ACT.Exp,
                                                      bias=nm[:, i % 4, 0:1], accum_out=z[:, i % 4, 0:1]))

            def turn2(i):
                pe.need(ex[i], mv.get(i - 1), mv.get(("a", i - 1)))
                for s in range(ES // P):
                    mm = nc.tensor.transpose(c.banks[4 + s // 4][:, (s % 4) * P:(s % 4 + 1) * P],
                                             Cx[i % 2][:, s * P:(s + 1) * P], c.ident)
                tr[i] = pe.done(mm)
                dve.need(tr[i], mx.get(i - 2))
                act.need(tr[i], mx.get(i - 2))
                mv[i] = dve.done(nc.vector.tensor_copy(CT[i % 2][:, 0:4, :], c.banks[4].rearrange("p (s n) -> p s n", n=P)))
                mv["a", i] = act.done(nc.scalar.copy(CT[i % 2][:, 4:8, :], c.banks[5].rearrange("p (s n) -> p s n", n=P)))

            def mix(i):
                t = half * n + i
                b = i // TB
                pe.need(mv[i], mv["a", i], ad.get(i - 2))
                for s in range(ES // P):
                    mm = nc.tensor.matmul(c.banks[6 + i % 2][:, 0:D], CT[i % 2][:, s, :], eout(s)[:, b, :],
                                          start=(s == 0), stop=(s == ES // P - 1))
                mx[i] = pe.done(mm)
                dve.need(mx[i], ex[i])
                dve.chain(nc.vector.reciprocal(zi[:, i % 4, 0:1], z[:, i % 4, 0:1]))
                ad[i] = dve.done(nc.vector.scalar_tensor_tensor(out=x[:, t, :], in0=c.banks[6 + i % 2][:, 0:D],
                                                                scalar=zi[:, i % 4, 0:1], in1=x[:, t, :],
                                                                op0=ALU.mult, op1=ALU.add))

            for i in range(n + 2):
                if i < n:
                    logits2(i)
                if 1 <= i <= n:
                    turn2(i - 1)
                if i >= 2:
                    mix(i - 2)
            c.stage(f"{name}_end{half}")


H3, HD3 = 16, 64
INNER = H3 * HD3
STEPS = 3
HP = H3 // 2


def iterated_attention(c, name, x, xnT, w, brow, gamma, beta):
    nc, pe, act, dve, pool = c.nc, c.pe, c.act, c.dve, c.pool
    S, PT, O, TQ, M = c.banks[0:2], c.banks[2:4], c.banks[4:6], c.banks[6], c.banks[7]
    with ExitStack() as ctx:
        sb = lambda k, s, dt=F32: ctx.enter_context(nc.sbuf_tensor(f"{name}_{k}", s, dt))
        q = [sb(f"q{i}", [P, HP, N]) for i in range(STEPS + 1)]
        k = [sb(f"k{i}", [P, HP, N]) for i in range(2)]
        V = [sb(f"v{i}", [P, TB, INNER]) for i in range(2)]
        wk = [sb(f"t{i}", [P, INNER]) for i in range(TB)]
        sq, move = sb("sq", [P, INNER]), sb("move", [P, HP, N])
        ss, rs, v_, t_ = (sb(n_, [P, TB, H3]) for n_ in ("ss", "rs", "var", "newton"))
        Pr = [sb(f"p{i}", [P, TB, N]) for i in range(3)]
        PTs = [sb(f"pt{i}", [P, TB, N]) for i in range(2)]
        nm = sb("nm", [P, 4, TB])
        rsum, rinv = sb("rsum", [P, 4, 2, TB]), sb("rinv", [P, 2, 2, TB])
        on = [sb(f"on{i}", [P, TB, 2, HD3]) for i in range(2)]
        y = [sb(f"y{i}", [P, NT, D]) for i in range(STEPS - 1)]
        moved2 = sb("moved2", [P, STEPS - 1, B])
        tot, flag = sb("tot", [P, STEPS - 1]), sb("flag", [P, STEPS - 1], U32)

        for kk in ("q", "k"):
            for m in (w[kk], brow[kk]):
                m3 = m.rearrange("p (h d) -> p h d", d=HD3)
                dve.chain(nc.vector.tensor_reduce(ss[:, 0, :], m3, AX.X, ALU.add))
                dve.chain(nc.vector.tensor_scalar(ss[:, 0, :], ss[:, 0, :], 1.0 / HD3, None, ALU.mult))
                dve.chain(nc.vector.tensor_tensor(m3, m3, spread(ss[:, 0, :], HD3), ALU.subtract))
        centred = (dve.sem, dve.count)

        st = {}
        ready = {}
        index = lambda b, s, h: (b * STEPS + s) * H3 + h
        scored, exped, turned, moved, pv, pair_read, newq, ydone, on_read = {}, {}, {}, {}, {}, {}, {}, {}, {}
        squared = {}

        def pieces(b):
            out = []
            pend = []

            def product(kk, t, half, then):
                def f():
                    while pend:
                        pend.pop(0)()
                    pe.need(centred, st.get("m"))
                    st["mm"] = pe.done(nc.tensor.matmul(M, xnT[:, b * N + t * P:b * N + (t + 1) * P],
                                                        w[kk][:, half * BANK:(half + 1) * BANK], start=True, stop=True))
                    pend.append(then)
                return f

            for kk in ("q", "k"):
                for t in range(TB):
                    for half in range(2):
                        def then(kk=kk, t=t, half=half):
                            dve.need(st["mm"], st.get(("wk", t)))
                            w_ = slice(half * BANK, (half + 1) * BANK)
                            st["m"] = dve.done(nc.vector.tensor_tensor(wk[t][:, w_], M, brow[kk][:, w_], ALU.add))
                        out.append(product(kk, t, half, then))

                    def sums(t=t):
                        while pend:
                            pend.pop(0)()
                        act.need(st["m"], st.get("sq"))
                        s = act.done(nc.scalar.activation(sq[:, :], wk[t][:, :], ACT.Square))
                        dve.need(s, st.get("rs_read"))
                        st["sq"] = dve.done(nc.vector.tensor_reduce(ss[:, t, :], sq[:, :].rearrange("p (h d) -> p h d", d=HD3),
                                                                    AX.X, ALU.add))
                    out.append(sums)

                def scale():
                    dve.need(st["sq"])
                    rsqrt_into(c, rs[:, :, :], ss[:, :, :], (v_[:, :, :], t_[:, :, :]), 1.0 / HD3, 1e-5)
                    pool.need((dve.sem, dve.count))
                    for t in range(TB):
                        w3 = wk[t][:, :].rearrange("p (h d) -> p h d", d=HD3)
                        st["rs_read"] = pool.done(nc.gpsimd.tensor_tensor(w3, w3, spread(rs[:, t, :], HD3), ALU.mult))
                out.append(scale)
                for t in range(TB):
                    for half in range(2):
                        def turn_(kk=kk, t=t, half=half):
                            pe.need(st["rs_read"], st["m"])
                            for j in range(4):
                                mm = nc.tensor.transpose(M[:, j * P:(j + 1) * P],
                                                         wk[t][:, (half * 4 + j) * P:(half * 4 + j + 1) * P], c.ident)
                            st["wk", t] = pe.done(mm)
                            dst = q[0] if kk == "q" else k[b % 2]
                            act.need(st["wk", t], scored.get(index(b - 1, 0, H3 - 1)) if kk == "q" else
                                     scored.get(index(b - 2, STEPS - 1, H3 - 1)),
                                     squared.get((b - 1, 0)) if kk == "q" else None)
                            st["m"] = act.done(nc.scalar.activation(
                                dst[:, half * 4:half * 4 + 4, t * P:(t + 1) * P], M.rearrange("p (j n) -> p j n", n=P),
                                ACT.Identity, bias=beta, scale=gamma))
                        out.append(turn_)
            for t in range(TB):
                for half in range(2):
                    def then(t=t, half=half):
                        dve.need(st["mm"], pv.get(index(b - 2, STEPS - 1, H3 - 1)))
                        w_ = slice(half * BANK, (half + 1) * BANK)
                        st["m"] = dve.done(nc.vector.tensor_tensor(V[b % 2][:, t, w_], M, brow["v"][:, w_], ALU.add))
                    out.append(product("v", t, half, then))

            def end():
                while pend:
                    pend.pop(0)()
                ready[b] = ((act.sem, act.count), (dve.sem, dve.count))
            out.append(end)
            return out

        def scores(i, b, s, h):
            hp, rows = h // 2, slice((h % 2) * HD3, (h % 2) * HD3 + HD3)
            pe.need(*ready[b], newq.get((b, s, hp)), exped.get(i - 2))
            for t in range(TB):
                mm = nc.tensor.matmul(S[i % 2][:, t * N:(t + 1) * N], q[s][rows, hp, t * P:(t + 1) * P],
                                      k[b % 2][rows, hp, :], start=True, stop=True)
            scored[i] = pe.done(mm)
            dve.need(scored[i], exped.get(i - 4))
            dve.chain(nc.vector.tensor_reduce(nm[:, i % 4, :], S[i % 2].rearrange("p (t n) -> p t n", t=TB),
                                              AX.X, ALU.max, negate=True))
            m = dve.done(nc.vector.tensor_scalar(nm[:, i % 4, :], nm[:, i % 4, :], 1.0 / 8.0, None, ALU.mult))
            act.need(m, turned.get(i - 3), pair_read.get(i // 2 - 4))
            for t in range(TB):
                e = nc.scalar.activation(Pr[i % 3][:, t, :], S[i % 2][:, t * N:(t + 1) * N], ACT.Exp,
                                         bias=nm[:, i % 4, t:t + 1], scale=1.0 / 8.0,
                                         accum_out=rsum[:, (i // 2) % 4, h % 2, t:t + 1])
            exped[i] = act.done(e)

        def turn(i):
            pe.need(exped[i], moved.get(i - 2))
            for kt in range(TB):
                for t in range(TB):
                    mm = nc.tensor.transpose(PT[i % 2][:, kt * N + t * P:kt * N + (t + 1) * P],
                                             Pr[i % 3][:, t, kt * P:(kt + 1) * P], c.ident)
            turned[i] = pe.done(mm)
            dst, src = PTs[i % 2][:, :, :], PT[i % 2].rearrange("p (k n) -> p k n", k=TB)
            e = dve if i % 3 else act
            e.need(turned[i], pv.get(i - 2))
            moved[i] = e.done(nc.vector.tensor_copy(dst, src) if i % 3 else nc.scalar.copy(dst, src))

        def weigh(i, b, s, h):
            pr = i // 2
            pe.need(moved[i], pair_read.get(pr - 2))
            for t in range(TB):
                for kt in range(TB):
                    mm = nc.tensor.matmul(O[pr % 2][:, t * P + (h % 2) * HD3:t * P + (h % 2 + 1) * HD3],
                                          PTs[i % 2][:, kt, t * P:(t + 1) * P], V[b % 2][:, kt, h * HD3:(h + 1) * HD3],
                                          start=(kt == 0), stop=(kt == TB - 1))
            pv[i] = pe.done(mm)

        def pair_end(i, b, s, h):
            pr, hp = i // 2, h // 2
            dve.need(pv[i], exped[i], on_read.get(pr - 2))
            dve.chain(nc.vector.reciprocal(rinv[:, pr % 2, :, :], rsum[:, pr % 4, :, :]))
            for t in range(TB):
                r = dve.done(nc.vector.tensor_tensor(
                    on[pr % 2][:, t, :, :], O[pr % 2][:, t * P:(t + 1) * P].rearrange("p (e d) -> p e d", d=HD3),
                    spread(rinv[:, pr % 2, :, t], HD3), ALU.mult))
            pair_read[pr] = r
            pe.need(r, st.get("tq"))
            for t in range(TB):
                mm = nc.tensor.transpose(TQ[:, t * P:(t + 1) * P], on[pr % 2][:, t, :, :].rearrange("p e d -> p (e d)"), c.ident)
            on_read[pr] = pe.done(mm)
            act.need(on_read[pr], ydone.get((b - 1, s)), squared.get((b - 1, s)), squared.get((b - 1, s + 1)),
                     scored.get(index(b - 1, s + 1, H3 - 1)) if s + 1 < STEPS else None)
            newq[b, s + 1, hp] = act.done(nc.scalar.copy(q[s + 1][:, hp, :], TQ[:, 0:N]))
            st["tq"] = newq[b, s + 1, hp]

        def step_end(b, s):
            pe.need(newq[b, s + 1, HP - 1])
            for t in range(TB):
                for hp in range(HP):
                    mm = nc.tensor.matmul(TQ[:, t * P:(t + 1) * P], q[s + 1][:, hp, t * P:(t + 1) * P], w["o"][:, hp, :],
                                          start=(hp == 0), stop=(hp == HP - 1))
            ydone[b, s] = pe.done(mm)
            dve.need(ydone[b, s])
            dst = y[s][:, b * TB:(b + 1) * TB, :] if s < STEPS - 1 else \
                xnT[:, b * N:(b + 1) * N].rearrange("p (t d) -> p t d", d=D)
            st["tq"] = dve.done(nc.vector.tensor_copy(dst, TQ[:, 0:N].rearrange("p (t d) -> p t d", d=D)))
            if s < STEPS - 1:
                pool.need(newq[b, s + 1, HP - 1], st.get("move"))
                r = pool.done(nc.gpsimd.tensor_tensor(move[:, :, :], q[s + 1][:, :, :], q[s][:, :, :], ALU.subtract))
                act.need(r)
                st["move"] = squared[b, s] = act.done(nc.scalar.activation(move[:, :, :], move[:, :, :], ACT.Square,
                                                                          accum_out=moved2[:, s, b:b + 1]))

        for f in pieces(0):
            f()
        order = [(b, s, h) for b in range(B) for s in range(STEPS) for h in range(H3)]
        todo = []
        NI = len(order)
        for i in range(NI + 4):
            if i < NI:
                b, s, h = order[i]
                if s == 1 and h == 6 and b + 1 < B:
                    todo = pieces(b + 1)
                scores(i, b, s, h)
            if 1 <= i <= NI:
                turn(i - 1)
            if 2 <= i < NI + 2:
                weigh(i - 2, *order[i - 2])
            if 3 <= i < NI + 3 and order[i - 3][2] % 2:
                pair_end(i - 3, *order[i - 3])
                if order[i - 3][2] == H3 - 1:
                    step_end(*order[i - 3][0:2])
            if todo:
                todo.pop(0)()
            if i < NI and order[i][1:] == (STEPS - 1, H3 - 1):
                while todo:
                    todo.pop(0)()

        dve.need(*[v for v in squared.values()])
        dve.chain(nc.vector.tensor_reduce(tot[:, :], moved2[:, :, :], AX.X, ALU.add))
        pe.need((dve.sem, dve.count), st["tq"])
        r = pe.done(nc.tensor.matmul(M[:, 0:STEPS - 1], c.ones, tot[:, :], start=True, stop=True))
        dve.need(r)
        dve.chain(nc.vector.tensor_scalar(flag[:, :], M[:, 0:STEPS - 1], 1e-8, None, ALU.is_lt))
        y3 = xnT[:, :].rearrange("p (t d) -> p t d", d=D)
        for s in range(STEPS - 2, -1, -1):
            for g in range(4):
                ys, yd = y[s][:, g * 8:(g + 1) * 8, :], y3[:, g * 8:(g + 1) * 8, :]
                m = flag[:, s:s + 1].unsqueeze(2).to_broadcast((P, 8, D))
                r = dve.done(nc.vector.copy_predicated(yd, m, ys))
            dve.need(r)
        for g in range(4):
            xs = x[:, g * 8:(g + 1) * 8, :]
            dve.done(nc.vector.tensor_tensor(xs, xs, y3[:, g * 8:(g + 1) * 8, :], ALU.add))
        c.stage(f"{name}_end")


def program(nc, a, const, out, layers=(0, 1, 2, 3)):
    c = Core(nc, a)
    with ExitStack() as ctx:
        sb = lambda k, s, dt=F32: ctx.enter_context(nc.sbuf_tensor(f"sb_{k}", s, dt))
        x, xnT = sb("x", [P, NT, D]), sb("xnT", [P, T])
        where, width = const_layout()
        table = sb("table", [P, width])
        c.stage("start")
        tab = lambda k: table[:, where[k][0]:where[k][0] + where[k][1]]
        c.ident, c.turn, c.ones = tab("ident"), tab("turn"), tab("ones")
        xd = a["L0_attn_x"].rearrange("b (t p) d -> p (b t) d", p=P)
        table_in = c.load("table", (table[:, :], const))
        x_in = c.load("x", *[(x[:, i * 8:(i + 1) * 8, :], xd[:, i * 8:(i + 1) * 8, :]) for i in range(4)])

        early = ExitStack()
        eb = lambda k, s, dt=F32: early.enter_context(nc.sbuf_tensor(f"sb_{k}", s, dt))
        if 0 in layers or 1 in layers:
            wsq, pairs = {}, []
            for k in ("L0_attn_Wq", "L0_attn_Wk", "L0_attn_Wv", "L0_attn_Wo",
                      "L1_attn_Wq", "L1_attn_Wk", "L1_attn_Wv", "L1_attn_W0"):
                wsq[k] = eb(k, [P, D])
                pairs.append((wsq[k][:, :], a[k]))
            wq8 = eb("wq8", [P, D // 4], mybir.dt.int32)
            pairs.append((wq8[:, :], a["L0_ffn_weight_q"]))
            rows = {}
            for k in ("L0_attn_bo", "L0_ffn_weight_scale", "L0_ffn_bias", "L1_attn_bv", "L1_attn_b0", "L1_ffn_b2"):
                rows[k] = eb(k, [P, D])
                pairs.append((rows[k][:, :], row(a[k])))
            bq, bk, b1 = eb("bq1", [P, 1]), eb("bk1", [P, 1]), eb("b1", [P, 4])
            pairs += [(bq[:, :], col(a["L1_attn_bq"])), (bk[:, :], col(a["L1_attn_bk"]))]
            pairs += [(b1[:, f:f + 1], col(a["L1_ffn_b1"][f * P:(f + 1) * P])) for f in range(4)]
            w1, w2 = eb("w1", [P, 4, D]), eb("w2", [P, 4 * P])
            pairs += [(w1[:, :, :], a["L1_ffn_W1"].rearrange("(t p) d -> p t d", p=P)), (w2[:, :], a["L1_ffn_W2"])]
            small_in = c.load("small", *pairs, eng=nc.scalar)
            mask400, future0, future1 = eb("mask400", [P, P], BF16), eb("fut0", [P, N], BF16), eb("fut1", [P, P], BF16)
            c.dve.need(table_in)
            nc.vector.tensor_scalar(mask400[:, :], c.ident, 400.0, None, ALU.mult)
            nc.vector.tensor_copy(future0[:, :], tab("future0"))
            c.dve.done(nc.vector.tensor_copy(future1[:, :], tab("future1")))
            c.mask400, c.future0, c.future1 = mask400[:, :], future0[:, :], future1[:, :]
        experts_in = None
        if 2 in layers:
            w2l, pairs = {}, []
            for k in ("L2_attn_Wq", "L2_attn_Wk", "L2_attn_Wv", "L2_attn_Wo", "L2_ffn_Ws1", "L2_ffn_Ws3", "L2_ffn_Ws2"):
                w2l[k] = eb(k, [P, D])
                pairs.append((w2l[k][:, :], a[k]))
            for k in ("L2_attn_bq", "L2_attn_bk"):
                w2l[k] = eb(k, [P, 1])
                pairs.append((w2l[k][:, :], col(a[k])))
            for k in ("L2_attn_bv", "L2_attn_bo"):
                w2l[k] = eb(k, [P, D])
                pairs.append((w2l[k][:, :], row(a[k])))
            w2l["g"] = eb("wgate", [P, NE2])
            w1e, w3e, w2e = eb("w1e", [P, NE2, HID]), eb("w3e", [P, NE2, HID]), eb("w2e", [P, NE2 // 2, D])
            pairs += [(w2l["g"][:, :], a["L2_ffn_Wg"]),
                      (w1e[:, :, :], a["L2_ffn_W1"].rearrange("e d h -> d e h")),
                      (w3e[:, :, :], a["L2_ffn_W3"].rearrange("e d h -> d e h")),
                      (w2e[:, :, :], a["L2_ffn_W2"].rearrange("(q e) h d -> (e h) q d", e=2))]
            experts_in = c.load("experts", *pairs, eng=nc.gpsimd)
        for l in c.lanes:
            l.need(table_in, x_in, *([small_in] if 0 in layers or 1 in layers else []))
        c.stage("loaded")

        def add_bias(*b):
            for v in b:
                for g in range(4):
                    xs = x[:, g * 8:(g + 1) * 8, :]
                    s = c.pool.done(nc.gpsimd.tensor_tensor(xs, xs, per_tile(v, 8), ALU.add))
                c.pool.need(s)

        if 0 in layers:
            with nc.sbuf_tensor("xn", [P, NT, D], F32) as xn:
                norm_tiles(c, "norm0", x, xn, NT, xnT)
                add_bias(rows["L0_attn_bo"][:, :], rows["L0_ffn_bias"][:, :])
                c.stage("ffn0")
                ffn_int8(c, "int8", x, xn, wq8[:, :].bitcast(I8), rows["L0_ffn_weight_scale"][:, :])
            attention8(c, "attn0", x, xnT, {k: wsq[f"L0_attn_W{k}"][:, :] for k in "qkvo"},
                       (tab("cos0"), tab("sin0")), tab("head0"), None, True, True)
        if 1 in layers:
            norm_tiles(c, "norm1", x, None, NT, xnT)
            add_bias(rows["L1_attn_b0"][:, :], rows["L1_ffn_b2"][:, :])
            c.stage("attn1")
            w = {k: wsq[f"L1_attn_W{k}"][:, :] for k in "qkv"} | {"o": wsq["L1_attn_W0"][:, :]}
            attention8(c, "attn1", x, xnT, w, (tab("cos1"), tab("sin1")), tab("head1"),
                       {"q": bq[:, 0:1], "k": bk[:, 0:1], "v": rows["L1_attn_bv"][:, :]}, False, False)
            ffn_ternary(c, "tern", x, xnT, w1[:, :, :], b1, w2[:, :])
        if 2 in layers:
            for l in c.lanes:
                l.need(experts_in)
            norm_tiles(c, "norm2", x, None, NT, xnT)
            add_bias(w2l["L2_attn_bo"][:, :])
            c.stage("attn2")
            chunk_attention(c, "chunks", x, xnT, {k: w2l[f"L2_attn_W{k}"][:, :] for k in "qkvo"},
                            {k: w2l[f"L2_attn_b{k}"][:, 0:1] for k in "qk"}, w2l["L2_attn_bv"][:, :],
                            tab("own1"), tab("block"))
            with nc.sbuf_tensor("weightT", [NE2, T], F32) as weightT:
                route(c, "route", xnT, w2l["g"][:, :], tab("expert"), tab("before"), weightT)
                experts(c, "moe", x, xnT, weightT, w1e, w3e, w2e,
                        [w2l[f"L2_ffn_Ws{k}"][:, :] for k in (1, 3, 2)], tab("sel"))
        early.close()
        c.stage("late")
        if 3 in layers:
            with ExitStack() as late:
                lb = lambda k, s, dt=F32: late.enter_context(nc.sbuf_tensor(f"sb_{k}", s, dt))
                xl, xlT = lb("xl", [P, NT, D]), lb("xlT", [P, T])
                seT, se = lb("seT", [P, ES]), lb("se", [P, ES // P, D])
                wg, wu, wd = lb("wg", [P, E3, F3]), lb("wu", [P, E3, F3]), lb("wd", [P, E3, FK, D])
                bgu, bgT, buT = lb("bgu", [E3 * FK, 2, P]), lb("bgT", [P, E3 * FK]), lb("buT", [P, E3 * FK])
                bd = lb("bd", [P, E3 // 2, D])
                rows = {k: lb(k, [P, D]) for k in ("L3_ffn_norm_g", "L3_ffn_norm_b", "L3_ffn_slot_g", "L3_ffn_slot_b",
                                                   "L3_attn_bo")}
                sc = lb("scale", [P, 1])
                bdr = a["L3_ffn_bd"].rearrange("(q e) o -> e q o", e=2)
                slots_in = c.load("slots_w", (se[:, :, :], a["L3_ffn_slot_embeds"].rearrange("(q e) s d -> (e s) q d", e=2)),
                                  (sc[:, :], row(a["L3_ffn_scale"])), *[(v[:, :], row(a[k])) for k, v in rows.items()],
                                  (bgu[:, 0, :], a["L3_ffn_bg"].rearrange("e (f p) -> (e f) p", p=P)),
                                  (bgu[:, 1, :], a["L3_ffn_bu"].rearrange("e (f p) -> (e f) p", p=P)),
                                  (bd[0:SL, :, :], bdr[0].partition_broadcast(SL)),
                                  (bd[SL:P, :, :], bdr[1].partition_broadcast(SL)))
                ffn_in = c.load("ffn_w", (wg[:, :, :], a["L3_ffn_Wg"].rearrange("e d f -> d e f")),
                                (wu[:, :, :], a["L3_ffn_Wu"].rearrange("e d f -> d e f")),
                                *[(wd[:, :, f, :], a["L3_ffn_Wd"].rearrange("e (f p) o -> f p e o", p=P)[f]) for f in range(FK)])
                norm_tiles(c, "norm3", x, xl, NT, xnT)
                for l in c.lanes:
                    l.need(slots_in)
                add_bias(rows["L3_attn_bo"][:, :])
                norm_tiles(c, "norm_ffn", xl, xl, NT, xlT, affine=(per_row(rows["L3_ffn_norm_g"]), per_row(rows["L3_ffn_norm_b"])))
                norm_tiles(c, "norm_slot", se, se, ES // P, None, affine=(per_row(rows["L3_ffn_slot_g"]), per_row(rows["L3_ffn_slot_b"])), groups=2)
                s = c.dve.done(nc.vector.tensor_scalar(se[:, :, :], se[:, :, :], sc[:, 0:1], None, ALU.mult))
                c.pe.need(s)
                for k in range(ES // P):
                    mm = nc.tensor.transpose(c.banks[k // 4][:, (k % 4) * P:(k % 4 + 1) * P], se[:, k, :], c.ident)
                for k in range(2):
                    nk = E3 * FK
                    mm = nc.tensor.transpose(c.banks[2][:, k * nk:(k + 1) * nk], bgu[:, k, :], c.ident[0:nk, 0:nk])
                c.dve.need(c.pe.done(mm))
                for k in range(2):
                    nc.vector.tensor_copy(seT[:, k * BANK:(k + 1) * BANK], c.banks[k])
                nc.vector.tensor_copy(bgT[:, :], c.banks[2][:, 0:nk])
                c.dve.done(nc.vector.tensor_copy(buT[:, :], c.banks[2][:, nk:2 * nk]))
                for l in c.lanes:
                    l.need(ffn_in)
                c.stage("slots")
                slot_experts(c, "slotmoe", x, xl, xlT, seT, wg, wu, wd, bgT, buT, bd)
            with ExitStack() as late:
                lb = lambda k, s, dt=F32: late.enter_context(nc.sbuf_tensor(f"sb_{k}", s, dt))
                w3 = {k: lb(f"L3w{k}", [P, INNER]) for k in "qkv"}
                wo3 = lb("L3wo", [P, HP, D])
                b3 = {k: lb(f"L3b{k}", [P, INNER]) for k in "qkv"}
                gam, bet = lb("gamma", [P, 1]), lb("beta", [P, 1])
                attn_in = c.load("attn3_w", *[(w3[k][:, :], a[f"L3_attn_W{k}"]) for k in "qkv"],
                                 *[(b3[k][:, :], row(a[f"L3_attn_b{k}"])) for k in "qkv"],
                                 (wo3[:, :, :], a["L3_attn_Wo"].rearrange("(q p) o -> p q o", p=P)),
                                 *[(dst[HD3 * e:HD3 * (e + 1), :], col(a[k])) for e in range(2)
                                   for dst, k in ((gam, "L3_attn_gamma"), (bet, "L3_attn_beta"))])
                for l in c.lanes:
                    l.need(attn_in)
                iterated_attention(c, "attn3", x, xnT, {k: v[:, :] for k, v in w3.items()} | {"o": wo3},
                                   {k: v[:, :] for k, v in b3.items()}, gam[:, 0:1], bet[:, 0:1])
        yd = out.rearrange("b (t p) d -> p (b t) d", p=P)
        stored = nc.alloc_semaphore("stored")
        for i in range(4):
            nc.sync.dma_start(yd[:, i * 8:(i + 1) * 8, :], x[:, i * 8:(i + 1) * 8, :]).then_inc(stored, 16)
        nc.sync.wait_ge(stored, 64)


def kernel(**inputs):
    import concourse.bacc as bacc
    from concourse.bass_utils import run_bass_kernel_spmd

    nc = bacc.Bacc("TRN2", target_bir_lowering=False, num_devices=1)
    arrays = {k: np.ascontiguousarray(v) for k, v in inputs.items()}
    arrays["L0_ffn_weight_q"] = arrays["L0_ffn_weight_q"].view(np.int32)
    arrays["const"] = np.concatenate(list(const_columns().values()), axis=1)
    aps = {k: nc.dram_tensor(f"in_{k}", v.shape, mybir.dt.from_np(v.dtype), kind="ExternalInput").ap()
           for k, v in arrays.items()}
    out = nc.dram_tensor("out", (B, N, D), F32, kind="ExternalOutput").ap()
    program(nc, aps, aps["const"], out)
    r = run_bass_kernel_spmd(nc, [{f"in_{k}": v for k, v in arrays.items()}], core_ids=[0])
    return r.results[0]["out"]
```

```python
from contextlib import ExitStack

import numpy as np

import concourse.bass as bass
from concourse import mybir

F32 = mybir.dt.float32
F32R = mybir.dt.float32r
BF16 = mybir.dt.bfloat16
I8 = mybir.dt.int8
U32 = mybir.dt.uint32
ALU = mybir.AluOpType
ACT = mybir.ActivationFunctionType
AX = mybir.AxisListType

P = 128
D = 128
B, N = 16, 256
T = B * N
NT = T // P
TB = N // P
CH = 512
NCH = T // CH
H8, HD8 = 16, 8
BANK = 512


def rope_tables():
    pos = np.arange(N, dtype=np.float32)[:, None]
    out = []
    for d in (HD8, D):
        inv = (np.float32(1.0) / np.power(np.float32(10000.0), np.arange(0, d, 2, dtype=np.float32) / np.float32(d)))
        ang = pos * inv.astype(np.float32)[None, :]
        for f in (np.cos, np.sin):
            t = np.repeat(f(ang).astype(np.float32), 2, axis=1)
            out.append(np.tile(t, (1, D // d)).T)
    return out


def const_columns():
    p = np.arange(P)
    c = {"ident": np.eye(P)}
    turn = np.zeros((P, P))
    turn[p ^ 1, p] = np.where(p % 2 == 0, -1.0, 1.0)
    c["turn"] = turn
    c["cos0"], c["sin0"], c["cos1"], c["sin1"] = rope_tables()
    c["rows4"] = p[:, None] // 32 == np.arange(4)[None, :]
    c["ones"] = np.ones((P, P))
    c["before"] = p[:, None] < p[None, :]
    k = np.arange(N)
    c["future0"] = np.where(k[None, :] > p[:, None], -25.0, 0.0)
    c["future1"] = np.where(p[None, :] > p[:, None], -25.0, 0.0)
    own = np.zeros((P, TB, 8))
    for t in range(TB):
        own[p, t, (t * P + p) // 32] = 1.0
    c["own1"] = (1.0 + own).reshape(P, TB * 8)
    c["block"] = (p[:, None] // 32) == np.arange(4)[None, :]
    c["expert"] = np.tile(np.arange(32), (P, 1))
    sel = np.zeros((P, 16, P))
    for pair in range(16):
        for m in range(P):
            sel[2 * pair + m // 64, pair, m] = 1.0
    c["sel"] = sel.reshape(P, 16 * P)
    return {k: np.ascontiguousarray(v, dtype=np.float32) for k, v in c.items()}


def stack_columns():
    r = np.arange(P)
    j, part, d = r // 32, r // HD8 % 4, r % HD8
    stack = np.zeros((P, 4, 4, P))
    kinds = (part < 2, part >= 2, part % 2 == 0, part % 2 == 1)
    for n, on in enumerate(kinds):
        for g in range(4):
            stack[(32 * g + HD8 * j + d)[on], n, g, r[on]] = 1.0
    dup = np.zeros((P, 2, P))
    for g in range(2):
        dup[64 * g + HD8 * (r // 16) + r % HD8, g, r] = 1.0
    return {"stack": stack.reshape(P, -1).astype(np.float32), "dup": dup.reshape(P, -1).astype(np.float32)}


def all_columns():
    return const_columns() | stack_columns()


def const_layout(columns):
    at, where = 0, {}
    for k, v in columns.items():
        where[k] = (at, v.shape[1])
        at += v.shape[1]
    return where, at


class Lane:

    def __init__(self, nc, eng, name):
        self.nc, self.eng, self.name = nc, eng, name
        self.seen = {}
        self.sem, self.count = None, 0

    def stage(self, name):
        self.sem, self.count = self.nc.alloc_semaphore(f"{name}_{self.name}"), 0

    def done(self, ins):
        ins.then_inc(self.sem, 1)
        self.count += 1
        return (self.sem, self.count)

    def need(self, *steps):
        for s in steps:
            if s is None:
                continue
            sem, v = s
            if self.seen.get(sem.name, 0) < v:
                self.eng.wait_ge(sem, v)
                self.seen[sem.name] = v

    def chain(self, ins):
        s = self.done(ins)
        self.need(s)
        return s


class Core:
    def __init__(self, nc, a):
        self.nc, self.a = nc, a
        self.pe = Lane(nc, nc.tensor, "pe")
        self.act = Lane(nc, nc.scalar, "act")
        self.dve = Lane(nc, nc.vector, "dve")
        self.pool = Lane(nc, nc.gpsimd, "pool")
        self.sp = Lane(nc, nc.sync, "sp")
        self.lanes = [self.pe, self.act, self.dve, self.pool]
        self.ps = nc.alloc_psum_tensor("psum", [P, 8, BANK], F32)
        self.banks = [self.ps[:, i, :] for i in range(8)]

    def stage(self, name):
        last = [(l.sem, l.count) for l in self.lanes if l.sem is not None and l.count]
        for l in self.lanes + [self.sp]:
            l.need(*last)
        for l in self.lanes:
            l.stage(name)

    def load(self, name, *pairs, eng=None):
        sem = self.nc.alloc_semaphore(f"{name}_landed")
        for dst, src in pairs:
            (eng or self.nc.sync).dma_start(dst, src).then_inc(sem, 16)
        return (sem, 16 * len(pairs))


def row(v):
    return v.partition_broadcast(P)


def col(v):
    return v.rearrange("(p o) -> p o", o=1)


def per_row(t):
    return t[:, :]


def per_tile(v, n):
    return v.unsqueeze(1).to_broadcast((v.shape[0], n, v.shape[1]))


def spread(v, n):
    return v.unsqueeze(2).to_broadcast((v.shape[0], v.shape[1], n))


def rsqrt_into(c, out, var, tmp, scale, eps):
    nc, act, dve = c.nc, c.act, c.dve
    v, t = tmp
    act.need(dve.chain(nc.vector.tensor_scalar(v, var, scale, eps, ALU.mult, ALU.add)))
    act.chain(nc.scalar.activation(out, v, ACT.Ln))
    dve.need(act.done(nc.scalar.activation(out, out, ACT.Exp, scale=-0.5)))
    dve.chain(nc.vector.tensor_tensor(t, out, out, ALU.mult))
    dve.chain(nc.vector.tensor_tensor(t, t, v, ALU.mult))
    dve.chain(nc.vector.tensor_scalar(t, t, -0.5, 1.5, ALU.mult, ALU.add))
    dve.chain(nc.vector.tensor_tensor(out, out, t, ALU.mult))


def norm_tiles(c, name, src, dst, n, dstT=None, affine=None, groups=4):
    nc, pe, act, dve, pool = c.nc, c.pe, c.act, c.dve, c.pool
    with ExitStack() as ctx:
        sb = lambda k, s: ctx.enter_context(nc.sbuf_tensor(f"{name}_{k}", s, F32))
        stats, mv = sb("stats", [P, n, 6]), sb("mv", [P, n, 2])
        rs, v, t = sb("rstd", [P, n]), sb("var", [P, n]), sb("newton", [P, n])
        g = n // groups
        ring = dst if dst is not None else sb("normed", [P, 2 * g, D])
        banks, read = c.banks, {}
        turned = {}
        for i in range(groups + 1):
            if i < groups:
                for k in range(i * g, i * g + g):
                    s = dve.done(nc.vector.bn_stats(stats[:, k, :], src[:, k, :]))
                dve.need(s)
                for k in range(i * g, i * g + g):
                    s = dve.done(nc.vector.bn_aggr(mv[:, k, :], stats[:, k, :]))
                dve.need(s)
                w = slice(i * g, i * g + g)
                rsqrt_into(c, rs[:, w], mv[:, w, 1], (v[:, w], t[:, w]), 1.0, 1e-5)
            if i >= 1:
                j = i - 1
                for k in range(j * g, j * g + g):
                    r = k if dst is not None else k % (2 * g)
                    if dst is None and k >= 2 * g:
                        dve.need(turned[(k - 2 * g) // 4])
                    s = dve.done(nc.vector.tensor_scalar(ring[:, r, :], src[:, k, :], mv[:, k, 0:1],
                                                         rs[:, k:k + 1], ALU.subtract, ALU.mult))
                    if affine is not None:
                        gamma, beta = affine
                        pool.need(s)
                        pool.chain(nc.gpsimd.tensor_tensor(ring[:, r, :], ring[:, r, :], gamma, ALU.mult))
                        s = pool.done(nc.gpsimd.tensor_tensor(ring[:, r, :], ring[:, r, :], beta, ALU.add))
                    if dstT is not None and k % 4 == 3:
                        q = k // 4
                        pe.need(s, read.get(q - 4))
                        for m in range(4):
                            rr = (k - 3 + m) if dst is not None else (k - 3 + m) % (2 * g)
                            mm = nc.tensor.transpose(banks[q % 4][:, m * P:(m + 1) * P], ring[:, rr, :], c.ident)
                        turned[q] = pe.done(mm)
                        act.need(turned[q])
                        read[q] = act.done(nc.scalar.copy(dstT[:, q * CH:(q + 1) * CH], banks[q % 4][:, :]))
        c.stage(f"{name}_end")


def transpose_into(c, dst, src, bank, before=()):
    c.pe.need(*before)
    s = c.pe.done(c.nc.tensor.transpose(bank[:, 0:P], src, c.ident))
    c.dve.need(s)
    return c.dve.done(c.nc.vector.tensor_copy(dst, bank[:, 0:P]))


def attention8(c, name, x, xnT, w, rope, scale, rows4, bias, causal, w_is_out_in):
    nc, pe, act, dve, pool = c.nc, c.pe, c.act, c.dve, c.pool
    cos, sin = rope
    S, PT, O, M = c.banks[0:2], c.banks[2:4], c.banks[4:6], c.banks[6:8]
    NH = B * H8
    GQ, GV = 4, 2
    HG = H8 // GV
    DIAG = D + 2 * HD8
    with ExitStack() as ctx:
        sb = lambda k, s, dt=F32: ctx.enter_context(nc.sbuf_tensor(f"{name}_{k}", s, dt))
        wt = {k: sb(f"w{k}", [P, D]) for k in ("q", "k", "v", "o", "qr", "kr")}
        bcol = {k: sb(f"b{k}", [P, 1]) for k in ("qr", "kr")}
        q = [sb(f"q{i}", [P, GQ, N], F32R) for i in range(2)]
        kz = [sb(f"k{i}", [P, H8, N], F32R) for i in range(2)]
        vz = [sb(f"v{i}", [P, TB, GV, HG * DIAG], F32R) for i in range(2)]
        part = {k: sb(f"part_{k}", [P, N], F32R) for k in ("hi", "lo")}
        stack = sb("stack", [P, 4, GQ, P], F32R)
        wo2 = sb("wo2", [P, GV, D])
        vb = sb("vb", [P, D])
        t1, t2, rot = sb("t1", [P, N]), sb("t2", [P, N]), sb("rot", [P, N])
        Pr = [sb(f"p{i}", [P, TB, N]) for i in range(3)]
        PTh = [sb(f"pth{i}", [P, TB, N], F32R) for i in range(2)]
        PTl = [sb(f"ptl{i}", [P, TB, N], F32R) for i in range(2)]
        nm, rsum, rinv = (sb(k, [P, 4, TB]) for k in ("nm", "rsum", "rinv"))
        oT = sb("oT", [P, GV, N])
        for v in vz:
            zeroed = pool.done(nc.gpsimd.memset(v[:, :, :, :].bitcast(F32), 0.0))
        raw = sb("stack_raw", [P, (4 * GQ + GV) * P])
        stack_raw, dup_raw = raw[:, 0:4 * GQ * P], raw[:, 4 * GQ * P:(4 * GQ + GV) * P]
        raw_in = c.load(f"{name}_stack", (stack_raw, c.const("stack")), (dup_raw, c.const("dup")))
        dve.need(raw_in)
        dve.done(nc.vector.tensor_copy(stack[:, :, :, :].rearrange("p a g m -> p (a g m)"), stack_raw))

        s = None
        for k in ("q", "k", "v", "o"):
            if w_is_out_in:
                s = transpose_into(c, wt[k][:, :], w[k], M[0], (s,))
            else:
                s = dve.done(nc.vector.tensor_copy(wt[k][:, :], w[k]))
        for k in ("q", "k"):
            if w_is_out_in:
                lhs = w[k]
            else:
                s = transpose_into(c, t1[:, 0:P], w[k], M[0], (s,))
                lhs = t1[:, 0:P]
            pe.need(s)
            s = pe.done(nc.tensor.matmul(M[0][:, 0:P], lhs, c.turn, start=True, stop=True))
            dve.need(s)
            s = dve.done(nc.vector.tensor_copy(wt[k + "r"][:, :], M[0][:, 0:P]))
            if bias is not None:
                pe.need(s)
                s = pe.done(nc.tensor.matmul(M[0][:, 0:1], c.turn, bias[k], start=True, stop=True))
                dve.need(s)
                s = dve.done(nc.vector.tensor_copy(bcol[k + "r"][:, :], M[0][:, 0:1]))
        pe.need(raw_in, s)
        for g in range(GV):
            mm = nc.tensor.matmul(M[0][:, g * D:(g + 1) * D], dup_raw[:, g * P:(g + 1) * P], wt["o"][:, :], start=True, stop=True)
        dve.need(pe.done(mm))
        s = dve.done(nc.vector.tensor_copy(wo2[:, :, :], M[0][:, 0:GV * D].rearrange("p (g d) -> p g d", g=GV)))
        weights_ready = s
        bias_of = {k: (0.0 if bias is None else (bias[k] if k in ("q", "k") else bcol[k][:, 0:1]))
                   for k in ("q", "qr", "k", "kr")}

        mread = [weights_ready, weights_ready]
        scored, maxed, exped, normed, turned, high, moved, pv_done = {}, {}, {}, {}, {}, {}, {}, {}
        out_read = {}
        ready = {}
        st = {}

        def project(b, k, m):
            last = (b - 1) * H8 - 1
            def pe_part():
                pe.need(weights_ready, mread[m])
                nc.tensor.matmul(M[m][:, 0:N], wt[k][:, :], xnT[:, b * N:(b + 1) * N], start=True, stop=True)
                st[m] = pe.done(nc.tensor.matmul(M[m][:, N:2 * N], wt[k + "r"][:, :], xnT[:, b * N:(b + 1) * N],
                                                 start=True, stop=True))
            def turn_part():
                dve.need(st[m], st.get("t_read"))
                nc.vector.scalar_tensor_tensor(out=t1[:, :], in0=M[m][:, 0:N], scalar=bias_of[k], in1=cos,
                                               op0=ALU.add, op1=ALU.mult)
                mread[m] = dve.done(nc.vector.scalar_tensor_tensor(out=t2[:, :], in0=M[m][:, N:2 * N], scalar=bias_of[k + "r"],
                                                                   in1=sin, op0=ALU.add, op1=ALU.mult))
                pool.need(mread[m], st.get("rot_read"))
                st["t_read"] = pool.done(nc.gpsimd.tensor_tensor(rot[:, :], t1[:, :], t2[:, :], ALU.add))
            def split_part():
                dve.need(st["t_read"], st.get("part_read"))
                if k == "q":
                    dve.chain(nc.vector.tensor_scalar(rot[:, :], rot[:, :], scale, None, ALU.mult))
                dve.chain(nc.vector.tensor_copy(part["hi"][:, :], rot[:, :]))
                st["rot_read"] = dve.done(nc.vector.tensor_tensor(part["lo"][:, :], rot[:, :], part["hi"][:, :].bitcast(F32), ALU.subtract))
            def stack_part(g0):
                def f():
                    pe.need(st["rot_read"], mread[m])
                    for g in (g0, g0 + 1):
                        for n_, pt in enumerate(("hi", "lo")):
                            mm = nc.tensor.matmul(M[m][:, (g - g0) * N:(g - g0 + 1) * N], stack[:, (0 if k == "q" else 2) + n_, g, :],
                                                  part[pt][:, :], start=(n_ == 0), stop=(n_ == 1))
                    st["part_read"] = pe.done(mm)
                    src = M[m].rearrange("p (g n) -> p g n", g=2)
                    if k == "q":
                        act.need(st["part_read"], scored.get(last))
                        mread[m] = act.done(nc.scalar.copy(q[b % 2][:, g0:g0 + 2, :], src))
                        ready.setdefault(b, []).append(mread[m])
                return f
            def rows_part(g0, j0):
                def f():
                    e = act if j0 else dve
                    e.need(mread[m] if j0 else None, st["part_read"], scored.get(last), weights_ready)
                    src = M[m].rearrange("p (g n) -> p g n", g=2)
                    for j in (j0, j0 + 1):
                        dst = kz[b % 2][:, 4 * g0 + j:4 * g0 + j + 5:4, :]
                        mread[m] = e.done(nc.scalar.activation(dst, src, ACT.Copy, scale=rows4[:, j:j + 1]) if j0 else
                                          nc.vector.tensor_scalar(dst, src, rows4[:, j:j + 1], None, ALU.mult))
                    ready.setdefault(b, []).append(mread[m])
                return f
            if k == "q":
                return [pe_part, turn_part, split_part, stack_part(0), stack_part(2)]
            return [pe_part, turn_part, split_part, stack_part(0), rows_part(0, 0), rows_part(0, 2),
                    stack_part(2), rows_part(2, 0), rows_part(2, 2)]

        def project_v(b):
            def pe_part():
                pe.need(mread[0])
                for t in range(TB):
                    mm = nc.tensor.matmul(M[0][:, t * P:(t + 1) * P], xnT[:, b * N + t * P:b * N + (t + 1) * P],
                                          wt["v"][:, :], start=True, stop=True)
                st["v"] = pe.done(mm)
            def rest():
                dve.need(st["v"], zeroed, pv_done.get((b - 1) * H8 - 1))
                for t in range(TB):
                    out = vz[b % 2][:, t, :, :].rearrange("p g (h c) -> p g h c", c=DIAG)
                    hi, lo = out[:, :, :, 0:HD8], out[:, :, :, HD8:2 * HD8]
                    src = M[0][:, t * P:(t + 1) * P].rearrange("p (g h d) -> p g h d", g=GV, d=HD8)
                    if bias is not None:
                        s = dve.chain(nc.vector.tensor_tensor(vb[:, :], M[0][:, t * P:(t + 1) * P], bias["v"], ALU.add))
                        src = vb[:, :].rearrange("p (g h d) -> p g h d", g=GV, d=HD8)
                    dve.chain(nc.vector.tensor_copy(hi, src))
                    s = dve.chain(nc.vector.tensor_tensor(lo, src, hi.bitcast(F32), ALU.subtract))
                mread[0] = s
                ready.setdefault(b, []).append(s)
            return [pe_part, rest]

        def pieces(b):
            return project(b, "q", 0) + project(b, "k", 1) + project_v(b)

        for f in pieces(0):
            f()

        def scores(i):
            b, h = divmod(i, H8)
            pe.need(*ready[b], exped.get(i - 2))
            bank = S[i % 2]
            for t in range(TB):
                o = bank[:, t * N:(t + 1) * N]
                mm = nc.tensor.matmul(o, q[b % 2][:, h // 4, t * P:(t + 1) * P], kz[b % 2][:, h, :], start=True, stop=not causal)
                if causal and t == 0:
                    mm = nc.tensor.matmul(o, c.mask400, c.future0, start=False, stop=True)
                elif causal:
                    mm = nc.tensor.matmul(o[:, P:N], c.mask400, c.future1, start=False, stop=True)
            scored[i] = pe.done(mm)
            dve.need(scored[i], exped.get(i - 4))
            maxed[i] = dve.done(nc.vector.tensor_reduce(nm[:, i % 4, :], bank.rearrange("p (t n) -> p t n", t=TB),
                                                        AX.X, ALU.max, negate=True))

        def exps(i):
            bank = S[i % 2]
            act.need(maxed[i], turned.get(i - 3), normed.get(i - 4))
            for t in range(TB):
                e = nc.scalar.activation(Pr[i % 3][:, t, :], bank[:, t * N:(t + 1) * N], ACT.Exp,
                                         bias=nm[:, i % 4, t:t + 1], accum_out=rsum[:, i % 4, t:t + 1])
            exped[i] = act.done(e)

        def norm(i):
            dve.need(exped[i], normed.get(i - 4))
            pool.need(dve.done(nc.vector.reciprocal(rinv[:, i % 4, :], rsum[:, i % 4, :])))
            normed[i] = pool.done(nc.gpsimd.tensor_tensor(Pr[i % 3][:, :, :], Pr[i % 3][:, :, :],
                                                          spread(rinv[:, i % 4, :], N), ALU.mult))

        def turn(i):
            pe.need(normed[i], moved.get(i - 2))
            for kt in range(TB):
                for t in range(TB):
                    mm = nc.tensor.transpose(PT[i % 2][:, kt * N + t * P:kt * N + (t + 1) * P],
                                             Pr[i % 3][:, t, kt * P:(kt + 1) * P], c.ident)
            turned[i] = pe.done(mm)
            src = PT[i % 2].rearrange("p (k n) -> p k n", k=TB)
            act.need(turned[i], pv_done.get(i - 2))
            high[i] = act.done(nc.scalar.copy(PTh[i % 2][:, :, :], src))

        def low(i):
            src = PT[i % 2].rearrange("p (k n) -> p k n", k=TB)
            dve.need(high[i], pv_done.get(i - 2))
            moved[i] = dve.done(nc.vector.tensor_tensor(PTl[i % 2][:, :, :], src, PTh[i % 2][:, :, :].bitcast(F32), ALU.subtract))

        def weigh(i):
            b, h = divmod(i, H8)
            pe.need(moved[i], out_read.get(b - 2))
            g, hh = divmod(h, HG)
            for kt in range(TB):
                for n_, pr in enumerate((PTh, PTl)):
                    mm = nc.tensor.matmul(O[b % 2][:, g * N:(g + 1) * N], vz[b % 2][:, kt, g, hh * D:(hh + 1) * D],
                                          pr[i % 2][:, kt, :], start=(hh == 0 and kt + n_ == 0),
                                          stop=(hh == HG - 1 and kt == TB - 1 and n_ == 1))
            pv_done[i] = pe.done(mm)

        def finish(b):
            act.need(pv_done[(b + 1) * H8 - 1], st.get("oT_read"))
            out_read[b] = act.done(nc.scalar.copy(oT[:, :, :], O[b % 2].rearrange("p (g n) -> p g n", g=GV)))
            pe.need(out_read[b], mread[1])
            for t in range(TB):
                for g in range(GV):
                    mm = nc.tensor.matmul(M[1][:, t * P:(t + 1) * P], oT[:, g, t * P:(t + 1) * P], wo2[:, g, :],
                                          start=(g == 0), stop=(g == GV - 1))
            st["oT_read"] = pe.done(mm)
            dve.need(st["oT_read"])
            xs = x[:, b * TB:(b + 1) * TB, :]
            mread[1] = dve.done(nc.vector.tensor_tensor(xs, xs, M[1][:, 0:N].rearrange("p (t d) -> p t d", d=D), ALU.add))

        todo = []
        for i in range(NH + 5):
            if i < NH and i % H8 == 0 and i // H8 + 1 < B:
                todo = pieces(i // H8 + 1)
            if 3 <= i < NH + 3:
                turn(i - 3)
            if 2 <= i < NH + 2:
                norm(i - 2)
            if 3 <= i < NH + 3:
                low(i - 3)
            if 4 <= i < NH + 4:
                weigh(i - 4)
            if i < NH:
                scores(i)
            if 1 <= i <= NH:
                exps(i - 1)
            if i >= 5 and (i - 5) % H8 == H8 - 1 or i == NH + 4:
                if (i - 4) // H8 - 1 not in out_read:
                    finish((i - 4) // H8 - 1)
            if todo and i % H8 not in (0, 1, 2, 3, 4):
                for _ in range(2 if i % H8 in (8, 9, 11, 13, 15) else 1):
                    if todo:
                        todo.pop(0)()
        c.stage(f"{name}_end")


def ffn_int8(c, name, x, xn, wq8, wscale):
    nc, pe, act, dve, pool = c.nc, c.pe, c.act, c.dve, c.pool
    G = 4
    with ExitStack() as ctx:
        sb = lambda k, s, dt=F32: ctx.enter_context(nc.sbuf_tensor(f"{name}_{k}", s, dt))
        wf, wT = sb("wf", [P, D]), sb("wT", [P, D], BF16)
        amax, xs, xi = sb("amax", [P, NT]), sb("xscale", [P, NT]), sb("xinv", [P, NT])
        xq = [sb(f"xq{i}", [P, G, D]) for i in range(2)]
        xqT = [sb(f"xqT{i}", [P, G, P], BF16) for i in range(2)]
        ys = [sb(f"y{i}", [P, G, D]) for i in range(2)]
        s = dve.done(nc.vector.tensor_copy(wf[:, :], wq8))
        pe.need(s)
        s = pe.done(nc.tensor.transpose(c.banks[7][:, 0:P], wf[:, :], c.ident))
        dve.need(s)
        w_ready = dve.done(nc.vector.tensor_copy(wT[:, :], c.banks[7][:, 0:P]))
        dve.chain(nc.vector.tensor_reduce(amax[:, :], xn[:, :, :], AX.X, ALU.max, apply_absolute_value=True))
        dve.chain(nc.vector.tensor_scalar(xs[:, :], amax[:, :], 1e-6, float(np.float32(1.0) / np.float32(127.0)),
                                          ALU.max, ALU.mult))
        dve.chain(nc.vector.reciprocal(xi[:, :], xs[:, :]))
        q_done, turned, moved, made, read, added = {}, {}, {}, {}, {}, {}
        ROUND = 12582912.0
        for g in range(NT // G + 2):
            if g < NT // G:
                dve.need(turned.get(g - 2))
                for t in range(G):
                    k = g * G + t
                    s = dve.done(nc.vector.tensor_scalar(xq[g % 2][:, t, :], xn[:, k, :], xi[:, k:k + 1], ROUND,
                                                         ALU.mult, ALU.add))
                dve.need(s)
                dve.chain(nc.vector.tensor_scalar(xq[g % 2][:, :, :], xq[g % 2][:, :, :], ROUND, -128.0,
                                                  ALU.subtract, ALU.max))
                q_done[g] = dve.done(nc.vector.tensor_scalar(xq[g % 2][:, :, :], xq[g % 2][:, :, :], 127.0, None, ALU.min))
            if 1 <= g <= NT // G:
                j = g - 1
                pe.need(q_done[j], moved.get(j - 2))
                for t in range(G):
                    mm = nc.tensor.transpose(c.banks[j % 2][:, t * P:(t + 1) * P], xq[j % 2][:, t, :], c.ident)
                turned[j] = pe.done(mm)
                act.need(turned[j], made.get(j - 2))
                moved[j] = act.done(nc.scalar.copy(xqT[j % 2][:, :, :],
                                                   c.banks[j % 2][:, :].rearrange("p (t q) -> p t q", t=G)))
            if g >= 2:
                j = g - 2
                bank = c.banks[2 + j % 2]
                pe.need(moved[j], w_ready, read.get(j - 2))
                for t in range(G):
                    mm = nc.tensor.matmul(bank[:, t * P:(t + 1) * P], xqT[j % 2][:, t, :], wT[:, :], start=True, stop=True)
                made[j] = pe.done(mm)
                dve.need(made[j], added.get(j - 2))
                for t in range(G):
                    k = j * G + t
                    s = dve.done(nc.vector.scalar_tensor_tensor(out=ys[j % 2][:, t, :], in0=bank[:, t * P:(t + 1) * P],
                                                                scalar=xs[:, k:k + 1], in1=wscale,
                                                                op0=ALU.mult, op1=ALU.mult))
                read[j] = s
                pool.need(s)
                xk = x[:, j * G:(j + 1) * G, :]
                added[j] = pool.done(nc.gpsimd.tensor_tensor(xk, xk, ys[j % 2][:, :, :], ALU.add))
        c.stage(f"{name}_end")


def ffn_ternary(c, name, x, xnT, w1, b1, w2):
    nc, pe, act, dve, pool = c.nc, c.pe, c.act, c.dve, c.pool
    F = w2.shape[1]
    FT = F // P
    with ExitStack() as ctx:
        sb = lambda k, s, dt=F32: ctx.enter_context(nc.sbuf_tensor(f"{name}_{k}", s, dt))
        tern = sb("tern", [P, F])
        w1T, w2T = sb("w1T", [P, FT, P]), sb("w2T", [P, FT, P])
        part, tot, inv = sb("part", [P, 1]), sb("tot", [P, 1]), sb("inv", [P, 1])
        h = [sb(f"h{i}", [P, FT, CH]) for i in range(2)]
        ROUND = 12582912.0
        s = None
        for wsrc, wdst in ((w1.rearrange("p t d -> p (t d)"), w1T), (w2, w2T)):
            dve.chain(nc.vector.tensor_reduce(part[:, :], wsrc, AX.X, ALU.add, apply_absolute_value=True))
            pe.need((dve.sem, dve.count))
            s = pe.done(nc.tensor.matmul(c.banks[7][:, 0:1], c.ones, part[:, :], start=True, stop=True))
            dve.need(s)
            dve.chain(nc.vector.tensor_scalar(tot[:, :], c.banks[7][:, 0:1], 1.0 / (F * D), 1e-8, ALU.mult, ALU.max))
            dve.chain(nc.vector.reciprocal(inv[:, :], tot[:, :]))
            dve.chain(nc.vector.tensor_scalar(tern[:, :], wsrc, inv[:, 0:1], ROUND, ALU.mult, ALU.add))
            dve.chain(nc.vector.tensor_scalar(tern[:, :], tern[:, :], ROUND, -1.0, ALU.subtract, ALU.max))
            dve.chain(nc.vector.tensor_scalar(tern[:, :], tern[:, :], 1.0, None, ALU.min))
            dve.chain(nc.vector.tensor_tensor(tern[:, :], tern[:, :], wsrc, ALU.subtract))
            pe.need(dve.chain(nc.vector.tensor_tensor(tern[:, :], tern[:, :], wsrc, ALU.add)))
            for t in range(FT):
                mm = nc.tensor.transpose(c.banks[6][:, t * P:(t + 1) * P], tern[:, t * P:(t + 1) * P], c.ident)
            s = pe.done(mm)
            dve.need(s)
            s = dve.done(nc.vector.tensor_copy(wdst[:, :, :], c.banks[6][:, :].rearrange("p (t d) -> p t d", t=FT)))
        w_ready = s
        made, gelued, out, read = {}, {}, {}, {}
        NG = NCH * FT
        for i in range(NG + 2):
            if i < NG:
                ch, f = divmod(i, FT)
                pe.need(w_ready, gelued.get(i - 4))
                made[i] = pe.done(nc.tensor.matmul(c.banks[i % 4], w1T[:, f, :], xnT[:, ch * CH:(ch + 1) * CH],
                                                   start=True, stop=True))
                act.need(made[i], out.get(ch - 2))
                gelued[i] = act.done(nc.scalar.activation(h[ch % 2][:, f, :], c.banks[i % 4], ACT.Gelu,
                                                          bias=b1[:, f:f + 1]))
            if i >= FT + 1 and (i - 1) % FT == 0:
                ch = (i - 1) // FT - 1
                bank = c.banks[4 + ch % 2]
                pe.need(gelued[ch * FT + FT - 1], read.get(ch - 2))
                for t in range(CH // P):
                    for f in range(FT):
                        mm = nc.tensor.matmul(bank[:, t * P:(t + 1) * P], h[ch % 2][:, f, t * P:(t + 1) * P],
                                              w2T[:, f, :], start=(f == 0), stop=(f == FT - 1))
                out[ch] = pe.done(mm)
                dve.need(out[ch])
                xs = x[:, ch * 4:(ch + 1) * 4, :]
                read[ch] = dve.done(nc.vector.tensor_tensor(xs, xs, bank[:, :].rearrange("p (t d) -> p t d", d=D), ALU.add))
        assert len(out) == NCH
        c.stage(f"{name}_end")


def chunk_attention(c, name, x, xnT, w, bcol, bv, own1, block):
    nc, pe, act, dve, pool = c.nc, c.pe, c.act, c.dve, c.pool
    NK, CK = N // 32, 32
    scale = float(np.float32(1.0) / np.sqrt(np.float32(D)))
    with ExitStack() as ctx:
        sb = lambda k, s, dt=F32: ctx.enter_context(nc.sbuf_tensor(f"{name}_{k}", s, dt))
        q, k = [sb(f"q{i}", [P, CH]) for i in range(2)], [sb(f"k{i}", [P, CH]) for i in range(2)]
        V = [sb(f"v{i}", [P, CH // P, D]) for i in range(2)]
        mx, z, zi = (sb(n, [P, 2, NK]) for n in ("mx", "z", "zi"))
        E = [sb(f"e{i}", [P, NK, CK]) for i in range(2)]
        W = sb("w", [P, 2, CK])
        Wb = [sb(f"wb{i}", [P, 4, CK]) for i in range(2)]
        WT = [sb(f"wt{i}", [P, P]) for i in range(2)]
        cT = [sb(f"ct{i}", [P, P]) for i in range(2)]
        scored, spread_, wide, mixed, comb, out = {}, {}, {}, {}, {}, {}
        ready = {}
        st = {}

        def project(ch):
            bank = c.banks[0]
            for dst, kk, last in ((q, "q", "r0"), (k, "k", "r1"), (V, "v", "r2")):
                bank = c.banks[{"q": 5, "k": 6, "v": 7}[kk]]
                pe.need(st.get(last))
                if kk == "v":
                    for t in range(CH // P):
                        mm = nc.tensor.matmul(bank[:, t * P:(t + 1) * P], xnT[:, ch * CH + t * P:ch * CH + (t + 1) * P],
                                              w["v"], start=True, stop=True)
                    s = pe.done(mm)
                    dve.need(s, mixed.get((ch - 1) * 4 - 1))
                    st[last] = dve.done(nc.vector.tensor_tensor(
                        V[ch % 2][:, :, :], bank[:, :].rearrange("p (t d) -> p t d", d=D), per_tile(bv, CH // P), ALU.add))
                else:
                    s = pe.done(nc.tensor.matmul(bank[:, :], w[kk], xnT[:, ch * CH:(ch + 1) * CH], start=True, stop=True))
                    act.need(s, scored.get((ch - 1) * 4 - 1))
                    st[last] = act.done(nc.scalar.activation(dst[ch % 2][:, :], bank[:, :], ACT.Identity, bias=bcol[kk]))
            ready[ch] = (st["r0"], st["r1"], st["r2"])

        def softmax(i):
            ch, off, t = i // 4, (i % 4) * P, i % TB
            boff = (i % 4) // TB * N
            bank = c.banks[i % 2]
            pe.need(*ready[ch], spread_.get(i - 2))
            scored[i] = pe.done(nc.tensor.matmul(bank[:, 0:N], q[ch % 2][:, off:off + P], k[ch % 2][:, boff:boff + N],
                                                 start=True, stop=True))
            sc = bank[:, 0:N].rearrange("p (m k) -> p m k", m=NK)
            j = i % 2
            dve.need(scored[i])
            dve.chain(nc.vector.tensor_reduce(mx[:, j, :], sc, AX.X, ALU.max))
            dve.need(wide.get(i - 2))
            spread_[i] = dve.done(nc.vector.tensor_tensor(E[j][:, :, :], sc, spread(mx[:, j, :], CK), ALU.subtract))
            act.need(spread_[i])
            st["exp", i] = act.done(nc.scalar.activation(E[j][:, :, :], E[j][:, :, :], ACT.Exp, scale=scale))

        def combine(i):
            j, t = i % 2, i % TB
            dve.need(st["exp", i])
            dve.chain(nc.vector.tensor_reduce(z[:, j, :], E[j][:, :, :], AX.X, ALU.add))
            dve.chain(nc.vector.reciprocal(zi[:, j, :], z[:, j, :]))
            s = dve.chain(nc.vector.tensor_tensor(zi[:, j, :], zi[:, j, :], own1[:, t * NK:(t + 1) * NK], ALU.mult))
            pool.need(s)
            s = pool.done(nc.gpsimd.tensor_tensor(E[j][:, :, :], E[j][:, :, :], spread(zi[:, j, :], CK), ALU.mult))
            dve.need(s)
            wide[i] = dve.chain(nc.vector.tensor_reduce(W[:, j, :], E[j][:, :, :].rearrange("p m k -> p k m"), AX.X, ALU.add))
            pool.need(wide[i], st.get(("turned", i - 2)))
            s = pool.done(nc.gpsimd.tensor_tensor(Wb[j][:, :, :], per_tile(W[:, j, :], 4), spread(block, CK), ALU.mult))
            pe.need(s, st.get(("t_read", i - 1)))
            s = pe.done(nc.tensor.transpose(c.banks[2][:, j * P:(j + 1) * P], Wb[j][:, :, :].rearrange("p m k -> p (m k)"), c.ident))
            st["turned", i] = s
            act.need(s, mixed.get(i - 2))
            st["t_read", i] = act.done(nc.scalar.copy(WT[j][:, :], c.banks[2][:, j * P:(j + 1) * P]))

        def mix(i):
            j, ch = i % 2, i // 4
            pe.need(st["t_read", i], comb.get(i - 1))
            mixed[i] = pe.done(nc.tensor.matmul(c.banks[3][:, j * P:(j + 1) * P], V[ch % 2][:, i % 4, :], WT[j][:, :],
                                                start=True, stop=True))
            act.need(mixed[i], st.get(("proj", i - 2)))
            comb[i] = act.done(nc.scalar.copy(cT[j][:, :], c.banks[3][:, j * P:(j + 1) * P]))
            pe.need(comb[i], out.get(i - 1))
            st["proj", i] = pe.done(nc.tensor.matmul(c.banks[4][:, j * P:(j + 1) * P], cT[j][:, :], w["o"], start=True, stop=True))
            dve.need(st["proj", i])
            out[i] = dve.done(nc.vector.tensor_tensor(x[:, i, :], x[:, i, :], c.banks[4][:, j * P:(j + 1) * P], ALU.add))

        project(0)
        for i in range(NT + 2):
            if i < NT:
                if i % 4 == 2 and i // 4 + 1 < NCH:
                    project(i // 4 + 1)
                softmax(i)
            if 1 <= i <= NT:
                combine(i - 1)
            if i >= 2:
                mix(i - 2)
        c.stage(f"{name}_end")


NE2, TOPK, HID = 32, 4, 64
CAP = 4 * (T * TOPK) // NE2


def route(c, name, xnT, wg, iota, before, weightT):
    nc, pe, act, dve, pool = c.nc, c.pe, c.act, c.dve, c.pool
    with ExitStack() as ctx:
        sb = lambda k, s, dt=F32: ctx.enter_context(nc.sbuf_tensor(f"{name}_{k}", s, dt))
        sc, wt, chosen, hit, rank = (sb(k, [P, NT, NE2]) for k in ("scores", "wt", "chosen", "hit", "rank"))
        m, z = sb("m", [P, NT]), sb("z", [P, NT])
        top, idx, idf = sb("top", [P, NT, 8]), sb("idx", [P, NT, 8], U32), sb("idf", [P, NT, TOPK])
        tot, run = sb("tot", [P, NT, NE2]), sb("run", [P, NT, NE2])
        half = NT // 2
        for t in range(NT):
            mm = nc.tensor.matmul(c.banks[t // half][:, (t % half) * NE2:(t % half + 1) * NE2],
                                  xnT[:, t * P:(t + 1) * P], wg, start=True, stop=True)
        dve.need(pe.done(mm))
        for b in range(2):
            s = dve.done(nc.vector.tensor_copy(sc[:, b * half:(b + 1) * half, :],
                                               c.banks[b][:, :].rearrange("p (t e) -> p t e", e=NE2)))
        dve.need(s)
        dve.chain(nc.vector.tensor_reduce(m[:, :], sc[:, :, :], AX.X, ALU.max))
        act.need(dve.done(nc.vector.tensor_tensor(sc[:, :, :], sc[:, :, :], spread(m[:, :], NE2), ALU.subtract)))
        dve.need(act.done(nc.scalar.activation(sc[:, :, :], sc[:, :, :], ACT.Exp)))
        dve.chain(nc.vector.tensor_reduce(z[:, :], sc[:, :, :], AX.X, ALU.add))
        dve.chain(nc.vector.reciprocal(z[:, :], z[:, :]))
        dve.chain(nc.vector.tensor_tensor(sc[:, :, :], sc[:, :, :], spread(z[:, :], NE2), ALU.mult))
        for t in range(NT):
            s = dve.done(nc.vector.max(top[:, t, :], sc[:, t, :]))
        dve.need(s)
        for t in range(NT):
            s = dve.done(nc.vector.max_index(idx[:, t, :], top[:, t, :], sc[:, t, :]))
        dve.need(s)
        dve.chain(nc.vector.tensor_copy(idf[:, :, :], idx[:, :, 0:TOPK]))
        for k in range(TOPK):
            s = dve.chain(nc.vector.tensor_tensor(hit[:, :, :], per_tile(iota, NT), spread(idf[:, :, k], NE2), ALU.is_equal))
            if k == 0:
                dve.chain(nc.vector.tensor_copy(chosen[:, :, :], hit[:, :, :]))
                dve.chain(nc.vector.tensor_tensor(wt[:, :, :], hit[:, :, :], spread(top[:, :, k], NE2), ALU.mult))
            else:
                dve.chain(nc.vector.tensor_tensor(chosen[:, :, :], chosen[:, :, :], hit[:, :, :], ALU.add))
                dve.chain(nc.vector.tensor_tensor(hit[:, :, :], hit[:, :, :], spread(top[:, :, k], NE2), ALU.mult))
                dve.chain(nc.vector.tensor_tensor(wt[:, :, :], wt[:, :, :], hit[:, :, :], ALU.add))
        pe.need((dve.sem, dve.count))
        for b in range(2):
            src = chosen[:, b * half:(b + 1) * half, :].rearrange("p t e -> p (t e)")
            nc.tensor.matmul(c.banks[2 + b][:, :], before, src, start=True, stop=True)
            s = pe.done(nc.tensor.matmul(c.banks[4 + b][:, :], c.ones, src, start=True, stop=True))
        dve.need(s)
        for b in range(2):
            w = slice(b * half, (b + 1) * half)
            nc.vector.tensor_copy(rank[:, w, :], c.banks[2 + b][:, :].rearrange("p (t e) -> p t e", e=NE2))
            dve.chain(nc.vector.tensor_copy(tot[:, w, :], c.banks[4 + b][:, :].rearrange("p (t e) -> p t e", e=NE2)))
        dve.chain(nc.vector.memset(run[:, 0, :], 0.0))
        for t in range(1, NT):
            dve.chain(nc.vector.tensor_tensor(run[:, t, :], run[:, t - 1, :], tot[:, t - 1, :], ALU.add))
        dve.chain(nc.vector.tensor_tensor(rank[:, :, :], rank[:, :, :], run[:, :, :], ALU.add))
        dve.chain(nc.vector.tensor_scalar(rank[:, :, :], rank[:, :, :], float(CAP), None, ALU.is_lt))
        pe.need(dve.chain(nc.vector.tensor_tensor(wt[:, :, :], wt[:, :, :], rank[:, :, :], ALU.mult)))
        read = {}
        for q in range(NT // 4):
            pe.need(read.get(q - 2))
            for k in range(4):
                mm = nc.tensor.transpose(c.banks[6 + q % 2][0:NE2, k * P:(k + 1) * P], wt[:, q * 4 + k, :], c.ident)
            act.need(pe.done(mm))
            read[q] = act.done(nc.scalar.copy(weightT[:, q * CH:(q + 1) * CH], c.banks[6 + q % 2][0:NE2, :]))
        c.stage(f"{name}_end")


def experts(c, name, x, xnT, weightT, w1, w3, w2, ws, sel):
    nc, pe, act, dve = c.nc, c.pe, c.act, c.dve
    NP2 = NE2 // 2
    R = NP2 + 1
    with ExitStack() as ctx:
        sb = lambda k, s, dt=F32: ctx.enter_context(nc.sbuf_tensor(f"{name}_{k}", s, dt))
        sg = [sb(f"sg{i}", [P, CH]) for i in range(2)]
        hh = [sb(f"h{i}", [P, CH]) for i in range(3)]
        G, U, Wb, Y = c.banks[0:2], c.banks[2:4], c.banks[4:6], c.banks[6:8]
        made, silu, half, hid, down, added = {}, {}, {}, {}, {}, {}

        def up(i):
            ch, p = divmod(i, R)
            xs = xnT[:, ch * CH:(ch + 1) * CH]
            if p < NP2:
                l1 = w1[:, 2 * p:2 * p + 2, :].rearrange("d e h -> d (e h)")
                l3 = w3[:, 2 * p:2 * p + 2, :].rearrange("d e h -> d (e h)")
            else:
                l1, l3 = ws[0], ws[1]
            pe.need(hid.get(i - 2))
            nc.tensor.matmul(G[i % 2][:, :], l1, xs, start=True, stop=True)
            mm = nc.tensor.matmul(U[i % 2][:, :], l3, xs, start=True, stop=True)
            if p < NP2:
                mm = nc.tensor.matmul(Wb[i % 2][:, :], sel[0:NE2, p * P:(p + 1) * P], weightT[:, ch * CH:(ch + 1) * CH],
                                      start=True, stop=True)
            made[i] = pe.done(mm)
            act.need(made[i], half.get(i - 2))
            silu[i] = act.done(nc.scalar.activation(sg[i % 2][:, :], G[i % 2][:, :], ACT.Silu))
            dve.need(silu[i], down.get(i - 3))
            half[i] = dve.chain(nc.vector.tensor_tensor(hh[i % 3][:, :], sg[i % 2][:, :], U[i % 2][:, :], ALU.mult))
            hid[i] = half[i]
            if p < NP2:
                hid[i] = dve.done(nc.vector.tensor_tensor(hh[i % 3][:, :], hh[i % 3][:, :], Wb[i % 2][:, :], ALU.mult))

        def low(i):
            ch, p = divmod(i, R)
            l2 = w2[:, p, :] if p < NP2 else ws[2]
            bank = Y[ch % 2]
            pe.need(hid[i], added.get(ch - 2))
            for t in range(CH // P):
                mm = nc.tensor.matmul(bank[:, t * P:(t + 1) * P], hh[i % 3][:, t * P:(t + 1) * P], l2,
                                      start=(p == 0 and t == 0), stop=(p == R - 1), skip_group_check=True)
            down[i] = pe.done(mm)
            if p == R - 1:
                dve.need(down[i])
                xs = x[:, ch * 4:(ch + 1) * 4, :]
                added[ch] = dve.done(nc.vector.tensor_tensor(xs, xs, bank[:, :].rearrange("p (t d) -> p t d", d=D), ALU.add))

        for i in range(NCH * R + 2):
            if i < NCH * R:
                up(i)
            if i >= 2:
                low(i - 2)
        c.stage(f"{name}_end")


E3, SL, F3 = 16, 64, 256
ES = E3 * SL
FK = F3 // P
HB = B // 2


def slot_experts(c, name, x, xl, xlT, seT, wg, wu, wd, bgT, buT, bd):
    nc, pe, act, dve, pool = c.nc, c.pe, c.act, c.dve, c.pool
    UT = ES // N
    with ExitStack() as ctx:
        sb = lambda k, s, dt=F32: ctx.enter_context(nc.sbuf_tensor(f"{name}_{k}", s, dt))
        slots = sb("slots", [P, E3, HB * SL])
        eout = lambda ep: slots[:, 2 * ep:2 * ep + 2, :].rearrange("p e r -> p (e r)").rearrange("p (b o) -> p b o", o=D)
        nm, z, zi = sb("nm", [P, 4, 2]), sb("z", [P, 4, 2]), sb("zi", [P, 4, 2])
        scratch = sb("scratch", [P, 4 * ES])
        cut = lambda at, n: scratch[:, at:at + n]
        Ex = [cut(i * 2 * N, 2 * N).rearrange("p (s n) -> p s n", s=2) for i in range(3)]
        Dn = [cut((3 + i) * 2 * N, 2 * N).rearrange("p (t n) -> p t n", t=TB) for i in range(2)]
        g = [cut(i * CH, CH) for i in range(2)]
        h = [cut((2 + i * FK) * CH, FK * CH).rearrange("p (f n) -> p f n", f=FK) for i in range(2)]
        Cx = [cut(i * ES, ES) for i in range(2)]
        CT = [cut((2 + i) * ES, ES).rearrange("p (s n) -> p s n", n=P) for i in range(2)]
        for half in range(2):
            n = HB * UT
            lg, ex, nd, tr, mv, sl, ev = {}, {}, {}, {}, {}, {}, {}
            L, TR, X = c.banks[0:3], c.banks[3:5], c.banks[5:7]

            def logits(i):
                b, u = half * HB + i // UT, i % UT
                pe.need(ex.get(i - 3))
                for s in range(2):
                    mm = nc.tensor.matmul(L[i % 3][:, s * N:(s + 1) * N], seT[:, (2 * u + s) * P:(2 * u + s + 1) * P],
                                          xlT[:, b * N:(b + 1) * N], start=True, stop=True)
                lg[i] = pe.done(mm)
                dve.need(lg[i], ex.get(i - 4))
                s_ = dve.done(nc.vector.tensor_reduce(nm[:, i % 4, :], L[i % 3].rearrange("p (s n) -> p s n", s=2),
                                                      AX.X, ALU.max, negate=True))
                act.need(s_, tr.get(i - 3), nd.get(i - 4))
                for s in range(2):
                    e = nc.scalar.activation(Ex[i % 3][:, s, :], L[i % 3][:, s * N:(s + 1) * N], ACT.Exp,
                                             bias=nm[:, i % 4, s:s + 1], accum_out=z[:, i % 4, s:s + 1])
                ex[i] = act.done(e)
                dve.need(ex[i], nd.get(i - 4))
                pool.need(dve.done(nc.vector.reciprocal(zi[:, i % 4, :], z[:, i % 4, :])))
                nd[i] = pool.done(nc.gpsimd.tensor_tensor(Ex[i % 3][:, :, :], Ex[i % 3][:, :, :],
                                                          spread(zi[:, i % 4, :], N), ALU.mult))

            def turn(i):
                pe.need(nd[i], mv.get(i - 2))
                for s in range(2):
                    for t in range(TB):
                        mm = nc.tensor.transpose(TR[i % 2][:, t * N + s * P:t * N + (s + 1) * P],
                                                 Ex[i % 3][:, s, t * P:(t + 1) * P], c.ident)
                tr[i] = pe.done(mm)
                e = act if i % 2 else dve
                e.need(tr[i], sl.get(i - 2))
                src = TR[i % 2].rearrange("p (t n) -> p t n", t=TB)
                mv[i] = e.done(nc.scalar.copy(Dn[i % 2][:, :, :], src) if i % 2 else
                               nc.vector.tensor_copy(Dn[i % 2][:, :, :], src))

            def gather(i):
                b, u = i // UT, i % UT
                pe.need(mv[i], ev.get(i - 2))
                for t in range(TB):
                    mm = nc.tensor.matmul(X[i % 2][:, 0:N], xl[:, (half * HB + b) * TB + t, :], Dn[i % 2][:, t, :],
                                          start=(t == 0), stop=(t == TB - 1))
                sl[i] = pe.done(mm)
                act.need(sl[i])
                ev[i] = act.done(nc.scalar.copy(slots[:, 4 * u:4 * u + 4, b * SL:(b + 1) * SL],
                                                X[i % 2][:, 0:N].rearrange("p (e s) -> p e s", s=SL)))

            for i in range(n + 3):
                if i < n:
                    logits(i)
                if 2 <= i < n + 2:
                    turn(i - 2)
                if i >= 3:
                    gather(i - 3)
            c.stage(f"{name}_experts{half}")

            made, gel, hid, down, wr = {}, {}, {}, {}, {}

            def up(j):
                e, f = divmod(j, FK)
                pe.need(hid.get(j - 2))
                for m, w in ((0, wg), (2, wu)):
                    mm = nc.tensor.matmul(c.banks[m + j % 2], w[:, e, f * P:(f + 1) * P], slots[:, e, :], start=True, stop=True)
                made[j] = pe.done(mm)
                act.need(made[j], hid.get(j - 2))
                gel[j] = act.done(nc.scalar.activation(g[j % 2], c.banks[j % 2], ACT.Gelu,
                                                       bias=bgT[:, j:j + 1]))
                dve.need(gel[j], down.get(e - 2))
                hid[j] = dve.done(nc.vector.scalar_tensor_tensor(out=h[e % 2][:, f, :], in0=c.banks[2 + j % 2],
                                                                 scalar=buT[:, j:j + 1], in1=g[j % 2],
                                                                 op0=ALU.add, op1=ALU.mult))

            def low(e):
                ep, rows = e // 2, slice((e % 2) * SL, (e % 2) * SL + SL)
                pe.need(hid[e * FK + FK - 1], wr.get(ep - 2))
                for b in range(HB):
                    bank = c.banks[4 + 2 * (ep % 2) + b // 4]
                    for f in range(FK):
                        mm = nc.tensor.matmul(bank[rows, (b % 4) * D:(b % 4 + 1) * D], h[e % 2][:, f, b * SL:(b + 1) * SL],
                                              wd[:, e, f, :], start=(f == 0), stop=(f == FK - 1))
                down[e] = pe.done(mm)
                if e % 2:
                    dve.need(down[e])
                    for q in range(2):
                        s = dve.done(nc.vector.tensor_tensor(
                            eout(ep)[:, 4 * q:4 * q + 4, :], c.banks[4 + 2 * (ep % 2) + q].rearrange("p (b o) -> p b o", o=D),
                            per_tile(bd[:, ep, :], 4), ALU.add))
                    wr[ep] = s

            for e in range(E3 + 1):
                if e < E3:
                    up(e * FK)
                    up(e * FK + 1)
                if e >= 1:
                    low(e - 1)
            c.stage(f"{name}_combine{half}")

            n = HB * TB
            lg, ex, tr, mv, mx, ad = {}, {}, {}, {}, {}, {}

            def logits2(i):
                t = half * n + i
                two = c.ps[:, 2 * (i % 2):2 * (i % 2) + 2, :]
                pe.need(ex.get(i - 2))
                for q in range(2):
                    mm = nc.tensor.matmul(two[:, q, :], xlT[:, t * P:(t + 1) * P], seT[:, q * BANK:(q + 1) * BANK],
                                          start=True, stop=True)
                lg[i] = pe.done(mm)
                dve.need(lg[i], ex.get(i - 4))
                s = dve.done(nc.vector.tensor_reduce(nm[:, i % 4, 0:1], two, AX.XY, ALU.max, negate=True))
                act.need(s, tr.get(i - 2), ad.get(i - 4))
                ex[i] = act.done(nc.scalar.activation(Cx[i % 2].rearrange("p (q n) -> p q n", q=2), two, ACT.Exp,
                                                      bias=nm[:, i % 4, 0:1], accum_out=z[:, i % 4, 0:1]))

            def turn2(i):
                pe.need(ex[i], mv.get(i - 1), mv.get(("a", i - 1)))
                for s in range(ES // P):
                    mm = nc.tensor.transpose(c.banks[4 + s // 4][:, (s % 4) * P:(s % 4 + 1) * P],
                                             Cx[i % 2][:, s * P:(s + 1) * P], c.ident)
                tr[i] = pe.done(mm)
                dve.need(tr[i], mx.get(i - 2))
                act.need(tr[i], mx.get(i - 2))
                mv[i] = dve.done(nc.vector.tensor_copy(CT[i % 2][:, 0:4, :], c.banks[4].rearrange("p (s n) -> p s n", n=P)))
                mv["a", i] = act.done(nc.scalar.copy(CT[i % 2][:, 4:8, :], c.banks[5].rearrange("p (s n) -> p s n", n=P)))

            def mix(i):
                t = half * n + i
                b = i // TB
                pe.need(mv[i], mv["a", i], ad.get(i - 2))
                for s in range(ES // P):
                    mm = nc.tensor.matmul(c.banks[6 + i % 2][:, 0:D], CT[i % 2][:, s, :], eout(s)[:, b, :],
                                          start=(s == 0), stop=(s == ES // P - 1))
                mx[i] = pe.done(mm)
                dve.need(mx[i], ex[i])
                dve.chain(nc.vector.reciprocal(zi[:, i % 4, 0:1], z[:, i % 4, 0:1]))
                ad[i] = dve.done(nc.vector.scalar_tensor_tensor(out=x[:, t, :], in0=c.banks[6 + i % 2][:, 0:D],
                                                                scalar=zi[:, i % 4, 0:1], in1=x[:, t, :],
                                                                op0=ALU.mult, op1=ALU.add))

            for i in range(n + 2):
                if i < n:
                    logits2(i)
                if 1 <= i <= n:
                    turn2(i - 1)
                if i >= 2:
                    mix(i - 2)
            c.stage(f"{name}_end{half}")


H3, HD3 = 16, 64
INNER = H3 * HD3
STEPS = 3
HP = H3 // 2


def iterated_attention(c, name, x, xnT, w, brow, gamma, beta):
    nc, pe, act, dve, pool = c.nc, c.pe, c.act, c.dve, c.pool
    S, PT, O, TQ, M = c.banks[0:2], c.banks[2:4], c.banks[4:6], c.banks[6], c.banks[7]
    with ExitStack() as ctx:
        sb = lambda k, s, dt=F32: ctx.enter_context(nc.sbuf_tensor(f"{name}_{k}", s, dt))
        q = [sb(f"q{i}", [P, HP, N]) for i in range(STEPS + 1)]
        k = [sb(f"k{i}", [P, HP, N]) for i in range(2)]
        V = [sb(f"v{i}", [P, TB, INNER]) for i in range(2)]
        wk = [sb(f"t{i}", [P, INNER]) for i in range(TB)]
        sq, move = sb("sq", [P, INNER]), sb("move", [P, HP, N])
        ss, rs, v_, t_ = (sb(n_, [P, TB, H3]) for n_ in ("ss", "rs", "var", "newton"))
        Pr = [sb(f"p{i}", [P, TB, N]) for i in range(3)]
        PTs = [sb(f"pt{i}", [P, TB, N]) for i in range(2)]
        nm = sb("nm", [P, 4, TB])
        rsum, rinv = sb("rsum", [P, 4, 2, TB]), sb("rinv", [P, 2, 2, TB])
        on = [sb(f"on{i}", [P, TB, 2, HD3]) for i in range(2)]
        y = [sb(f"y{i}", [P, NT, D]) for i in range(STEPS - 1)]
        moved2 = sb("moved2", [P, STEPS - 1, B])
        tot, flag = sb("tot", [P, STEPS - 1]), sb("flag", [P, STEPS - 1], U32)

        for kk in ("q", "k"):
            for m in (w[kk], brow[kk]):
                m3 = m.rearrange("p (h d) -> p h d", d=HD3)
                dve.chain(nc.vector.tensor_reduce(ss[:, 0, :], m3, AX.X, ALU.add))
                dve.chain(nc.vector.tensor_scalar(ss[:, 0, :], ss[:, 0, :], 1.0 / HD3, None, ALU.mult))
                dve.chain(nc.vector.tensor_tensor(m3, m3, spread(ss[:, 0, :], HD3), ALU.subtract))
        centred = (dve.sem, dve.count)

        st = {}
        ready = {}
        index = lambda b, s, h: (b * STEPS + s) * H3 + h
        scored, exped, turned, moved, pv, pair_read, newq, ydone, on_read = {}, {}, {}, {}, {}, {}, {}, {}, {}
        squared = {}

        def pieces(b):
            out = []
            pend = []

            def product(kk, t, half, then):
                def f():
                    while pend:
                        pend.pop(0)()
                    pe.need(centred, st.get("m"))
                    st["mm"] = pe.done(nc.tensor.matmul(M, xnT[:, b * N + t * P:b * N + (t + 1) * P],
                                                        w[kk][:, half * BANK:(half + 1) * BANK], start=True, stop=True))
                    pend.append(then)
                return f

            for kk in ("q", "k"):
                for t in range(TB):
                    for half in range(2):
                        def then(kk=kk, t=t, half=half):
                            dve.need(st["mm"], st.get(("wk", t)))
                            w_ = slice(half * BANK, (half + 1) * BANK)
                            st["m"] = dve.done(nc.vector.tensor_tensor(wk[t][:, w_], M, brow[kk][:, w_], ALU.add))
                        out.append(product(kk, t, half, then))

                    def sums(t=t):
                        while pend:
                            pend.pop(0)()
                        act.need(st["m"], st.get("sq"))
                        s = act.done(nc.scalar.activation(sq[:, :], wk[t][:, :], ACT.Square))
                        dve.need(s, st.get("rs_read"))
                        st["sq"] = dve.done(nc.vector.tensor_reduce(ss[:, t, :], sq[:, :].rearrange("p (h d) -> p h d", d=HD3),
                                                                    AX.X, ALU.add))
                    out.append(sums)

                def scale():
                    dve.need(st["sq"])
                    rsqrt_into(c, rs[:, :, :], ss[:, :, :], (v_[:, :, :], t_[:, :, :]), 1.0 / HD3, 1e-5)
                    pool.need((dve.sem, dve.count))
                    for t in range(TB):
                        w3 = wk[t][:, :].rearrange("p (h d) -> p h d", d=HD3)
                        st["rs_read"] = pool.done(nc.gpsimd.tensor_tensor(w3, w3, spread(rs[:, t, :], HD3), ALU.mult))
                out.append(scale)
                for t in range(TB):
                    for half in range(2):
                        def turn_(kk=kk, t=t, half=half):
                            pe.need(st["rs_read"], st["m"])
                            for j in range(4):
                                mm = nc.tensor.transpose(M[:, j * P:(j + 1) * P],
                                                         wk[t][:, (half * 4 + j) * P:(half * 4 + j + 1) * P], c.ident)
                            st["wk", t] = pe.done(mm)
                            dst = q[0] if kk == "q" else k[b % 2]
                            act.need(st["wk", t], scored.get(index(b - 1, 0, H3 - 1)) if kk == "q" else
                                     scored.get(index(b - 2, STEPS - 1, H3 - 1)),
                                     squared.get((b - 1, 0)) if kk == "q" else None)
                            st["m"] = act.done(nc.scalar.activation(
                                dst[:, half * 4:half * 4 + 4, t * P:(t + 1) * P], M.rearrange("p (j n) -> p j n", n=P),
                                ACT.Identity, bias=beta, scale=gamma))
                        out.append(turn_)
            for t in range(TB):
                for half in range(2):
                    def then(t=t, half=half):
                        dve.need(st["mm"], pv.get(index(b - 2, STEPS - 1, H3 - 1)))
                        w_ = slice(half * BANK, (half + 1) * BANK)
                        st["m"] = dve.done(nc.vector.tensor_tensor(V[b % 2][:, t, w_], M, brow["v"][:, w_], ALU.add))
                    out.append(product("v", t, half, then))

            def end():
                while pend:
                    pend.pop(0)()
                ready[b] = ((act.sem, act.count), (dve.sem, dve.count))
            out.append(end)
            return out

        def scores(i, b, s, h):
            hp, rows = h // 2, slice((h % 2) * HD3, (h % 2) * HD3 + HD3)
            pe.need(*ready[b], newq.get((b, s, hp)), exped.get(i - 2))
            for t in range(TB):
                mm = nc.tensor.matmul(S[i % 2][:, t * N:(t + 1) * N], q[s][rows, hp, t * P:(t + 1) * P],
                                      k[b % 2][rows, hp, :], start=True, stop=True)
            scored[i] = pe.done(mm)
            dve.need(scored[i], exped.get(i - 4))
            dve.chain(nc.vector.tensor_reduce(nm[:, i % 4, :], S[i % 2].rearrange("p (t n) -> p t n", t=TB),
                                              AX.X, ALU.max, negate=True))
            m = dve.done(nc.vector.tensor_scalar(nm[:, i % 4, :], nm[:, i % 4, :], 1.0 / 8.0, None, ALU.mult))
            act.need(m, turned.get(i - 3), pair_read.get(i // 2 - 4))
            for t in range(TB):
                e = nc.scalar.activation(Pr[i % 3][:, t, :], S[i % 2][:, t * N:(t + 1) * N], ACT.Exp,
                                         bias=nm[:, i % 4, t:t + 1], scale=1.0 / 8.0,
                                         accum_out=rsum[:, (i // 2) % 4, h % 2, t:t + 1])
            exped[i] = act.done(e)

        def turn(i):
            pe.need(exped[i], moved.get(i - 2))
            for kt in range(TB):
                for t in range(TB):
                    mm = nc.tensor.transpose(PT[i % 2][:, kt * N + t * P:kt * N + (t + 1) * P],
                                             Pr[i % 3][:, t, kt * P:(kt + 1) * P], c.ident)
            turned[i] = pe.done(mm)
            dst, src = PTs[i % 2][:, :, :], PT[i % 2].rearrange("p (k n) -> p k n", k=TB)
            e = dve if i % 3 else act
            e.need(turned[i], pv.get(i - 2))
            moved[i] = e.done(nc.vector.tensor_copy(dst, src) if i % 3 else nc.scalar.copy(dst, src))

        def weigh(i, b, s, h):
            pr = i // 2
            pe.need(moved[i], pair_read.get(pr - 2))
            for t in range(TB):
                for kt in range(TB):
                    mm = nc.tensor.matmul(O[pr % 2][:, t * P + (h % 2) * HD3:t * P + (h % 2 + 1) * HD3],
                                          PTs[i % 2][:, kt, t * P:(t + 1) * P], V[b % 2][:, kt, h * HD3:(h + 1) * HD3],
                                          start=(kt == 0), stop=(kt == TB - 1))
            pv[i] = pe.done(mm)

        def pair_end(i, b, s, h):
            pr, hp = i // 2, h // 2
            dve.need(pv[i], exped[i], on_read.get(pr - 2))
            dve.chain(nc.vector.reciprocal(rinv[:, pr % 2, :, :], rsum[:, pr % 4, :, :]))
            for t in range(TB):
                r = dve.done(nc.vector.tensor_tensor(
                    on[pr % 2][:, t, :, :], O[pr % 2][:, t * P:(t + 1) * P].rearrange("p (e d) -> p e d", d=HD3),
                    spread(rinv[:, pr % 2, :, t], HD3), ALU.mult))
            pair_read[pr] = r
            pe.need(r, st.get("tq"))
            for t in range(TB):
                mm = nc.tensor.transpose(TQ[:, t * P:(t + 1) * P], on[pr % 2][:, t, :, :].rearrange("p e d -> p (e d)"), c.ident)
            on_read[pr] = pe.done(mm)
            act.need(on_read[pr], ydone.get((b - 1, s)), squared.get((b - 1, s)), squared.get((b - 1, s + 1)),
                     scored.get(index(b - 1, s + 1, H3 - 1)) if s + 1 < STEPS else None)
            newq[b, s + 1, hp] = act.done(nc.scalar.copy(q[s + 1][:, hp, :], TQ[:, 0:N]))
            st["tq"] = newq[b, s + 1, hp]

        def step_end(b, s):
            pe.need(newq[b, s + 1, HP - 1])
            for t in range(TB):
                for hp in range(HP):
                    mm = nc.tensor.matmul(TQ[:, t * P:(t + 1) * P], q[s + 1][:, hp, t * P:(t + 1) * P], w["o"][:, hp, :],
                                          start=(hp == 0), stop=(hp == HP - 1))
            ydone[b, s] = pe.done(mm)
            dve.need(ydone[b, s])
            dst = y[s][:, b * TB:(b + 1) * TB, :] if s < STEPS - 1 else \
                xnT[:, b * N:(b + 1) * N].rearrange("p (t d) -> p t d", d=D)
            st["tq"] = dve.done(nc.vector.tensor_copy(dst, TQ[:, 0:N].rearrange("p (t d) -> p t d", d=D)))
            if s < STEPS - 1:
                pool.need(newq[b, s + 1, HP - 1], st.get("move"))
                r = pool.done(nc.gpsimd.tensor_tensor(move[:, :, :], q[s + 1][:, :, :], q[s][:, :, :], ALU.subtract))
                act.need(r)
                st["move"] = squared[b, s] = act.done(nc.scalar.activation(move[:, :, :], move[:, :, :], ACT.Square,
                                                                          accum_out=moved2[:, s, b:b + 1]))

        for f in pieces(0):
            f()
        order = [(b, s, h) for b in range(B) for s in range(STEPS) for h in range(H3)]
        todo = []
        NI = len(order)
        for i in range(NI + 4):
            if i < NI:
                b, s, h = order[i]
                if s == 1 and h == 6 and b + 1 < B:
                    todo = pieces(b + 1)
                scores(i, b, s, h)
            if 1 <= i <= NI:
                turn(i - 1)
            if 2 <= i < NI + 2:
                weigh(i - 2, *order[i - 2])
            if 3 <= i < NI + 3 and order[i - 3][2] % 2:
                pair_end(i - 3, *order[i - 3])
                if order[i - 3][2] == H3 - 1:
                    step_end(*order[i - 3][0:2])
            if todo:
                todo.pop(0)()
            if i < NI and order[i][1:] == (STEPS - 1, H3 - 1):
                while todo:
                    todo.pop(0)()

        dve.need(*[v for v in squared.values()])
        dve.chain(nc.vector.tensor_reduce(tot[:, :], moved2[:, :, :], AX.X, ALU.add))
        pe.need((dve.sem, dve.count), st["tq"])
        r = pe.done(nc.tensor.matmul(M[:, 0:STEPS - 1], c.ones, tot[:, :], start=True, stop=True))
        dve.need(r)
        dve.chain(nc.vector.tensor_scalar(flag[:, :], M[:, 0:STEPS - 1], 1e-8, None, ALU.is_lt))
        y3 = xnT[:, :].rearrange("p (t d) -> p t d", d=D)
        for s in range(STEPS - 2, -1, -1):
            for g in range(4):
                ys, yd = y[s][:, g * 8:(g + 1) * 8, :], y3[:, g * 8:(g + 1) * 8, :]
                m = flag[:, s:s + 1].unsqueeze(2).to_broadcast((P, 8, D))
                r = dve.done(nc.vector.copy_predicated(yd, m, ys))
            dve.need(r)
        for g in range(4):
            xs = x[:, g * 8:(g + 1) * 8, :]
            dve.done(nc.vector.tensor_tensor(xs, xs, y3[:, g * 8:(g + 1) * 8, :], ALU.add))
        c.stage(f"{name}_end")


def program(nc, a, const, out, layers=(0, 1, 2, 3)):
    c = Core(nc, a)
    with ExitStack() as ctx:
        sb = lambda k, s, dt=F32: ctx.enter_context(nc.sbuf_tensor(f"sb_{k}", s, dt))
        x, xnT = sb("x", [P, NT, D]), sb("xnT", [P, T])
        where, width = const_layout(const_columns())
        all_where, _ = const_layout(all_columns())
        c.const = lambda k: const[:, all_where[k][0]:all_where[k][0] + all_where[k][1]]
        table = sb("table", [P, width])
        c.stage("start")
        tab = lambda k: table[:, where[k][0]:where[k][0] + where[k][1]]
        c.ident, c.turn, c.ones = tab("ident"), tab("turn"), tab("ones")
        xd = a["L0_attn_x"].rearrange("b (t p) d -> p (b t) d", p=P)
        table_in = c.load("table", (table[:, :], const[:, 0:width]))
        x_in = c.load("x", *[(x[:, i * 8:(i + 1) * 8, :], xd[:, i * 8:(i + 1) * 8, :]) for i in range(4)])

        early = ExitStack()
        eb = lambda k, s, dt=F32: early.enter_context(nc.sbuf_tensor(f"sb_{k}", s, dt))
        if 0 in layers or 1 in layers:
            wsq, pairs = {}, []
            for k in ("L0_attn_Wq", "L0_attn_Wk", "L0_attn_Wv", "L0_attn_Wo",
                      "L1_attn_Wq", "L1_attn_Wk", "L1_attn_Wv", "L1_attn_W0"):
                wsq[k] = eb(k, [P, D])
                pairs.append((wsq[k][:, :], a[k]))
            wq8 = eb("wq8", [P, D // 4], mybir.dt.int32)
            pairs.append((wq8[:, :], a["L0_ffn_weight_q"]))
            rows = {}
            for k in ("L0_attn_bo", "L0_ffn_weight_scale", "L0_ffn_bias", "L1_attn_bv", "L1_attn_b0", "L1_ffn_b2"):
                rows[k] = eb(k, [P, D])
                pairs.append((rows[k][:, :], row(a[k])))
            bq, bk, b1 = eb("bq1", [P, 1]), eb("bk1", [P, 1]), eb("b1", [P, 4])
            pairs += [(bq[:, :], col(a["L1_attn_bq"])), (bk[:, :], col(a["L1_attn_bk"]))]
            pairs += [(b1[:, f:f + 1], col(a["L1_ffn_b1"][f * P:(f + 1) * P])) for f in range(4)]
            w1, w2 = eb("w1", [P, 4, D]), eb("w2", [P, 4 * P])
            pairs += [(w1[:, :, :], a["L1_ffn_W1"].rearrange("(t p) d -> p t d", p=P)), (w2[:, :], a["L1_ffn_W2"])]
            small_in = c.load("small", *pairs, eng=nc.scalar)
            mask400, future0, future1 = eb("mask400", [P, P], BF16), eb("fut0", [P, N], BF16), eb("fut1", [P, P], BF16)
            c.dve.need(table_in)
            nc.vector.tensor_scalar(mask400[:, :], c.ident, 400.0, None, ALU.mult)
            nc.vector.tensor_copy(future0[:, :], tab("future0"))
            c.dve.done(nc.vector.tensor_copy(future1[:, :], tab("future1")))
            c.mask400, c.future0, c.future1 = mask400[:, :], future0[:, :], future1[:, :]
        experts_in = None
        if 2 in layers:
            w2l, pairs = {}, []
            for k in ("L2_attn_Wq", "L2_attn_Wk", "L2_attn_Wv", "L2_attn_Wo", "L2_ffn_Ws1", "L2_ffn_Ws3", "L2_ffn_Ws2"):
                w2l[k] = eb(k, [P, D])
                pairs.append((w2l[k][:, :], a[k]))
            for k in ("L2_attn_bq", "L2_attn_bk"):
                w2l[k] = eb(k, [P, 1])
                pairs.append((w2l[k][:, :], col(a[k])))
            for k in ("L2_attn_bv", "L2_attn_bo"):
                w2l[k] = eb(k, [P, D])
                pairs.append((w2l[k][:, :], row(a[k])))
            w2l["g"] = eb("wgate", [P, NE2])
            w1e, w3e, w2e = eb("w1e", [P, NE2, HID]), eb("w3e", [P, NE2, HID]), eb("w2e", [P, NE2 // 2, D])
            pairs += [(w2l["g"][:, :], a["L2_ffn_Wg"]),
                      (w1e[:, :, :], a["L2_ffn_W1"].rearrange("e d h -> d e h")),
                      (w3e[:, :, :], a["L2_ffn_W3"].rearrange("e d h -> d e h")),
                      (w2e[:, :, :], a["L2_ffn_W2"].rearrange("(q e) h d -> (e h) q d", e=2))]
            experts_in = c.load("experts", *pairs, eng=nc.gpsimd)
        for l in c.lanes:
            l.need(table_in, x_in, *([small_in] if 0 in layers or 1 in layers else []))
        c.stage("loaded")

        def add_bias(*b):
            for v in b:
                for g in range(4):
                    xs = x[:, g * 8:(g + 1) * 8, :]
                    s = c.pool.done(nc.gpsimd.tensor_tensor(xs, xs, per_tile(v, 8), ALU.add))
                c.pool.need(s)

        if 0 in layers:
            with nc.sbuf_tensor("xn", [P, NT, D], F32) as xn:
                norm_tiles(c, "norm0", x, xn, NT, xnT)
                add_bias(rows["L0_attn_bo"][:, :], rows["L0_ffn_bias"][:, :])
                c.stage("ffn0")
                ffn_int8(c, "int8", x, xn, wq8[:, :].bitcast(I8), rows["L0_ffn_weight_scale"][:, :])
            attention8(c, "attn0", x, xnT, {k: wsq[f"L0_attn_W{k}"][:, :] for k in "qkvo"},
                       (tab("cos0"), tab("sin0")), 1.0 / HD8, tab("rows4"), None, True, True)
        if 1 in layers:
            norm_tiles(c, "norm1", x, None, NT, xnT)
            add_bias(rows["L1_attn_b0"][:, :], rows["L1_ffn_b2"][:, :])
            c.stage("attn1")
            w = {k: wsq[f"L1_attn_W{k}"][:, :] for k in "qkv"} | {"o": wsq["L1_attn_W0"][:, :]}
            attention8(c, "attn1", x, xnT, w, (tab("cos1"), tab("sin1")), float(np.float32(1.0) / np.sqrt(np.float32(HD8))), tab("rows4"),
                       {"q": bq[:, 0:1], "k": bk[:, 0:1], "v": rows["L1_attn_bv"][:, :]}, False, False)
            ffn_ternary(c, "tern", x, xnT, w1[:, :, :], b1, w2[:, :])
        if 2 in layers:
            for l in c.lanes:
                l.need(experts_in)
            norm_tiles(c, "norm2", x, None, NT, xnT)
            add_bias(w2l["L2_attn_bo"][:, :])
            c.stage("attn2")
            chunk_attention(c, "chunks", x, xnT, {k: w2l[f"L2_attn_W{k}"][:, :] for k in "qkvo"},
                            {k: w2l[f"L2_attn_b{k}"][:, 0:1] for k in "qk"}, w2l["L2_attn_bv"][:, :],
                            tab("own1"), tab("block"))
            with nc.sbuf_tensor("weightT", [NE2, T], F32) as weightT:
                route(c, "route", xnT, w2l["g"][:, :], tab("expert"), tab("before"), weightT)
                experts(c, "moe", x, xnT, weightT, w1e, w3e, w2e,
                        [w2l[f"L2_ffn_Ws{k}"][:, :] for k in (1, 3, 2)], tab("sel"))
        early.close()
        c.stage("late")
        if 3 in layers:
            with ExitStack() as late:
                lb = lambda k, s, dt=F32: late.enter_context(nc.sbuf_tensor(f"sb_{k}", s, dt))
                xl, xlT = lb("xl", [P, NT, D]), lb("xlT", [P, T])
                seT, se = lb("seT", [P, ES]), lb("se", [P, ES // P, D])
                wg, wu, wd = lb("wg", [P, E3, F3]), lb("wu", [P, E3, F3]), lb("wd", [P, E3, FK, D])
                bgu, bgT, buT = lb("bgu", [E3 * FK, 2, P]), lb("bgT", [P, E3 * FK]), lb("buT", [P, E3 * FK])
                bd = lb("bd", [P, E3 // 2, D])
                rows = {k: lb(k, [P, D]) for k in ("L3_ffn_norm_g", "L3_ffn_norm_b", "L3_ffn_slot_g", "L3_ffn_slot_b",
                                                   "L3_attn_bo")}
                sc = lb("scale", [P, 1])
                bdr = a["L3_ffn_bd"].rearrange("(q e) o -> e q o", e=2)
                slots_in = c.load("slots_w", (se[:, :, :], a["L3_ffn_slot_embeds"].rearrange("(q e) s d -> (e s) q d", e=2)),
                                  (sc[:, :], row(a["L3_ffn_scale"])), *[(v[:, :], row(a[k])) for k, v in rows.items()],
                                  (bgu[:, 0, :], a["L3_ffn_bg"].rearrange("e (f p) -> (e f) p", p=P)),
                                  (bgu[:, 1, :], a["L3_ffn_bu"].rearrange("e (f p) -> (e f) p", p=P)),
                                  (bd[0:SL, :, :], bdr[0].partition_broadcast(SL)),
                                  (bd[SL:P, :, :], bdr[1].partition_broadcast(SL)))
                ffn_in = c.load("ffn_w", (wg[:, :, :], a["L3_ffn_Wg"].rearrange("e d f -> d e f")),
                                (wu[:, :, :], a["L3_ffn_Wu"].rearrange("e d f -> d e f")),
                                *[(wd[:, :, f, :], a["L3_ffn_Wd"].rearrange("e (f p) o -> f p e o", p=P)[f]) for f in range(FK)])
                norm_tiles(c, "norm3", x, xl, NT, xnT)
                for l in c.lanes:
                    l.need(slots_in)
                add_bias(rows["L3_attn_bo"][:, :])
                norm_tiles(c, "norm_ffn", xl, xl, NT, xlT, affine=(per_row(rows["L3_ffn_norm_g"]), per_row(rows["L3_ffn_norm_b"])))
                norm_tiles(c, "norm_slot", se, se, ES // P, None, affine=(per_row(rows["L3_ffn_slot_g"]), per_row(rows["L3_ffn_slot_b"])), groups=2)
                s = c.dve.done(nc.vector.tensor_scalar(se[:, :, :], se[:, :, :], sc[:, 0:1], None, ALU.mult))
                c.pe.need(s)
                for k in range(ES // P):
                    mm = nc.tensor.transpose(c.banks[k // 4][:, (k % 4) * P:(k % 4 + 1) * P], se[:, k, :], c.ident)
                for k in range(2):
                    nk = E3 * FK
                    mm = nc.tensor.transpose(c.banks[2][:, k * nk:(k + 1) * nk], bgu[:, k, :], c.ident[0:nk, 0:nk])
                c.dve.need(c.pe.done(mm))
                for k in range(2):
                    nc.vector.tensor_copy(seT[:, k * BANK:(k + 1) * BANK], c.banks[k])
                nc.vector.tensor_copy(bgT[:, :], c.banks[2][:, 0:nk])
                c.dve.done(nc.vector.tensor_copy(buT[:, :], c.banks[2][:, nk:2 * nk]))
                for l in c.lanes:
                    l.need(ffn_in)
                c.stage("slots")
                slot_experts(c, "slotmoe", x, xl, xlT, seT, wg, wu, wd, bgT, buT, bd)
            with ExitStack() as late:
                lb = lambda k, s, dt=F32: late.enter_context(nc.sbuf_tensor(f"sb_{k}", s, dt))
                w3 = {k: lb(f"L3w{k}", [P, INNER]) for k in "qkv"}
                wo3 = lb("L3wo", [P, HP, D])
                b3 = {k: lb(f"L3b{k}", [P, INNER]) for k in "qkv"}
                gam, bet = lb("gamma", [P, 1]), lb("beta", [P, 1])
                attn_in = c.load("attn3_w", *[(w3[k][:, :], a[f"L3_attn_W{k}"]) for k in "qkv"],
                                 *[(b3[k][:, :], row(a[f"L3_attn_b{k}"])) for k in "qkv"],
                                 (wo3[:, :, :], a["L3_attn_Wo"].rearrange("(q p) o -> p q o", p=P)),
                                 *[(dst[HD3 * e:HD3 * (e + 1), :], col(a[k])) for e in range(2)
                                   for dst, k in ((gam, "L3_attn_gamma"), (bet, "L3_attn_beta"))])
                for l in c.lanes:
                    l.need(attn_in)
                iterated_attention(c, "attn3", x, xnT, {k: v[:, :] for k, v in w3.items()} | {"o": wo3},
                                   {k: v[:, :] for k, v in b3.items()}, gam[:, 0:1], bet[:, 0:1])
        yd = out.rearrange("b (t p) d -> p (b t) d", p=P)
        stored = nc.alloc_semaphore("stored")
        for i in range(4):
            nc.sync.dma_start(yd[:, i * 8:(i + 1) * 8, :], x[:, i * 8:(i + 1) * 8, :]).then_inc(stored, 16)
        nc.sync.wait_ge(stored, 64)


def kernel(**inputs):
    import concourse.bacc as bacc
    from concourse.bass_utils import run_bass_kernel_spmd

    nc = bacc.Bacc("TRN2", target_bir_lowering=False, num_devices=1)
    arrays = {k: np.ascontiguousarray(v) for k, v in inputs.items()}
    arrays["L0_ffn_weight_q"] = arrays["L0_ffn_weight_q"].view(np.int32)
    arrays["const"] = np.concatenate(list(all_columns().values()), axis=1)
    aps = {k: nc.dram_tensor(f"in_{k}", v.shape, mybir.dt.from_np(v.dtype), kind="ExternalInput").ap()
           for k, v in arrays.items()}
    out = nc.dram_tensor("out", (B, N, D), F32, kind="ExternalOutput").ap()
    program(nc, aps, aps["const"], out)
    r = run_bass_kernel_spmd(nc, [{f"in_{k}": v for k, v in arrays.items()}], core_ids=[0])
    return r.results[0]["out"]
```

```python
from contextlib import ExitStack

import numpy as np

import concourse.bass as bass
from concourse import mybir

F32 = mybir.dt.float32
F32R = mybir.dt.float32r
BF16 = mybir.dt.bfloat16
I8 = mybir.dt.int8
U32 = mybir.dt.uint32
ALU = mybir.AluOpType
ACT = mybir.ActivationFunctionType
AX = mybir.AxisListType

P = 128
D = 128
B, N = 16, 256
T = B * N
NT = T // P
TB = N // P
CH = 512
NCH = T // CH
H8, HD8 = 16, 8
BANK = 512


def rope_tables():
    pos = np.arange(N, dtype=np.float32)[:, None]
    out = []
    for d in (HD8, D):
        inv = (np.float32(1.0) / np.power(np.float32(10000.0), np.arange(0, d, 2, dtype=np.float32) / np.float32(d)))
        ang = pos * inv.astype(np.float32)[None, :]
        for f in (np.cos, np.sin):
            t = np.repeat(f(ang).astype(np.float32), 2, axis=1)
            out.append(np.tile(t, (1, D // d)).T)
    return out


def const_columns():
    p = np.arange(P)
    c = {"ident": np.eye(P)}
    turn = np.zeros((P, P))
    turn[p ^ 1, p] = np.where(p % 2 == 0, -1.0, 1.0)
    c["turn"] = turn
    c["cos0"], c["sin0"], c["cos1"], c["sin1"] = rope_tables()
    c["ones"] = np.ones((P, P))
    c["before"] = p[:, None] < p[None, :]
    k = np.arange(N)
    c["future0"] = np.where(k[None, :] > p[:, None], -25.0, 0.0)
    c["future1"] = np.where(p[None, :] > p[:, None], -25.0, 0.0)
    own = np.zeros((P, TB, 8))
    for t in range(TB):
        own[p, t, (t * P + p) // 32] = 1.0
    c["own1"] = (1.0 + own).reshape(P, TB * 8)
    c["block"] = (p[:, None] // 32) == np.arange(4)[None, :]
    c["expert"] = np.tile(np.arange(32), (P, 1))
    sel = np.zeros((P, 16, P))
    for pair in range(16):
        for m in range(P):
            sel[2 * pair + m // 64::32, pair, m][0:2] = 1.0
    c["sel"] = sel.reshape(P, 16 * P)
    return {k: np.ascontiguousarray(v, dtype=np.float32) for k, v in c.items()}


def stack_columns():
    r = np.arange(P)
    j, part, d = r // 32, r // HD8 % 4, r % HD8
    stack = np.zeros((P, 4, 4, P))
    kinds = (part < 2, part >= 2, part % 2 == 0, part % 2 == 1)
    for n, on in enumerate(kinds):
        for g in range(4):
            stack[(32 * g + HD8 * j + d)[on], n, g, r[on]] = 1.0
    dup = np.zeros((P, 2, P))
    for g in range(2):
        dup[64 * g + HD8 * (r // 16) + r % HD8, g, r] = 1.0
    return {"stack": stack.reshape(P, -1).astype(np.float32), "dup": dup.reshape(P, -1).astype(np.float32)}


def all_columns():
    return const_columns() | stack_columns()


def const_layout(columns):
    at, where = 0, {}
    for k, v in columns.items():
        where[k] = (at, v.shape[1])
        at += v.shape[1]
    return where, at


class Lane:

    def __init__(self, nc, eng, name):
        self.nc, self.eng, self.name = nc, eng, name
        self.seen = {}
        self.sem, self.count = None, 0

    def stage(self, name):
        self.sem, self.count = self.nc.alloc_semaphore(f"{name}_{self.name}"), 0

    def done(self, ins):
        ins.then_inc(self.sem, 1)
        self.count += 1
        return (self.sem, self.count)

    def need(self, *steps):
        for s in steps:
            if s is None:
                continue
            sem, v = s
            if self.seen.get(sem.name, 0) < v:
                self.eng.wait_ge(sem, v)
                self.seen[sem.name] = v

    def chain(self, ins):
        s = self.done(ins)
        self.need(s)
        return s


class Core:
    def __init__(self, nc, a):
        self.nc, self.a = nc, a
        self.pe = Lane(nc, nc.tensor, "pe")
        self.act = Lane(nc, nc.scalar, "act")
        self.dve = Lane(nc, nc.vector, "dve")
        self.pool = Lane(nc, nc.gpsimd, "pool")
        self.sp = Lane(nc, nc.sync, "sp")
        self.lanes = [self.pe, self.act, self.dve, self.pool]
        self.ps = nc.alloc_psum_tensor("psum", [P, 8, BANK], F32)
        self.banks = [self.ps[:, i, :] for i in range(8)]

    def stage(self, name):
        last = [(l.sem, l.count) for l in self.lanes if l.sem is not None and l.count]
        for l in self.lanes + [self.sp]:
            l.need(*last)
        for l in self.lanes:
            l.stage(name)

    def load(self, name, *pairs, eng=None):
        sem = self.nc.alloc_semaphore(f"{name}_landed")
        for dst, src in pairs:
            (eng or self.nc.sync).dma_start(dst, src).then_inc(sem, 16)
        return (sem, 16 * len(pairs))


def row(v):
    return v.partition_broadcast(P)


def col(v):
    return v.rearrange("(p o) -> p o", o=1)


def per_row(t):
    return t[:, :]


def per_tile(v, n):
    return v.unsqueeze(1).to_broadcast((v.shape[0], n, v.shape[1]))


def spread(v, n):
    return v.unsqueeze(2).to_broadcast((v.shape[0], v.shape[1], n))


def rsqrt_into(c, out, var, tmp, scale, eps):
    nc, act, dve = c.nc, c.act, c.dve
    v, t = tmp
    act.need(dve.chain(nc.vector.tensor_scalar(v, var, scale, eps, ALU.mult, ALU.add)))
    act.chain(nc.scalar.activation(out, v, ACT.Ln))
    dve.need(act.done(nc.scalar.activation(out, out, ACT.Exp, scale=-0.5)))
    dve.chain(nc.vector.tensor_tensor(t, out, out, ALU.mult))
    dve.chain(nc.vector.tensor_tensor(t, t, v, ALU.mult))
    dve.chain(nc.vector.tensor_scalar(t, t, -0.5, 1.5, ALU.mult, ALU.add))
    dve.chain(nc.vector.tensor_tensor(out, out, t, ALU.mult))


def norm_tiles(c, name, src, dst, n, dstT=None, affine=None, groups=4, biases=(), landed=None, bias_landed=None):
    nc, pe, act, dve, pool = c.nc, c.pe, c.act, c.dve, c.pool
    with ExitStack() as ctx:
        sb = lambda k, s: ctx.enter_context(nc.sbuf_tensor(f"{name}_{k}", s, F32))
        stats, mv = sb("stats", [P, n, 6]), sb("mv", [P, n, 2])
        nc.scalar.preload_act_table_set("natural_log_exp_and_others")
        rs, v, t = sb("rstd", [P, n]), sb("var", [P, n]), sb("newton", [P, n])
        g = n // groups
        ring = dst if dst is not None else sb("normed", [P, 2 * g, D])
        banks, read = c.banks, {}
        turned = {}
        pool.need(bias_landed)
        for v_ in biases[1:]:
            pool.chain(nc.gpsimd.tensor_tensor(biases[0], biases[0], v_, ALU.add))
        for i in range(groups + 1):
            if i < groups:
                if landed:
                    dve.need(landed[i])
                for k in range(i * g, i * g + g):
                    s = dve.done(nc.vector.bn_stats(stats[:, k, :], src[:, k, :]))
                dve.need(s)
                for k in range(i * g, i * g + g):
                    s = dve.done(nc.vector.bn_aggr(mv[:, k, :], stats[:, k, :]))
                dve.need(s)
                w = slice(i * g, i * g + g)
                rsqrt_into(c, rs[:, w], mv[:, w, 1], (v[:, w], t[:, w]), 1.0, 1e-5)
            if i >= 1:
                j = i - 1
                for k in range(j * g, j * g + g):
                    r = k if dst is not None else k % (2 * g)
                    if dst is None and k >= 2 * g:
                        dve.need(turned[(k - 2 * g) // 4])
                    s = dve.done(nc.vector.tensor_scalar(ring[:, r, :], src[:, k, :], mv[:, k, 0:1],
                                                         rs[:, k:k + 1], ALU.subtract, ALU.mult))
                    if affine is not None:
                        gamma, beta = affine
                        pool.need(s)
                        pool.chain(nc.gpsimd.tensor_tensor(ring[:, r, :], ring[:, r, :], gamma, ALU.mult))
                        s = pool.done(nc.gpsimd.tensor_tensor(ring[:, r, :], ring[:, r, :], beta, ALU.add))
                    if dstT is not None and k % 4 == 3:
                        q = k // 4
                        pe.need(s, read.get(q - 4))
                        for m in range(4):
                            rr = (k - 3 + m) if dst is not None else (k - 3 + m) % (2 * g)
                            mm = nc.tensor.transpose(banks[q % 4][:, m * P:(m + 1) * P], ring[:, rr, :], c.ident)
                        turned[q] = pe.done(mm)
                        act.need(turned[q])
                        read[q] = act.done(nc.scalar.copy(dstT[:, q * CH:(q + 1) * CH], banks[q % 4][:, :]))
                if biases:
                    pool.need(s)
                    xs = src[:, j * g:(j + 1) * g, :]
                    pool.done(nc.gpsimd.tensor_tensor(xs, xs, per_tile(biases[0], g), ALU.add))
        c.stage(f"{name}_end")


def transpose_into(c, dst, src, bank, before=()):
    c.pe.need(*before)
    s = c.pe.done(c.nc.tensor.transpose(bank[:, 0:P], src, c.ident))
    c.dve.need(s)
    return c.dve.done(c.nc.vector.tensor_copy(dst, bank[:, 0:P]))


def attention8(c, name, x, xnT, w, rope, scale, bias, causal, w_is_out_in):
    nc, pe, act, dve, pool = c.nc, c.pe, c.act, c.dve, c.pool
    cos, sin = rope
    S, PT, O, M = c.banks[0:3], c.banks[3:5], c.banks[5], c.banks[6:8]
    NH = B * H8
    GQ, GV = 4, 2
    HG = H8 // GV
    DIAG = D + 2 * HD8
    with ExitStack() as ctx:
        sb = lambda k, s, dt=F32: ctx.enter_context(nc.sbuf_tensor(f"{name}_{k}", s, dt))
        wt = {k: sb(f"w{k}", [P, D]) for k in ("q", "k", "v", "o", "qr", "kr")}
        bcol = {k: sb(f"b{k}", [P, 1]) for k in ("qr", "kr")}
        q = [sb(f"q{i}", [P, GQ, N], F32R) for i in range(2)]
        ks = [sb(f"k{i}", [P, GQ, N], F32R) for i in range(2)]
        vz = [sb(f"v{i}", [P, TB, GV, HG * DIAG], F32R) for i in range(2)]
        part = {k: sb(f"part_{k}", [P, N], F32R) for k in ("hi", "lo")}
        stack = sb("stack", [P, 4, GQ, P], F32R)
        wo2 = sb("wo2", [P, GV, D])
        vb = sb("vb", [P, D])
        t1, t2, rot = sb("t1", [P, N]), sb("t2", [P, N]), sb("rot", [P, N])
        Pr = sb("p", [P, 4, TB, N])
        PTh = [sb(f"pth{i}", [P, TB, N], F32R) for i in range(2)]
        PTl = [sb(f"ptl{i}", [P, TB, N], F32R) for i in range(2)]
        nm, rsum, rinv = (sb(k, [P, 4, TB]) for k in ("nm", "rsum", "rinv"))
        oT = sb("oT", [P, GV, N])
        for v in vz:
            zeroed = pool.done(nc.gpsimd.memset(v[:, :, :, :].bitcast(F32), 0.0))
        stack_raw, dup_raw = Pr[:, :, :, :].rearrange("p i t n -> p (i t n)"), rot[:, 0:GV * P]
        raw_in = c.load(f"{name}_stack", (stack_raw, c.const("stack")), (dup_raw, c.const("dup")))
        dve.need(raw_in)
        dve.done(nc.vector.tensor_copy(stack[:, :, :, :].rearrange("p a g m -> p (a g m)"), stack_raw))

        s = None
        for k in ("q", "k", "v", "o"):
            if w_is_out_in:
                s = transpose_into(c, wt[k][:, :], w[k], M[0], (s,))
            else:
                s = dve.done(nc.vector.tensor_copy(wt[k][:, :], w[k]))
        for k in ("q", "k"):
            if w_is_out_in:
                lhs = w[k]
            else:
                s = transpose_into(c, t1[:, 0:P], w[k], M[0], (s,))
                lhs = t1[:, 0:P]
            pe.need(s)
            s = pe.done(nc.tensor.matmul(M[0][:, 0:P], lhs, c.turn, start=True, stop=True))
            dve.need(s)
            s = dve.done(nc.vector.tensor_copy(wt[k + "r"][:, :], M[0][:, 0:P]))
            if bias is not None:
                pe.need(s)
                s = pe.done(nc.tensor.matmul(M[0][:, 0:1], c.turn, bias[k], start=True, stop=True))
                dve.need(s)
                s = dve.done(nc.vector.tensor_copy(bcol[k + "r"][:, :], M[0][:, 0:1]))
        pe.need(raw_in, s)
        for g in range(GV):
            mm = nc.tensor.matmul(M[0][:, g * D:(g + 1) * D], dup_raw[:, g * P:(g + 1) * P], wt["o"][:, :], start=True, stop=True)
        dve.need(pe.done(mm))
        s = dve.done(nc.vector.tensor_copy(wo2[:, :, :], M[0][:, 0:GV * D].rearrange("p (g d) -> p g d", g=GV)))
        weights_ready = s
        bias_of = {k: (0.0 if bias is None else (bias[k] if k in ("q", "k") else bcol[k][:, 0:1]))
                   for k in ("q", "qr", "k", "kr")}

        mread = [weights_ready, weights_ready]
        scored, maxed, exped, normed, turned, high, moved, pv_done = {}, {}, {}, {}, {}, {}, {}, {}
        out_read = {}
        ready = {}
        st = {}

        def project(b, k, m, r, r_stack):
            last = (b - 1) * H8 - 1
            def pe_part():
                pe.need(weights_ready, mread[m])
                nc.tensor.matmul(M[m][:, 0:N], wt[k][:, :], xnT[:, b * N:(b + 1) * N], start=True, stop=True)
                st[m] = pe.done(nc.tensor.matmul(M[m][:, N:2 * N], wt[k + "r"][:, :], xnT[:, b * N:(b + 1) * N],
                                                 start=True, stop=True))
            def turn_part():
                dve.need(st[m], st.get("t_read"))
                nc.vector.scalar_tensor_tensor(out=t1[:, :], in0=M[m][:, 0:N], scalar=bias_of[k], in1=cos,
                                               op0=ALU.add, op1=ALU.mult)
                mread[m] = dve.done(nc.vector.scalar_tensor_tensor(out=t2[:, :], in0=M[m][:, N:2 * N], scalar=bias_of[k + "r"],
                                                                   in1=sin, op0=ALU.add, op1=ALU.mult))
                pool.need(mread[m], st.get("rot_read"))
                st["t_read"] = pool.done(nc.gpsimd.tensor_tensor(rot[:, :], t1[:, :], t2[:, :], ALU.add))
            def split_part():
                dve.need(st["t_read"], st.get("part_read"))
                if k == "q":
                    dve.chain(nc.vector.tensor_scalar(rot[:, :], rot[:, :], scale, None, ALU.mult))
                dve.chain(nc.vector.tensor_copy(part["hi"][:, :], rot[:, :]))
                st["rot_read"] = dve.done(nc.vector.tensor_tensor(part["lo"][:, :], rot[:, :], part["hi"][:, :].bitcast(F32), ALU.subtract))
            def stack_part(g0):
                pe.need(st["rot_read"], mread[m])
                for g in (g0, g0 + 1):
                    for n_, pt in enumerate(("hi", "lo")):
                        mm = nc.tensor.matmul(M[m][:, (g - g0) * N:(g - g0 + 1) * N], stack[:, (0 if k == "q" else 2) + n_, g, :],
                                              part[pt][:, :], start=(n_ == 0), stop=(n_ == 1))
                st["part_read"] = pe.done(mm)

            def copy_part(g0):
                act.need(st["part_read"], scored.get(last))
                mread[m] = act.done(nc.scalar.copy((q if k == "q" else ks)[b % 2][:, g0:g0 + 2, :],
                                                   M[m].rearrange("p (g n) -> p g n", g=2)))
                ready.setdefault(b, []).append(mread[m])

            return [(r, 2, pe_part), (r + 1, 0, turn_part), (r + 2, 1, split_part),
                    (r_stack, 2, lambda: stack_part(0)), (r_stack + 1, 0, lambda: copy_part(0)),
                    (r_stack + 1, 2, lambda: stack_part(2)), (r_stack + 2, 0, lambda: copy_part(2))]

        def project_v(b, r):
            def pe_part():
                pe.need(mread[0])
                for t in range(TB):
                    mm = nc.tensor.matmul(M[0][:, t * P:(t + 1) * P], xnT[:, b * N + t * P:b * N + (t + 1) * P],
                                          wt["v"][:, :], start=True, stop=True)
                st["v"] = pe.done(mm)

            def parts(t):
                dve.need(st["v"], zeroed, pv_done.get((b - 1) * H8 - 1))
                out = vz[b % 2][:, t, :, :].rearrange("p g (h c) -> p g h c", c=DIAG)
                hi, lo = out[:, :, :, 0:HD8], out[:, :, :, HD8:2 * HD8]
                src = M[0][:, t * P:(t + 1) * P].rearrange("p (g h d) -> p g h d", g=GV, d=HD8)
                if bias is not None:
                    s = dve.chain(nc.vector.tensor_tensor(vb[:, :], M[0][:, t * P:(t + 1) * P], bias["v"], ALU.add))
                    src = vb[:, :].rearrange("p (g h d) -> p g h d", g=GV, d=HD8)
                dve.chain(nc.vector.tensor_copy(hi, src))
                mread[0] = dve.chain(nc.vector.tensor_tensor(lo, src, hi.bitcast(F32), ALU.subtract))
                ready.setdefault(b, []).append(mread[0])
            return [(r, 2, pe_part), (r + 1, 0, lambda: parts(0)), (r + 2, 0, lambda: parts(1))]

        def pieces(b):
            out = project(b, "q", 0, 1, 5) + project(b, "k", 1, 8, 11) + project_v(b, 13)
            return sorted(out, key=lambda o: o[0:2])

        for _, _, f in pieces(0):
            f()

        def scores(i):
            b, h = divmod(i, H8)
            pe.need(*ready[b], exped.get(i - 3))
            bank, rows = S[i % 3], slice(32 * (h % 4), 32 * (h % 4) + 32)
            for t in range(TB):
                o = bank[:, t * N:(t + 1) * N]
                mm = nc.tensor.matmul(o, q[b % 2][rows, h // 4, t * P:(t + 1) * P], ks[b % 2][rows, h // 4, :],
                                      start=True, stop=not causal)
                if causal and t == 0:
                    mm = nc.tensor.matmul(o, c.mask400, c.future0, start=False, stop=True)
                elif causal:
                    mm = nc.tensor.matmul(o[:, P:N], c.mask400, c.future1, start=False, stop=True)
            scored[i] = pe.done(mm)
            dve.need(scored[i], exped.get(i - 4))
            maxed[i] = dve.done(nc.vector.tensor_reduce(nm[:, i % 4, :], bank.rearrange("p (t n) -> p t n", t=TB),
                                                        AX.X, ALU.max, negate=True))

        def exps(i):
            bank = S[i % 3]
            act.need(maxed[i], turned.get(i - 4), normed.get(i - 4))
            for t in range(TB):
                e = nc.scalar.activation(Pr[:, i % 4, t, :], bank[:, t * N:(t + 1) * N], ACT.Exp,
                                         bias=nm[:, i % 4, t:t + 1], accum_out=rsum[:, i % 4, t:t + 1])
            exped[i] = act.done(e)

        def norm(i):
            dve.need(exped[i], normed.get(i - 4))
            pool.need(dve.done(nc.vector.reciprocal(rinv[:, i % 4, :], rsum[:, i % 4, :])))
            normed[i] = pool.done(nc.gpsimd.tensor_tensor(Pr[:, i % 4, :, :], Pr[:, i % 4, :, :],
                                                          spread(rinv[:, i % 4, :], N), ALU.mult))

        def turn(i):
            pe.need(normed[i], moved.get(i - 2))
            for kt in range(TB):
                for t in range(TB):
                    mm = nc.tensor.transpose(PT[i % 2][:, kt * N + t * P:kt * N + (t + 1) * P],
                                             Pr[:, i % 4, t, kt * P:(kt + 1) * P], c.ident)
            turned[i] = pe.done(mm)

        def high_part(i):
            src = PT[i % 2].rearrange("p (k n) -> p k n", k=TB)
            act.need(turned[i], pv_done.get(i - 2))
            high[i] = act.done(nc.scalar.copy(PTh[i % 2][:, :, :], src))

        def low(i):
            src = PT[i % 2].rearrange("p (k n) -> p k n", k=TB)
            dve.need(high[i], pv_done.get(i - 2))
            moved[i] = dve.done(nc.vector.tensor_tensor(PTl[i % 2][:, :, :], src, PTh[i % 2][:, :, :].bitcast(F32), ALU.subtract))

        def weigh(i):
            b, h = divmod(i, H8)
            pe.need(moved[i], out_read.get(b - 1))
            g, hh = divmod(h, HG)
            for kt in range(TB):
                for n_, pr in enumerate((PTh, PTl)):
                    mm = nc.tensor.matmul(O[:, g * N:(g + 1) * N], vz[b % 2][:, kt, g, hh * D:(hh + 1) * D],
                                          pr[i % 2][:, kt, :], start=(hh == 0 and kt + n_ == 0),
                                          stop=(hh == HG - 1 and kt == TB - 1 and n_ == 1))
            pv_done[i] = pe.done(mm)

        def copy_out(b):
            act.need(pv_done[(b + 1) * H8 - 1], st.get("oT_read"))
            out_read[b] = act.done(nc.scalar.copy(oT[:, :, :], O.rearrange("p (g n) -> p g n", g=GV)))

        def through_wo(b):
            pe.need(out_read[b], mread[1])
            for t in range(TB):
                for g in range(GV):
                    mm = nc.tensor.matmul(M[1][:, t * P:(t + 1) * P], oT[:, g, t * P:(t + 1) * P], wo2[:, g, :],
                                          start=(g == 0), stop=(g == GV - 1))
            st["oT_read"] = pe.done(mm)

        def add(b):
            dve.need(st["oT_read"])
            xs = x[:, b * TB:(b + 1) * TB, :]
            mread[1] = dve.done(nc.vector.tensor_tensor(xs, xs, M[1][:, 0:N].rearrange("p (t d) -> p t d", d=D), ALU.add))

        todo = []
        for i in range(NH + 8):
            if i < NH and i % H8 == 0 and i // H8 + 1 < B:
                todo = pieces(i // H8 + 1)

            def background(place):
                while todo and todo[0][0:2] <= (i % H8, place):
                    todo.pop(0)[2]()

            if 5 <= i < NH + 5:
                turn(i - 5)
            if 3 <= i < NH + 3:
                norm(i - 3)
            if 2 <= i < NH + 2:
                exps(i - 2)
            background(0)
            if i >= H8 + 7 and (i - 7) % H8 == 0:
                add((i - 7) // H8 - 1)
            if 5 <= i < NH + 5:
                high_part(i - 5)
                low(i - 5)
            if i < NH:
                scores(i)
            if 6 <= i < NH + 6:
                weigh(i - 6)
            background(1)
            if i >= H8 + 5 and (i - 5) % H8 == 0:
                copy_out((i - 5) // H8 - 1)
            if i >= H8 + 6 and (i - 6) % H8 == 0:
                through_wo((i - 6) // H8 - 1)
            background(2)
        c.stage(f"{name}_end")


def ffn_int8(c, name, x, xn, wq8, wscale):
    nc, pe, act, dve, pool = c.nc, c.pe, c.act, c.dve, c.pool
    G = 4
    with ExitStack() as ctx:
        sb = lambda k, s, dt=F32: ctx.enter_context(nc.sbuf_tensor(f"{name}_{k}", s, dt))
        wf, wT = sb("wf", [P, D]), sb("wT", [P, D], BF16)
        amax, xs, xi = sb("amax", [P, NT]), sb("xscale", [P, NT]), sb("xinv", [P, NT])
        xq = [sb(f"xq{i}", [P, G, D]) for i in range(2)]
        xqT = [sb(f"xqT{i}", [P, G, P], BF16) for i in range(2)]
        ys = [sb(f"y{i}", [P, G, D]) for i in range(2)]
        s = dve.done(nc.vector.tensor_copy(wf[:, :], wq8))
        pe.need(s)
        s = pe.done(nc.tensor.transpose(c.banks[7][:, 0:P], wf[:, :], c.ident))
        dve.need(s)
        w_ready = dve.done(nc.vector.tensor_copy(wT[:, :], c.banks[7][:, 0:P]))
        dve.chain(nc.vector.tensor_reduce(amax[:, :], xn[:, :, :], AX.X, ALU.max, apply_absolute_value=True))
        dve.chain(nc.vector.tensor_scalar(xs[:, :], amax[:, :], 1e-6, float(np.float32(1.0) / np.float32(127.0)),
                                          ALU.max, ALU.mult))
        dve.chain(nc.vector.reciprocal(xi[:, :], xs[:, :]))
        q_done, turned, moved, made, read, added = {}, {}, {}, {}, {}, {}
        ROUND = 12582912.0
        for g in range(NT // G + 2):
            if g < NT // G:
                dve.need(turned.get(g - 2))
                for t in range(G):
                    k = g * G + t
                    s = dve.done(nc.vector.tensor_scalar(xq[g % 2][:, t, :], xn[:, k, :], xi[:, k:k + 1], ROUND,
                                                         ALU.mult, ALU.add))
                dve.need(s)
                dve.chain(nc.vector.tensor_scalar(xq[g % 2][:, :, :], xq[g % 2][:, :, :], ROUND, -128.0,
                                                  ALU.subtract, ALU.max))
                q_done[g] = dve.done(nc.vector.tensor_scalar(xq[g % 2][:, :, :], xq[g % 2][:, :, :], 127.0, None, ALU.min))
            if 1 <= g <= NT // G:
                j = g - 1
                pe.need(q_done[j], moved.get(j - 2))
                for t in range(G):
                    mm = nc.tensor.transpose(c.banks[j % 2][:, t * P:(t + 1) * P], xq[j % 2][:, t, :], c.ident)
                turned[j] = pe.done(mm)
                act.need(turned[j], made.get(j - 2))
                moved[j] = act.done(nc.scalar.copy(xqT[j % 2][:, :, :],
                                                   c.banks[j % 2][:, :].rearrange("p (t q) -> p t q", t=G)))
            if g >= 2:
                j = g - 2
                bank = c.banks[2 + j % 2]
                pe.need(moved[j], w_ready, read.get(j - 2))
                for t in range(G):
                    mm = nc.tensor.matmul(bank[:, t * P:(t + 1) * P], xqT[j % 2][:, t, :], wT[:, :], start=True, stop=True)
                made[j] = pe.done(mm)
                dve.need(made[j], added.get(j - 2))
                for t in range(G):
                    k = j * G + t
                    s = dve.done(nc.vector.scalar_tensor_tensor(out=ys[j % 2][:, t, :], in0=bank[:, t * P:(t + 1) * P],
                                                                scalar=xs[:, k:k + 1], in1=wscale,
                                                                op0=ALU.mult, op1=ALU.mult))
                read[j] = s
                pool.need(s)
                xk = x[:, j * G:(j + 1) * G, :]
                added[j] = pool.done(nc.gpsimd.tensor_tensor(xk, xk, ys[j % 2][:, :, :], ALU.add))
        c.stage(f"{name}_end")


def ffn_ternary(c, name, x, xnT, w1, b1, w2):
    nc, pe, act, dve, pool = c.nc, c.pe, c.act, c.dve, c.pool
    F = w2.shape[1]
    FT = F // P
    with ExitStack() as ctx:
        sb = lambda k, s, dt=F32: ctx.enter_context(nc.sbuf_tensor(f"{name}_{k}", s, dt))
        tern = sb("tern", [P, F])
        w1T, w2T = sb("w1T", [P, FT, P]), sb("w2T", [P, FT, P])
        part, tot, inv = sb("part", [P, 1]), sb("tot", [P, 1]), sb("inv", [P, 1])
        h = [sb(f"h{i}", [P, FT, CH]) for i in range(2)]
        ROUND = 12582912.0
        s = None
        for wsrc, wdst in ((w1.rearrange("p t d -> p (t d)"), w1T), (w2, w2T)):
            dve.chain(nc.vector.tensor_reduce(part[:, :], wsrc, AX.X, ALU.add, apply_absolute_value=True))
            pe.need((dve.sem, dve.count))
            s = pe.done(nc.tensor.matmul(c.banks[7][:, 0:1], c.ones, part[:, :], start=True, stop=True))
            dve.need(s)
            dve.chain(nc.vector.tensor_scalar(tot[:, :], c.banks[7][:, 0:1], 1.0 / (F * D), 1e-8, ALU.mult, ALU.max))
            dve.chain(nc.vector.reciprocal(inv[:, :], tot[:, :]))
            dve.chain(nc.vector.tensor_scalar(tern[:, :], wsrc, inv[:, 0:1], ROUND, ALU.mult, ALU.add))
            dve.chain(nc.vector.tensor_scalar(tern[:, :], tern[:, :], ROUND, -1.0, ALU.subtract, ALU.max))
            dve.chain(nc.vector.tensor_scalar(tern[:, :], tern[:, :], 1.0, None, ALU.min))
            dve.chain(nc.vector.tensor_tensor(tern[:, :], tern[:, :], wsrc, ALU.subtract))
            pe.need(dve.chain(nc.vector.tensor_tensor(tern[:, :], tern[:, :], wsrc, ALU.add)))
            for t in range(FT):
                mm = nc.tensor.transpose(c.banks[6][:, t * P:(t + 1) * P], tern[:, t * P:(t + 1) * P], c.ident)
            s = pe.done(mm)
            dve.need(s)
            s = dve.done(nc.vector.tensor_copy(wdst[:, :, :], c.banks[6][:, :].rearrange("p (t d) -> p t d", t=FT)))
        w_ready = s
        made, gelued, out, read = {}, {}, {}, {}
        NG = NCH * FT
        for i in range(NG + 2):
            if i < NG:
                ch, f = divmod(i, FT)
                pe.need(w_ready, gelued.get(i - 4))
                made[i] = pe.done(nc.tensor.matmul(c.banks[i % 4], w1T[:, f, :], xnT[:, ch * CH:(ch + 1) * CH],
                                                   start=True, stop=True))
                act.need(made[i], out.get(ch - 2))
                gelued[i] = act.done(nc.scalar.activation(h[ch % 2][:, f, :], c.banks[i % 4], ACT.Gelu,
                                                          bias=b1[:, f:f + 1]))
            if i >= FT + 1 and (i - 1) % FT == 0:
                ch = (i - 1) // FT - 1
                bank = c.banks[4 + ch % 2]
                pe.need(gelued[ch * FT + FT - 1], read.get(ch - 2))
                for t in range(CH // P):
                    for f in range(FT):
                        mm = nc.tensor.matmul(bank[:, t * P:(t + 1) * P], h[ch % 2][:, f, t * P:(t + 1) * P],
                                              w2T[:, f, :], start=(f == 0), stop=(f == FT - 1))
                out[ch] = pe.done(mm)
                dve.need(out[ch])
                xs = x[:, ch * 4:(ch + 1) * 4, :]
                read[ch] = dve.done(nc.vector.tensor_tensor(xs, xs, bank[:, :].rearrange("p (t d) -> p t d", d=D), ALU.add))
        assert len(out) == NCH
        c.stage(f"{name}_end")


def chunk_attention(c, name, x, xnT, w, bcol, bv, own1, block):
    nc, pe, act, dve, pool = c.nc, c.pe, c.act, c.dve, c.pool
    NK, CK = N // 32, 32
    NB = CH // N
    R = 4
    scale = float(np.float32(1.0) / np.sqrt(np.float32(D)))
    with ExitStack() as ctx:
        sb = lambda k, s, dt=F32: ctx.enter_context(nc.sbuf_tensor(f"{name}_{k}", s, dt))
        q, k = [sb(f"q{i}", [P, CH]) for i in range(2)], [sb(f"k{i}", [P, CH]) for i in range(2)]
        V = [sb(f"v{i}", [P, CH // P, D]) for i in range(4)]
        mx, z, zi = (sb(n, [P, R, TB * NK]) for n in ("mx", "z", "zi"))
        E = [sb(f"e{i}", [P, TB * NK, CK]) for i in range(R)]
        W = sb("w", [P, 2, TB, CK])
        Wb = [sb(f"wb{i}", [P, TB, 4, CK]) for i in range(2)]
        WT, cT = ([sb(f"{n}{i}", [P, TB, P]) for i in range(2)] for n in ("wt", "ct"))
        S, TR, X, Y, M = c.banks[0:2], c.banks[2], c.banks[3], c.banks[4], dict(zip("qkv", c.banks[5:8]))
        scored, centred, exped, zed, scaled_, summed, wide, turned, moved, mixed, comb, proj, added = ({} for _ in range(13))
        ready, read = {}, {}

        def project(ch):
            for kk in "qk":
                pe.need(read.get(kk))
                s = pe.done(nc.tensor.matmul(M[kk], w[kk], xnT[:, ch * CH:(ch + 1) * CH], start=True, stop=True))
                act.need(s, scored.get(NB * (ch - 1) - 1))
                read[kk] = act.done(nc.scalar.activation((q if kk == "q" else k)[ch % 2][:, :], M[kk], ACT.Identity, bias=bcol[kk]))
            pe.need(read.get("v"))
            for t in range(CH // P):
                mm = nc.tensor.matmul(M["v"][:, t * P:(t + 1) * P], xnT[:, ch * CH + t * P:ch * CH + (t + 1) * P],
                                      w["v"], start=True, stop=True)
            s = pe.done(mm)
            dve.need(s, mixed.get(NB * (ch - 3) - 1))
            read["v"] = dve.done(nc.vector.tensor_tensor(V[ch % 4][:, :, :], M["v"].rearrange("p (t d) -> p t d", d=D),
                                                         per_tile(bv, CH // P), ALU.add))
            ready[ch] = (read["q"], read["k"], read["v"])

        def scores(b):
            ch, off = b // NB, b % NB * N
            pe.need(*ready[ch], centred.get(b - 2))
            for t in range(TB):
                mm = nc.tensor.matmul(S[b % 2][:, t * N:(t + 1) * N], q[ch % 2][:, off + t * P:off + (t + 1) * P],
                                      k[ch % 2][:, off:off + N], start=True, stop=True)
            scored[b] = pe.done(mm)

        def maxima(b):
            sc = S[b % 2].rearrange("p (m k) -> p m k", k=CK)
            dve.need(scored[b], summed.get(b - R))
            dve.chain(nc.vector.tensor_reduce(mx[:, b % R, :], sc, AX.X, ALU.max))
            centred[b] = dve.done(nc.vector.tensor_tensor(E[b % R][:, :, :], sc, spread(mx[:, b % R, :], CK), ALU.subtract))

        def exps(b):
            act.need(centred[b])
            exped[b] = act.done(nc.scalar.activation(E[b % R][:, :, :], E[b % R][:, :, :], ACT.Exp, scale=scale))

        def norm(b):
            dve.need(exped[b])
            dve.chain(nc.vector.tensor_reduce(z[:, b % R, :], E[b % R][:, :, :], AX.X, ALU.add))
            dve.chain(nc.vector.reciprocal(zi[:, b % R, :], z[:, b % R, :]))
            zed[b] = dve.done(nc.vector.tensor_tensor(zi[:, b % R, :], zi[:, b % R, :], own1, ALU.mult))
            pool.need(zed[b])
            scaled_[b] = pool.done(nc.gpsimd.tensor_tensor(E[b % R][:, :, :], E[b % R][:, :, :],
                                                           spread(zi[:, b % R, :], CK), ALU.mult))

        def over_chunks(b):
            dve.need(scaled_[b], wide.get(b - 2))
            summed[b] = dve.done(nc.vector.tensor_reduce(W[:, b % 2, :, :], E[b % R].rearrange("p (t m) k -> p t k m", m=NK),
                                                         AX.X, ALU.add))
            pool.need(summed[b], turned.get(b - 2))
            wide[b] = pool.done(nc.gpsimd.tensor_tensor(
                Wb[b % 2][:, :, :, :], W[:, b % 2, :, :].unsqueeze(2).to_broadcast((P, TB, 4, CK)),
                spread(block, CK).unsqueeze(1).to_broadcast((P, TB, 4, CK)), ALU.mult))

        def turn(b):
            pe.need(wide[b], moved.get(b - 1))
            for t in range(TB):
                mm = nc.tensor.transpose(TR[:, t * P:(t + 1) * P], Wb[b % 2][:, t, :, :].rearrange("p m k -> p (m k)"), c.ident)
            turned[b] = pe.done(mm)
            act.need(turned[b], mixed.get(b - 2))
            moved[b] = act.done(nc.scalar.copy(WT[b % 2][:, :, :], TR[:, 0:N].rearrange("p (t n) -> p t n", t=TB)))

        def mix(b):
            pe.need(moved[b], comb.get(b - 1))
            for t in range(TB):
                mm = nc.tensor.matmul(X[:, t * P:(t + 1) * P], V[b // NB % 4][:, b % NB * TB + t, :], WT[b % 2][:, t, :],
                                      start=True, stop=True)
            mixed[b] = pe.done(mm)
            act.need(mixed[b], proj.get(b - 2))
            comb[b] = act.done(nc.scalar.copy(cT[b % 2][:, :, :], X[:, 0:N].rearrange("p (t n) -> p t n", t=TB)))

        def output(b):
            pe.need(comb[b], added.get(b - 1))
            for t in range(TB):
                mm = nc.tensor.matmul(Y[:, t * D:(t + 1) * D], cT[b % 2][:, t, :], w["o"], start=True, stop=True)
            proj[b] = pe.done(mm)
            dve.need(proj[b])
            xs = x[:, b * TB:(b + 1) * TB, :]
            added[b] = dve.done(nc.vector.tensor_tensor(xs, xs, Y[:, 0:N].rearrange("p (t d) -> p t d", d=D), ALU.add))

        project(0)
        for r in range(B + 6):
            for lag, step in ((0, scores), (4, turn), (5, mix), (6, output), (3, over_chunks), (2, norm), (0, maxima), (1, exps)):
                if lag <= r < B + lag:
                    step(r - lag)
            if r % NB == 0 and r // NB + 1 < B // NB:
                project(r // NB + 1)
        c.stage(f"{name}_end")


NE2, TOPK, HID = 32, 4, 64
CAP = 4 * (T * TOPK) // NE2


def route(c, name, xnT, wg, iota, before, weightT):
    nc, pe, act, dve, pool = c.nc, c.pe, c.act, c.dve, c.pool
    with ExitStack() as ctx:
        sb = lambda k, s, dt=F32: ctx.enter_context(nc.sbuf_tensor(f"{name}_{k}", s, dt))
        sc, wt, chosen, hit, rank = (sb(k, [P, NT, NE2]) for k in ("scores", "wt", "chosen", "hit", "rank"))
        m, z = sb("m", [P, NT]), sb("z", [P, NT])
        top, idx, idf = sb("top", [P, NT, 8]), sb("idx", [P, NT, 8], U32), sb("idf", [P, NT, TOPK])
        tot, run = sb("tot", [P, NT, NE2]), sb("run", [P, NT, NE2])
        half = NT // 2
        for t in range(NT):
            mm = nc.tensor.matmul(c.banks[t // half][:, (t % half) * NE2:(t % half + 1) * NE2],
                                  xnT[:, t * P:(t + 1) * P], wg, start=True, stop=True)
        dve.need(pe.done(mm))
        for b in range(2):
            s = dve.done(nc.vector.tensor_copy(sc[:, b * half:(b + 1) * half, :],
                                               c.banks[b][:, :].rearrange("p (t e) -> p t e", e=NE2)))
        dve.need(s)
        dve.chain(nc.vector.tensor_reduce(m[:, :], sc[:, :, :], AX.X, ALU.max))
        act.need(dve.done(nc.vector.tensor_tensor(sc[:, :, :], sc[:, :, :], spread(m[:, :], NE2), ALU.subtract)))
        dve.need(act.done(nc.scalar.activation(sc[:, :, :], sc[:, :, :], ACT.Exp)))
        dve.chain(nc.vector.tensor_reduce(z[:, :], sc[:, :, :], AX.X, ALU.add))
        dve.chain(nc.vector.reciprocal(z[:, :], z[:, :]))
        dve.chain(nc.vector.tensor_tensor(sc[:, :, :], sc[:, :, :], spread(z[:, :], NE2), ALU.mult))
        for t in range(NT):
            s = dve.done(nc.vector.max(top[:, t, :], sc[:, t, :]))
        dve.need(s)
        for t in range(NT):
            s = dve.done(nc.vector.max_index(idx[:, t, :], top[:, t, :], sc[:, t, :]))
        dve.need(s)
        dve.chain(nc.vector.tensor_copy(idf[:, :, :], idx[:, :, 0:TOPK]))
        for k in range(TOPK):
            s = dve.chain(nc.vector.tensor_tensor(hit[:, :, :], per_tile(iota, NT), spread(idf[:, :, k], NE2), ALU.is_equal))
            if k == 0:
                dve.chain(nc.vector.tensor_copy(chosen[:, :, :], hit[:, :, :]))
                dve.chain(nc.vector.tensor_tensor(wt[:, :, :], hit[:, :, :], spread(top[:, :, k], NE2), ALU.mult))
            else:
                dve.chain(nc.vector.tensor_tensor(chosen[:, :, :], chosen[:, :, :], hit[:, :, :], ALU.add))
                dve.chain(nc.vector.tensor_tensor(hit[:, :, :], hit[:, :, :], spread(top[:, :, k], NE2), ALU.mult))
                dve.chain(nc.vector.tensor_tensor(wt[:, :, :], wt[:, :, :], hit[:, :, :], ALU.add))
        pe.need((dve.sem, dve.count))
        for b in range(2):
            src = chosen[:, b * half:(b + 1) * half, :].rearrange("p t e -> p (t e)")
            nc.tensor.matmul(c.banks[2 + b][:, :], before, src, start=True, stop=True)
            s = pe.done(nc.tensor.matmul(c.banks[4 + b][:, :], c.ones, src, start=True, stop=True))
        dve.need(s)
        for b in range(2):
            w = slice(b * half, (b + 1) * half)
            nc.vector.tensor_copy(rank[:, w, :], c.banks[2 + b][:, :].rearrange("p (t e) -> p t e", e=NE2))
            dve.chain(nc.vector.tensor_copy(tot[:, w, :], c.banks[4 + b][:, :].rearrange("p (t e) -> p t e", e=NE2)))
        dve.chain(nc.vector.memset(run[:, 0, :], 0.0))
        for t in range(1, NT):
            dve.chain(nc.vector.tensor_tensor(run[:, t, :], run[:, t - 1, :], tot[:, t - 1, :], ALU.add))
        dve.chain(nc.vector.tensor_tensor(rank[:, :, :], rank[:, :, :], run[:, :, :], ALU.add))
        dve.chain(nc.vector.tensor_scalar(rank[:, :, :], rank[:, :, :], float(CAP), None, ALU.is_lt))
        pe.need(dve.chain(nc.vector.tensor_tensor(wt[:, :, :], wt[:, :, :], rank[:, :, :], ALU.mult)))
        read = {}
        for q in range(NT // 4):
            pe.need(read.get(q - 2))
            for k in range(4):
                mm = nc.tensor.transpose(c.banks[6 + q % 2][0:NE2, k * P:(k + 1) * P], wt[:, q * 4 + k, :], c.ident)
            act.need(pe.done(mm))
            read[q] = act.done(nc.scalar.copy(weightT[:, q * CH:(q + 1) * CH], c.banks[6 + q % 2][0:NE2, :]))
        c.stage(f"{name}_end")


def experts(c, name, x, xnT, weightT, w1, w3, w2, ws, sel):
    nc, pe, act, dve, pool = c.nc, c.pe, c.act, c.dve, c.pool
    NP2 = NE2 // 2
    R = NP2 + 1
    with ExitStack() as ctx:
        sb = lambda k, s, dt=F32: ctx.enter_context(nc.sbuf_tensor(f"{name}_{k}", s, dt))
        sg = [sb(f"sg{i}", [P, CH]) for i in range(2)]
        hh = [sb(f"h{i}", [P, CH]) for i in range(3)]
        high = [sb(f"w{m}_high", [P, R, P], F32R) for m in range(2)]
        low_ = [sb(f"w{m}_low", [P, R, P], F32R) for m in range(2)]
        xh, xlo, wp = ([sb(f"{k}{i}", [P, CH], F32R) for i in range(2)] for k in ("xh", "xlo", "wp"))
        picks = sb("sel", [P, NP2 * P], F32R)
        G, U, Wb, Y = c.banks[0:2], c.banks[2:4], c.banks[4:6], c.banks[6:8]
        made, silu, half, hid, down, added, split = {}, {}, {}, {}, {}, {}, {}

        for v in wp:
            zeroed = pool.done(nc.gpsimd.memset(v[:, :].bitcast(F32), 0.0))

        def chunk_parts(ch):
            xs, wt = xnT[:, ch * CH:(ch + 1) * CH], weightT[:, ch * CH:(ch + 1) * CH]
            h, l, w_ = xh[ch % 2], xlo[ch % 2], wp[ch % 2]
            dve.need(made.get((ch - 1) * R - 1), zeroed)
            dve.done(nc.vector.tensor_copy(h[:, :], xs))
            dve.chain(nc.vector.tensor_copy(w_[0:NE2, :], wt))
            dve.done(nc.vector.tensor_tensor(l[:, :], xs, h[:, :].bitcast(F32), ALU.subtract))
            split[ch] = dve.done(nc.vector.tensor_tensor(w_[NE2:2 * NE2, :], wt, w_[0:NE2, :].bitcast(F32), ALU.subtract))

        chunk_parts(0)
        pairs = lambda w, p0, n: w[:, 2 * p0:2 * (p0 + n), :].rearrange("d (p e) h -> d p (e h)", e=2)
        weights = {}
        n = NP2 // 4
        picked = dve.done(nc.vector.tensor_copy(picks[:, :], sel))
        for p0 in range(0, NP2 + 1, n):
            for m, w in enumerate((w1, w3)):
                ps_, src = (slice(p0, p0 + n), pairs(w, p0, n)) if p0 < NP2 else (slice(p0, p0 + 1), ws[m].unsqueeze(1))
                act_part = act.done(nc.scalar.copy(high[m][:, ps_, :], src))
                dve.need(act_part)
                s = dve.done(nc.vector.tensor_tensor(low_[m][:, ps_, :], src, high[m][:, ps_, :].bitcast(F32), ALU.subtract))
            for p in range(p0, min(p0 + n, R)):
                weights[p] = s

        def up(i):
            ch, p = divmod(i, R)
            b = ch % 2
            pe.need(weights[p], picked, split[ch])
            pe.need(hid.get(i - 2))
            for m, bank in enumerate((G, U)):
                for n_, (l_, r_) in enumerate(((high, xh), (high, xlo), (low_, xh))):
                    mm = nc.tensor.matmul(bank[i % 2][:, :], l_[m][:, p, :], r_[b][:, :], start=(n_ == 0), stop=(n_ == 2))
            if p < NP2:
                mm = nc.tensor.matmul(Wb[i % 2][:, :], picks[:, p * P:(p + 1) * P], wp[b][:, :], start=True, stop=True)
            made[i] = pe.done(mm)
            act.need(made[i], half.get(i - 2))
            silu[i] = act.done(nc.scalar.activation(sg[i % 2][:, :], G[i % 2][:, :], ACT.Silu))
            dve.need(silu[i], down.get(i - 3))
            half[i] = dve.chain(nc.vector.tensor_tensor(hh[i % 3][:, :], sg[i % 2][:, :], U[i % 2][:, :], ALU.mult))
            hid[i] = half[i]
            if p < NP2:
                hid[i] = dve.done(nc.vector.tensor_tensor(hh[i % 3][:, :], hh[i % 3][:, :], Wb[i % 2][:, :], ALU.mult))
            if p == R // 2 and ch + 1 < NCH:
                chunk_parts(ch + 1)

        def low(i):
            ch, p = divmod(i, R)
            l2 = w2[:, p, :] if p < NP2 else ws[2]
            bank = Y[ch % 2]
            pe.need(hid[i], added.get(ch - 2))
            for t in range(CH // P):
                mm = nc.tensor.matmul(bank[:, t * P:(t + 1) * P], hh[i % 3][:, t * P:(t + 1) * P], l2,
                                      start=(p == 0 and t == 0), stop=(p == R - 1), skip_group_check=True)
            down[i] = pe.done(mm)
            if p == R - 1:
                dve.need(down[i])
                xs = x[:, ch * 4:(ch + 1) * 4, :]
                added[ch] = dve.done(nc.vector.tensor_tensor(xs, xs, bank[:, :].rearrange("p (t d) -> p t d", d=D), ALU.add))

        for i in range(NCH * R + 2):
            if i < NCH * R:
                up(i)
            if i >= 2:
                low(i - 2)
        c.stage(f"{name}_end")


E3, SL, F3 = 16, 64, 256
ES = E3 * SL
FK = F3 // P
HB = B // 2


def slot_experts(c, name, x, xl, xlT, seT, wg, wu, wd, bgT, buT, bd):
    nc, pe, act, dve, pool = c.nc, c.pe, c.act, c.dve, c.pool
    UT = ES // N
    with ExitStack() as ctx:
        sb = lambda k, s, dt=F32: ctx.enter_context(nc.sbuf_tensor(f"{name}_{k}", s, dt))
        slots = sb("slots", [P, E3, HB * SL])
        eout = lambda ep: slots[:, 2 * ep:2 * ep + 2, :].rearrange("p e r -> p (e r)").rearrange("p (b o) -> p b o", o=D)
        nm, z, zi = sb("nm", [P, 4, 2]), sb("z", [P, 4, 2]), sb("zi", [P, 4, 2])
        scratch = sb("scratch", [P, 4 * ES])
        cut = lambda at, n: scratch[:, at:at + n]
        Ex = [cut(i * 2 * N, 2 * N).rearrange("p (s n) -> p s n", s=2) for i in range(3)]
        Dn = [cut((3 + i) * 2 * N, 2 * N).rearrange("p (t n) -> p t n", t=TB) for i in range(2)]
        g = [cut(i * CH, CH) for i in range(2)]
        h = [cut((2 + i * FK) * CH, FK * CH).rearrange("p (f n) -> p f n", f=FK) for i in range(2)]
        Cx = [cut(i * ES, ES) for i in range(2)]
        CT = [cut((2 + i) * ES, ES).rearrange("p (s n) -> p s n", n=P) for i in range(2)]
        for half in range(2):
            n = HB * UT
            lg, ex, nd, tr, mv, sl, ev = {}, {}, {}, {}, {}, {}, {}
            L, TR, X = c.banks[0:3], c.banks[3:5], c.banks[5:7]

            def logits(i):
                b, u = half * HB + i // UT, i % UT
                pe.need(ex.get(i - 3))
                for s in range(2):
                    mm = nc.tensor.matmul(L[i % 3][:, s * N:(s + 1) * N], seT[:, (2 * u + s) * P:(2 * u + s + 1) * P],
                                          xlT[:, b * N:(b + 1) * N], start=True, stop=True)
                lg[i] = pe.done(mm)
                dve.need(lg[i], ex.get(i - 4))
                s_ = dve.done(nc.vector.tensor_reduce(nm[:, i % 4, :], L[i % 3].rearrange("p (s n) -> p s n", s=2),
                                                      AX.X, ALU.max, negate=True))
                act.need(s_, tr.get(i - 3), nd.get(i - 4))
                for s in range(2):
                    e = nc.scalar.activation(Ex[i % 3][:, s, :], L[i % 3][:, s * N:(s + 1) * N], ACT.Exp,
                                             bias=nm[:, i % 4, s:s + 1], accum_out=z[:, i % 4, s:s + 1])
                ex[i] = act.done(e)
                dve.need(ex[i], nd.get(i - 4))
                pool.need(dve.done(nc.vector.reciprocal(zi[:, i % 4, :], z[:, i % 4, :])))
                nd[i] = pool.done(nc.gpsimd.tensor_tensor(Ex[i % 3][:, :, :], Ex[i % 3][:, :, :],
                                                          spread(zi[:, i % 4, :], N), ALU.mult))

            def turn(i):
                pe.need(nd[i], mv.get(i - 2))
                for s in range(2):
                    for t in range(TB):
                        mm = nc.tensor.transpose(TR[i % 2][:, t * N + s * P:t * N + (s + 1) * P],
                                                 Ex[i % 3][:, s, t * P:(t + 1) * P], c.ident)
                tr[i] = pe.done(mm)
                e = act if i % 2 else dve
                e.need(tr[i], sl.get(i - 2))
                src = TR[i % 2].rearrange("p (t n) -> p t n", t=TB)
                mv[i] = e.done(nc.scalar.copy(Dn[i % 2][:, :, :], src) if i % 2 else
                               nc.vector.tensor_copy(Dn[i % 2][:, :, :], src))

            def gather(i):
                b, u = i // UT, i % UT
                pe.need(mv[i], ev.get(i - 2))
                for t in range(TB):
                    mm = nc.tensor.matmul(X[i % 2][:, 0:N], xl[:, (half * HB + b) * TB + t, :], Dn[i % 2][:, t, :],
                                          start=(t == 0), stop=(t == TB - 1))
                sl[i] = pe.done(mm)
                act.need(sl[i])
                ev[i] = act.done(nc.scalar.copy(slots[:, 4 * u:4 * u + 4, b * SL:(b + 1) * SL],
                                                X[i % 2][:, 0:N].rearrange("p (e s) -> p e s", s=SL)))

            for i in range(n + 3):
                if i < n:
                    logits(i)
                if 2 <= i < n + 2:
                    turn(i - 2)
                if i >= 3:
                    gather(i - 3)
            c.stage(f"{name}_experts{half}")

            made, gel, hid, down, wr = {}, {}, {}, {}, {}

            def up(j):
                e, f = divmod(j, FK)
                pe.need(hid.get(j - 2))
                for m, w in ((0, wg), (2, wu)):
                    mm = nc.tensor.matmul(c.banks[m + j % 2], w[:, e, f * P:(f + 1) * P], slots[:, e, :], start=True, stop=True)
                made[j] = pe.done(mm)
                act.need(made[j], hid.get(j - 2))
                gel[j] = act.done(nc.scalar.activation(g[j % 2], c.banks[j % 2], ACT.Gelu,
                                                       bias=bgT[:, j:j + 1]))
                dve.need(gel[j], down.get(e - 2))
                hid[j] = dve.done(nc.vector.scalar_tensor_tensor(out=h[e % 2][:, f, :], in0=c.banks[2 + j % 2],
                                                                 scalar=buT[:, j:j + 1], in1=g[j % 2],
                                                                 op0=ALU.add, op1=ALU.mult))

            def low(e):
                ep, rows = e // 2, slice((e % 2) * SL, (e % 2) * SL + SL)
                pe.need(hid[e * FK + FK - 1], wr.get(ep - 2))
                for b in range(HB):
                    bank = c.banks[4 + 2 * (ep % 2) + b // 4]
                    for f in range(FK):
                        mm = nc.tensor.matmul(bank[rows, (b % 4) * D:(b % 4 + 1) * D], h[e % 2][:, f, b * SL:(b + 1) * SL],
                                              wd[:, e, f, :], start=(f == 0), stop=(f == FK - 1))
                down[e] = pe.done(mm)
                if e % 2:
                    dve.need(down[e])
                    for q in range(2):
                        s = dve.done(nc.vector.tensor_tensor(
                            eout(ep)[:, 4 * q:4 * q + 4, :], c.banks[4 + 2 * (ep % 2) + q].rearrange("p (b o) -> p b o", o=D),
                            per_tile(bd[:, ep, :], 4), ALU.add))
                    wr[ep] = s

            for e in range(E3 + 1):
                if e < E3:
                    up(e * FK)
                    up(e * FK + 1)
                if e >= 1:
                    low(e - 1)
            c.stage(f"{name}_combine{half}")

            n = HB * TB
            lg, ex, tr, mv, mx, ad = {}, {}, {}, {}, {}, {}

            def logits2(i):
                t = half * n + i
                two = c.ps[:, 2 * (i % 2):2 * (i % 2) + 2, :]
                pe.need(ex.get(i - 2))
                for q in range(2):
                    mm = nc.tensor.matmul(two[:, q, :], xlT[:, t * P:(t + 1) * P], seT[:, q * BANK:(q + 1) * BANK],
                                          start=True, stop=True)
                lg[i] = pe.done(mm)
                dve.need(lg[i], ex.get(i - 4))
                s = dve.done(nc.vector.tensor_reduce(nm[:, i % 4, 0:1], two, AX.XY, ALU.max, negate=True))
                act.need(s, tr.get(i - 2), ad.get(i - 4))
                ex[i] = act.done(nc.scalar.activation(Cx[i % 2].rearrange("p (q n) -> p q n", q=2), two, ACT.Exp,
                                                      bias=nm[:, i % 4, 0:1], accum_out=z[:, i % 4, 0:1]))

            def turn2(i):
                pe.need(ex[i], mv.get(i - 1), mv.get(("a", i - 1)))
                for s in range(ES // P):
                    mm = nc.tensor.transpose(c.banks[4 + s // 4][:, (s % 4) * P:(s % 4 + 1) * P],
                                             Cx[i % 2][:, s * P:(s + 1) * P], c.ident)
                tr[i] = pe.done(mm)
                dve.need(tr[i], mx.get(i - 2))
                act.need(tr[i], mx.get(i - 2))
                mv[i] = dve.done(nc.vector.tensor_copy(CT[i % 2][:, 0:4, :], c.banks[4].rearrange("p (s n) -> p s n", n=P)))
                mv["a", i] = act.done(nc.scalar.copy(CT[i % 2][:, 4:8, :], c.banks[5].rearrange("p (s n) -> p s n", n=P)))

            def mix(i):
                t = half * n + i
                b = i // TB
                pe.need(mv[i], mv["a", i], ad.get(i - 2))
                for s in range(ES // P):
                    mm = nc.tensor.matmul(c.banks[6 + i % 2][:, 0:D], CT[i % 2][:, s, :], eout(s)[:, b, :],
                                          start=(s == 0), stop=(s == ES // P - 1))
                mx[i] = pe.done(mm)
                dve.need(mx[i], ex[i])
                dve.chain(nc.vector.reciprocal(zi[:, i % 4, 0:1], z[:, i % 4, 0:1]))
                ad[i] = dve.done(nc.vector.scalar_tensor_tensor(out=x[:, t, :], in0=c.banks[6 + i % 2][:, 0:D],
                                                                scalar=zi[:, i % 4, 0:1], in1=x[:, t, :],
                                                                op0=ALU.mult, op1=ALU.add))

            for i in range(n + 2):
                if i < n:
                    logits2(i)
                if 1 <= i <= n:
                    turn2(i - 1)
                if i >= 2:
                    mix(i - 2)
            c.stage(f"{name}_end{half}")


H3, HD3 = 16, 64
INNER = H3 * HD3
STEPS = 3
HP = H3 // 2
GH = 8
GP, GW = GH // 2, GH * HD3
NU = B * H3 // GH


def iterated_attention(c, name, x, xnT, w, wo_dram, brow, gamma, beta, store):
    nc, pe, act, dve, pool = c.nc, c.pe, c.act, c.dve, c.pool
    S, PT, O, M = c.banks[0:3], c.banks[3:5], c.banks[5:7], c.banks[7]
    qslot, fslot = (lambda u, s: (4 * u + s) % 3), (lambda u, s: (3 * u + s) % 3)
    with ExitStack() as ctx:
        sb = lambda k, s, dt=F32: ctx.enter_context(nc.sbuf_tensor(f"{name}_{k}", s, dt))
        qh = [sb(f"qh{i}", [P, GP, N], F32R) for i in range(3)]
        ql = [sb(f"ql{i}", [P, GP, N], F32R) for i in range(3)]
        qf = [sb(f"qf{i}", [P, GP, N]) for i in range(3)]
        kh = [sb(f"kh{i}", [P, GH, N], F32R) for i in range(2)]
        kl = [sb(f"kl{i}", [P, GH, N], F32R) for i in range(2)]
        V = [sb(f"v{i}", [P, TB, GW]) for i in range(2)]
        wo = sb("wo", [P, HP, 2, D], F32R)
        wks = {kk: sb(f"w{kk}", [P, TB, GW]) for kk in ("q", "k")}
        sq = sb("sq", [P, TB, GW])
        kt_ = [sb(f"kt{i}", [P, GP, P]) for i in range(TB)]
        move = [sb(f"move{i}", [P, N]) for i in range(2)]
        ss, rs, v_, t_ = (sb(n_, [P, TB, GH]) for n_ in ("ss", "rs", "var", "newton"))
        mean = sb("mean", [P, H3])
        Pr = [sb(f"p{i}", [P, TB, N]) for i in range(4)]
        PTs = [sb(f"pt{i}", [P, TB, N]) for i in range(2)]
        nm, rsum, rinv = (sb(k, [P, 4, TB]) for k in ("nm", "rsum", "rinv"))
        g8, b8 = sb("gamma8", [P, 1]), sb("beta8", [P, 1])
        y = [sb(f"y{i}", [P, NT, D]) for i in range(STEPS - 1)]
        moved2 = sb("moved2", [P, STEPS - 1, NU * GP])
        tot, flag = sb("tot", [P, STEPS - 1]), sb("flag", [P, STEPS - 1], U32)

        wo_raw = sq[:, :, :].rearrange("p t n -> p (t n)").rearrange("p (q o) -> p q o", o=D)
        wo_in = c.load(f"{name}_wo", (wo_raw, wo_dram.rearrange("(q p) o -> p q o", p=P)))

        for kk in ("q", "k"):
            for m in (w[kk], brow[kk]):
                m3 = m.rearrange("p (h d) -> p h d", d=HD3)
                dve.chain(nc.vector.tensor_reduce(mean[:, :], m3, AX.X, ALU.add))
                dve.chain(nc.vector.tensor_scalar(mean[:, :], mean[:, :], 1.0 / HD3, None, ALU.mult))
                dve.chain(nc.vector.tensor_tensor(m3, m3, spread(mean[:, :], HD3), ALU.subtract))
        nc.vector.tensor_scalar(g8[:, :], gamma, 1.0 / 8.0, None, ALU.mult)
        nc.vector.tensor_scalar(b8[:, :], beta, 1.0 / 8.0, None, ALU.mult)
        dve.need(wo_in)
        dve.chain(nc.vector.tensor_copy(wo[:, :, 0, :], wo_raw))
        centred = dve.done(nc.vector.tensor_tensor(wo[:, :, 1, :], wo_raw, wo[:, :, 0, :].bitcast(F32), ALU.subtract))
        for b_ in kh + kl:
            zeroed = pool.done(nc.gpsimd.memset(b_[:, :, :].bitcast(F32), 0.0))

        index = lambda u, s, h: (u * STEPS + s) * GH + h
        NI = NU * STEPS * GH
        scored, maxed, exped, normed, turned, moved, pv = {}, {}, {}, {}, {}, {}, {}
        newq, pair_read, ydone, yread, moved_by, squared, ready = {}, {}, {}, {}, {}, {}, {}
        turned_k = {}
        st = {"m": centred}

        def projections(u):
            b, g = divmod(u, 2)
            cols = slice(g * GW, (g + 1) * GW)
            last = lambda v, s: scored.get(index(v, s, GH - 1))
            out = []
            at = lambda r, place, f, *a: out.append((r, place, lambda: f(*a)))

            def product(kk, t):
                pe.need(centred, st["m"])
                st["mm"] = pe.done(nc.tensor.matmul(M, xnT[:, b * N + t * P:b * N + (t + 1) * P], w[kk][:, cols],
                                                    start=True, stop=True))

            def biased(kk, t):
                dve.need(st["mm"], pv.get(index(u - 2, STEPS - 1, GH - 1)) if kk == "v" else turned_k.get((kk, t)))
                dst = V[u % 2][:, t, :] if kk == "v" else wks[kk][:, t, :]
                st["m"] = st["biased", kk, t] = dve.done(nc.vector.tensor_tensor(dst, M, brow[kk][:, cols], ALU.add))

            def square(kk, t):
                act.need(st["biased", kk, t], st.get(("summed", t)))
                st["sq", t] = act.done(nc.scalar.activation(sq[:, t, :], wks[kk][:, t, :], ACT.Square))

            def summed(t):
                dve.need(st["sq", t], st.get("scaled"))
                st["summed"] = st["summed", t] = dve.done(nc.vector.tensor_reduce(
                    ss[:, t, :], sq[:, t, :].rearrange("p (h d) -> p h d", d=HD3), AX.X, ALU.add))

            def root():
                dve.need(st["summed"])
                s = dve.done(nc.vector.tensor_scalar(v_[:, :, :], ss[:, :, :], 1.0 / HD3, 1e-5, ALU.mult, ALU.add))
                act.need(s, st.get("scaled"))
                act.chain(nc.scalar.activation(rs[:, :, :], v_[:, :, :], ACT.Ln))
                st["root"] = act.done(nc.scalar.activation(rs[:, :, :], rs[:, :, :], ACT.Exp, scale=-0.5))

            def newton():
                dve.need(st["root"])
                dve.chain(nc.vector.tensor_tensor(t_[:, :, :], rs[:, :, :], rs[:, :, :], ALU.mult))
                dve.chain(nc.vector.tensor_tensor(t_[:, :, :], t_[:, :, :], v_[:, :, :], ALU.mult))
                dve.chain(nc.vector.tensor_scalar(t_[:, :, :], t_[:, :, :], -0.5, 1.5, ALU.mult, ALU.add))
                st["rs"] = dve.done(nc.vector.tensor_tensor(rs[:, :, :], rs[:, :, :], t_[:, :, :], ALU.mult))

            def scaled(kk, t):
                pool.need(st["rs"])
                w3 = wks[kk][:, t, :].rearrange("p (h d) -> p h d", d=HD3)
                st["scaled"] = st["scaled", kk, t] = pool.done(nc.gpsimd.tensor_tensor(w3, w3, spread(rs[:, t, :], HD3), ALU.mult))

            def turn_(kk, t):
                pe.need(st["scaled", kk, t], st["m"])
                for j in range(GP):
                    mm = nc.tensor.transpose(M[:, j * P:(j + 1) * P], wks[kk][:, t, j * P:(j + 1) * P], c.ident)
                st["turned", t] = turned_k[kk, t] = pe.done(mm)

            def affine(kk, t):
                act.need(st["turned", t], *([moved_by.get((u - 1, 0, GP - 1))] if kk == "q" else [st.get(("split", t))]))
                dst = qf[fslot(u, 0)][:, :, t * P:(t + 1) * P] if kk == "q" else kt_[t][:, :, :]
                gb = (gamma, beta) if kk == "q" else (g8[:, 0:1], b8[:, 0:1])
                st["m"] = st["affine", t] = act.done(nc.scalar.activation(dst, M.rearrange("p (j n) -> p j n", n=P),
                                                                          ACT.Identity, bias=gb[1], scale=gb[0]))

            def q_parts(t):
                dve.need(st["affine", t], last(u - 1, 1), ydone.get((u - 1, 0)))
                n_ = slice(t * P, (t + 1) * P)
                hi, lo, f = qh[qslot(u, 0)][:, :, n_], ql[qslot(u, 0)][:, :, n_], qf[fslot(u, 0)][:, :, n_]
                dve.chain(nc.vector.tensor_copy(hi, f))
                st["q"] = dve.done(nc.vector.tensor_tensor(lo, f, hi.bitcast(F32), ALU.subtract))

            def k_part(t, e, low):
                rows = slice(e * HD3, (e + 1) * HD3)
                hi, lo = (m[u % 2][rows, e::2, t * P:(t + 1) * P] for m in (kh, kl))
                if low:
                    dve.need(st["high", t, e], last(u - 2, STEPS - 1), zeroed)
                    st["split", t] = dve.done(nc.vector.tensor_tensor(lo, kt_[t][rows, :, :], hi.bitcast(F32), ALU.subtract))
                else:
                    act.need(last(u - 2, STEPS - 1), zeroed, st.get(("split", t)))
                    st["high", t, e] = act.done(nc.scalar.copy(hi, kt_[t][rows, :, :]))

            def end():
                ready[u] = (st["q"], st["split", 0], st["split", 1])

            for kk, r, scale_at, turn_at in (("k", 0, 7, 9), ("q", 7, 14, 18)):
                at(r + 5, 1, root)
                at(r + 6, 1, newton)
                for t in range(TB):
                    at(r + t, 2, product, kk, t)
                    at(r + 1 + t, 0, biased, kk, t)
                    at(r + 2 + t, 1, square, kk, t)
                    at(r + 3 + t, 1, summed, t)
                    at(scale_at + t, 1, scaled, kk, t)
                    at(turn_at + t, 2, turn_, kk, t)
                    at(turn_at + 1 + t, 0, affine, kk, t)
            for t, highs, lows in ((0, 11, (12, 13)), (1, 14, (16, 21))):
                at(15 + t, 2, product, "v", t)
                at(16 + t, 0, biased, "v", t)
                for e in range(2):
                    at(highs, 1, k_part, t, e, False)
                    at(lows[e], 1, k_part, t, e, True)
                at(20 + t, 1, q_parts, t)
            at(22, 2, end)
            out.sort(key=lambda o: o[0:2])
            return out

        def scores(i, u, s, h):
            hp = h // 2
            n = qslot(u, s)
            pe.need(*(ready[u] if s == 0 else newq[u, s, hp]), exped.get(i - 3))
            for t in range(TB):
                for n_, (a_, b_) in enumerate(((qh, kh), (qh, kl), (ql, kh))):
                    mm = nc.tensor.matmul(S[i % 3][:, t * N:(t + 1) * N], a_[n][:, hp, t * P:(t + 1) * P],
                                          b_[u % 2][:, h, :], start=(n_ == 0), stop=(n_ == 2))
            scored[i] = pe.done(mm)
            dve.need(scored[i], exped.get(i - 4))
            maxed[i] = dve.done(nc.vector.tensor_reduce(nm[:, i % 4, :], S[i % 3].rearrange("p (t n) -> p t n", t=TB),
                                                        AX.X, ALU.max, negate=True))

        def exps(i):
            act.need(maxed[i], turned.get(i - 4), normed.get(i - 4))
            for t in range(TB):
                e = nc.scalar.activation(Pr[i % 4][:, t, :], S[i % 3][:, t * N:(t + 1) * N], ACT.Exp,
                                         bias=nm[:, i % 4, t:t + 1], accum_out=rsum[:, i % 4, t:t + 1])
            exped[i] = act.done(e)

        def norm(i):
            dve.need(exped[i], normed.get(i - 4))
            pool.need(dve.done(nc.vector.reciprocal(rinv[:, i % 4, :], rsum[:, i % 4, :])))
            normed[i] = pool.done(nc.gpsimd.tensor_tensor(Pr[i % 4][:, :, :], Pr[i % 4][:, :, :],
                                                          spread(rinv[:, i % 4, :], N), ALU.mult))

        def turn(i):
            pe.need(normed[i], moved.get(i - 2))
            for kt in range(TB):
                for t in range(TB):
                    mm = nc.tensor.transpose(PT[i % 2][:, kt * N + t * P:kt * N + (t + 1) * P],
                                             Pr[i % 4][:, t, kt * P:(kt + 1) * P], c.ident)
            turned[i] = pe.done(mm)

        def move_out(i):
            dst, src = PTs[i % 2][:, :, :], PT[i % 2].rearrange("p (k n) -> p k n", k=TB)
            e = act if i % 2 == 0 else dve
            e.need(turned[i], pv.get(i - 2))
            moved[i] = e.done(nc.vector.tensor_copy(dst, src) if e is dve else nc.scalar.copy(dst, src))

        def weigh(i, u, s, h):
            pe.need(moved[i], pair_read.get(i // 2 - 2))
            rows = slice((h % 2) * HD3, (h % 2 + 1) * HD3)
            for kt in range(TB):
                mm = nc.tensor.matmul(O[i // 2 % 2][rows, 0:N], V[u % 2][:, kt, h * HD3:(h + 1) * HD3],
                                      PTs[i % 2][:, kt, :], start=(kt == 0), stop=(kt == TB - 1))
            pv[i] = pe.done(mm)

        def pair_end(i, u, s, h):
            pr, hp = i // 2, h // 2
            out = O[pr % 2][:, 0:N]
            hi, lo = (m[qslot(u, s + 1)][:, hp, :] for m in (qh, ql))
            before = {0: (scored.get(index(u - 1, 2, GH - 1)), ydone.get((u - 1, 1))), 1: (ydone.get((u - 1, 2)),),
                      2: (scored.get(index(u, 0, GH - 1)),)}[s]
            act.need(pv[i], *before)
            r = act.done(nc.scalar.copy(hi, out))
            if s < STEPS - 1:
                act.need(moved_by.get((u - 1, 1, hp)))
                r = act.done(nc.scalar.copy(qf[fslot(u, s + 1)][:, hp, :], out))
            dve.need(r, *before)
            pair_read[pr] = dve.done(nc.vector.tensor_tensor(lo, out, hi.bitcast(F32), ALU.subtract))
            newq[u, s + 1, hp] = (r, pair_read[pr])

        def out_product(u, s, hp):
            if hp == 0:
                pe.need(st["m"])
            pe.need(*newq[u, s + 1, hp], centred)
            for n_, m in enumerate((qh, ql)):
                for t in range(TB):
                    mm = nc.tensor.matmul(M[:, t * 2 * D:(t + 1) * 2 * D], m[qslot(u, s + 1)][:, hp, t * P:(t + 1) * P],
                                          wo[:, u % 2 * GP + hp, :, :].rearrange("p a d -> p (a d)"),
                                          start=(hp == 0 and n_ == 0 and t == 0), stop=(hp == GP - 1 and n_ == 1),
                                          skip_group_check=True)
            if hp == GP - 1:
                ydone[u, s] = pe.done(mm)

        def step_end(u, s):
            b, g = divmod(u, 2)
            dst = y[s][:, b * TB:(b + 1) * TB, :] if s < STEPS - 1 else \
                xnT[:, b * N:(b + 1) * N].rearrange("p (t d) -> p t d", d=D)
            Y4 = M.rearrange("p (t a d) -> p t a d", t=TB, a=2)
            dve.need(ydone[u, s])
            if g == 0:
                dve.chain(nc.vector.tensor_copy(dst, Y4[:, :, 0, :]))
            else:
                dve.chain(nc.vector.tensor_tensor(dst, dst, Y4[:, :, 0, :], ALU.add))
            st["m"] = dve.done(nc.vector.tensor_tensor(dst, dst, Y4[:, :, 1, :], ALU.add))

        def pair_move(i, u, s, h):
            hp = h // 2
            n_ = i // 2 % 2
            pool.need(newq[u, s + 1, hp][0], squared.get(i // 2 - 2))
            moved_by[u, s, hp] = pool.done(nc.gpsimd.tensor_tensor(move[n_][:, :], qf[fslot(u, s + 1)][:, hp, :],
                                                                   qf[fslot(u, s)][:, hp, :], ALU.subtract))

        def pair_square(i, u, s, h):
            hp = h // 2
            n_ = i // 2 % 2
            act.need(moved_by[u, s, hp])
            at_ = u * GP + hp
            squared[i // 2] = st["move"] = act.done(nc.scalar.activation(move[n_][:, :], move[n_][:, :], ACT.Square,
                                                                         accum_out=moved2[:, s, at_:at_ + 1]))

        for _, _, f in projections(0):
            f()
        order = [(u, s, h) for u in range(NU) for s in range(STEPS) for h in range(GH)]
        rounds = STEPS * GH
        todo = []
        for i in range(NI + 9):
            if i % rounds == 0 and i // rounds + 1 < NU:
                todo = projections(i // rounds + 1)

            def background(place):
                while todo and todo[0][0:2] <= (i % rounds, place):
                    todo.pop(0)[2]()

            if 4 <= i < NI + 4:
                turn(i - 4)
            if 2 <= i < NI + 2:
                norm(i - 2)
            if 1 <= i <= NI:
                exps(i - 1)
            if i >= 15 and i % GH == 7:
                step_end(*order[i - 15][0:2])
            background(0)
            if 4 <= i < NI + 4:
                move_out(i - 4)
            if i < NI:
                scores(i, *order[i])
            if 5 <= i < NI + 5:
                weigh(i - 5, *order[i - 5])
            if 6 <= i < NI + 6 and order[i - 6][2] % 2:
                pair_end(i - 6, *order[i - 6])
            background(1)
            if i >= 12 and i % GH in (4, 5, 6):
                for hp in {4: (0, 1), 5: (2,), 6: (3,)}[i % GH]:
                    out_product(*order[i - 12][0:2], hp)
            if 7 <= i < NI + 7 and order[i - 7][2] % 2 and order[i - 7][1] < STEPS - 1:
                pair_move(i - 7, *order[i - 7])
            if 9 <= i < NI + 9 and order[i - 9][2] % 2 and order[i - 9][1] < STEPS - 1:
                pair_square(i - 9, *order[i - 9])
            background(2)

        dve.need(st["move"])
        dve.chain(nc.vector.tensor_reduce(tot[:, :], moved2[:, :, :], AX.X, ALU.add))
        pe.need((dve.sem, dve.count), st["m"])
        r = pe.done(nc.tensor.matmul(M[:, 0:STEPS - 1], c.ones, tot[:, :], start=True, stop=True))
        dve.need(r)
        dve.chain(nc.vector.tensor_scalar(flag[:, :], M[:, 0:STEPS - 1], 1e-8, None, ALU.is_lt))
        y3 = xnT[:, :].rearrange("p (t d) -> p t d", d=D)
        for g in range(4):
            w_ = slice(g * 8, (g + 1) * 8)
            for s in range(STEPS - 2, -1, -1):
                m = flag[:, s:s + 1].unsqueeze(2).to_broadcast((P, 8, D))
                dve.chain(nc.vector.copy_predicated(y3[:, w_, :], m, y[s][:, w_, :]))
            store(g, dve.done(nc.vector.tensor_tensor(x[:, w_, :], x[:, w_, :], y3[:, w_, :], ALU.add)))
        c.stage(f"{name}_end")


def program(nc, a, const, out, layers=(0, 1, 2, 3)):
    c = Core(nc, a)
    with ExitStack() as ctx:
        sb = lambda k, s, dt=F32: ctx.enter_context(nc.sbuf_tensor(f"sb_{k}", s, dt))
        x, xnT = sb("x", [P, NT, D]), sb("xnT", [P, T])
        where, width = const_layout(const_columns())
        all_where, _ = const_layout(all_columns())
        c.const = lambda k: const[:, all_where[k][0]:all_where[k][0] + all_where[k][1]]
        kept = sb("kept", [P, 2, P])
        c.stage("start")
        early = ExitStack()
        eb = lambda k, s, dt=F32: early.enter_context(nc.sbuf_tensor(f"sb_{k}", s, dt))
        table = eb("table", [P, width])
        tab = lambda k: table[:, where[k][0]:where[k][0] + where[k][1]]
        c.ident, c.turn, c.ones = kept[:, 0, :], tab("turn"), kept[:, 1, :]
        xd = a["L0_attn_x"].rearrange("b (t p) d -> p (b t) d", p=P)
        kept_in = c.load("kept", (kept[:, 0, :], c.const("ident")), (kept[:, 1, :], c.const("ones")))
        x_in = [c.load(f"x{i}", (x[:, i * 8:(i + 1) * 8, :], xd[:, i * 8:(i + 1) * 8, :])) for i in range(4)]
        table_in = c.load("table", (table[:, :], const[:, 0:width]))

        if 0 in layers or 1 in layers:
            wsq, pairs = {}, []
            for k in ("L0_attn_Wq", "L0_attn_Wk", "L0_attn_Wv", "L0_attn_Wo",
                      "L1_attn_Wq", "L1_attn_Wk", "L1_attn_Wv", "L1_attn_W0"):
                wsq[k] = eb(k, [P, D])
                pairs.append((wsq[k][:, :], a[k]))
            wq8 = eb("wq8", [P, D // 4], mybir.dt.int32)
            pairs.append((wq8[:, :], a["L0_ffn_weight_q"]))
            rows = {}
            for k in ("L0_attn_bo", "L0_ffn_weight_scale", "L0_ffn_bias", "L1_attn_bv", "L1_attn_b0", "L1_ffn_b2"):
                rows[k] = eb(k, [P, D])
                pairs.append((rows[k][:, :], row(a[k])))
            bq, bk, b1 = eb("bq1", [P, 1]), eb("bk1", [P, 1]), eb("b1", [P, 4])
            pairs += [(bq[:, :], col(a["L1_attn_bq"])), (bk[:, :], col(a["L1_attn_bk"]))]
            pairs += [(b1[:, f:f + 1], col(a["L1_ffn_b1"][f * P:(f + 1) * P])) for f in range(4)]
            w1, w2 = eb("w1", [P, 4, D]), eb("w2", [P, 4 * P])
            pairs += [(w1[:, :, :], a["L1_ffn_W1"].rearrange("(t p) d -> p t d", p=P)), (w2[:, :], a["L1_ffn_W2"])]
            small_in = c.load("small", *pairs, eng=nc.scalar)
            mask400, future0, future1 = eb("mask400", [P, P], BF16), eb("fut0", [P, N], BF16), eb("fut1", [P, P], BF16)
            c.mask400, c.future0, c.future1 = mask400[:, :], future0[:, :], future1[:, :]
        experts_in = None
        if 2 in layers:
            w2l, pairs = {}, []
            for k in ("L2_attn_Wq", "L2_attn_Wk", "L2_attn_Wv", "L2_attn_Wo", "L2_ffn_Ws1", "L2_ffn_Ws3", "L2_ffn_Ws2"):
                w2l[k] = eb(k, [P, D])
                pairs.append((w2l[k][:, :], a[k]))
            for k in ("L2_attn_bq", "L2_attn_bk"):
                w2l[k] = eb(k, [P, 1])
                pairs.append((w2l[k][:, :], col(a[k])))
            for k in ("L2_attn_bv", "L2_attn_bo"):
                w2l[k] = eb(k, [P, D])
                pairs.append((w2l[k][:, :], row(a[k])))
            w2l["g"] = eb("wgate", [P, NE2])
            w1e, w3e, w2e = eb("w1e", [P, NE2, HID]), eb("w3e", [P, NE2, HID]), eb("w2e", [P, NE2 // 2, D])
            pairs += [(w2l["g"][:, :], a["L2_ffn_Wg"]),
                      (w1e[:, :, :], a["L2_ffn_W1"].rearrange("e d h -> d e h")),
                      (w3e[:, :, :], a["L2_ffn_W3"].rearrange("e d h -> d e h")),
                      (w2e[:, :, :], a["L2_ffn_W2"].rearrange("(q e) h d -> (e h) q d", e=2))]
            experts_in = c.load("experts", *pairs)
        for l in c.lanes:
            l.need(kept_in)
        if 0 not in layers:
            for l in c.lanes + [c.sp]:
                l.need(table_in, *x_in, *([small_in] if 1 in layers else []))
        c.stage("loaded")

        if 0 in layers:
            with nc.sbuf_tensor("xn", [P, NT, D], F32) as xn:
                norm_tiles(c, "norm0", x, xn, NT, xnT, biases=(rows["L0_attn_bo"][:, :], rows["L0_ffn_bias"][:, :]),
                           landed=x_in, bias_landed=small_in)
                c.dve.need(table_in)
                nc.vector.tensor_scalar(mask400[:, :], c.ident, 400.0, None, ALU.mult)
                nc.vector.tensor_copy(future0[:, :], tab("future0"))
                c.dve.done(nc.vector.tensor_copy(future1[:, :], tab("future1")))
                for l in c.lanes:
                    l.need(table_in, small_in)
                c.stage("ffn0")
                ffn_int8(c, "int8", x, xn, wq8[:, :].bitcast(I8), rows["L0_ffn_weight_scale"][:, :])
            attention8(c, "attn0", x, xnT, {k: wsq[f"L0_attn_W{k}"][:, :] for k in "qkvo"},
                       (tab("cos0"), tab("sin0")), 1.0 / HD8, None, True, True)
        if 1 in layers:
            norm_tiles(c, "norm1", x, None, NT, xnT, biases=(rows["L1_attn_b0"][:, :], rows["L1_ffn_b2"][:, :]))
            c.stage("attn1")
            w = {k: wsq[f"L1_attn_W{k}"][:, :] for k in "qkv"} | {"o": wsq["L1_attn_W0"][:, :]}
            attention8(c, "attn1", x, xnT, w, (tab("cos1"), tab("sin1")), float(np.float32(1.0) / np.sqrt(np.float32(HD8))),
                       {"q": bq[:, 0:1], "k": bk[:, 0:1], "v": rows["L1_attn_bv"][:, :]}, False, False)
            ffn_ternary(c, "tern", x, xnT, w1[:, :, :], b1, w2[:, :])
        if 2 in layers:
            for l in c.lanes:
                l.need(experts_in)
            norm_tiles(c, "norm2", x, None, NT, xnT, biases=(w2l["L2_attn_bo"][:, :],))
            c.stage("attn2")
            chunk_attention(c, "chunks", x, xnT, {k: w2l[f"L2_attn_W{k}"][:, :] for k in "qkvo"},
                            {k: w2l[f"L2_attn_b{k}"][:, 0:1] for k in "qk"}, w2l["L2_attn_bv"][:, :],
                            tab("own1"), tab("block"))
            with nc.sbuf_tensor("weightT", [NE2, T], F32) as weightT:
                route(c, "route", xnT, w2l["g"][:, :], tab("expert"), tab("before"), weightT)
                experts(c, "moe", x, xnT, weightT, w1e, w3e, w2e,
                        [w2l[f"L2_ffn_Ws{k}"][:, :] for k in (1, 3, 2)], tab("sel"))
        early.close()
        c.stage("late")
        yd = out.rearrange("b (t p) d -> p (b t) d", p=P)
        stored = nc.alloc_semaphore("stored")

        def store(g, ready):
            c.sp.need(ready)
            nc.sync.dma_start(yd[:, g * 8:(g + 1) * 8, :], x[:, g * 8:(g + 1) * 8, :]).then_inc(stored, 16)

        if 3 not in layers:
            for g in range(4):
                store(g, None)
            nc.sync.wait_ge(stored, 64)
        if 3 in layers:
            w3 = {k: sb(f"L3w{k}", [P, INNER]) for k in "qkv"}
            b3 = {k: sb(f"L3b{k}", [P, INNER]) for k in "qkv"}
            gam, bet = sb("gamma", [P, 1]), sb("beta", [P, 1])

            def load_attention():
                return c.load("attn3_w", *[(w3[k][:, :], a[f"L3_attn_W{k}"]) for k in "qkv"],
                              *[(b3[k][:, :], row(a[f"L3_attn_b{k}"])) for k in "qkv"],
                              *[(dst[HD3 * e:HD3 * (e + 1), :], col(a[k])) for e in range(2)
                                for dst, k in ((gam, "L3_attn_gamma"), (bet, "L3_attn_beta"))])

            with ExitStack() as late:
                lb = lambda k, s, dt=F32: late.enter_context(nc.sbuf_tensor(f"sb_{k}", s, dt))
                xl, xlT = lb("xl", [P, NT, D]), lb("xlT", [P, T])
                seT, se = lb("seT", [P, ES]), lb("se", [P, ES // P, D])
                wg, wu, wd = lb("wg", [P, E3, F3]), lb("wu", [P, E3, F3]), lb("wd", [P, E3, FK, D])
                bgu, bgT, buT = lb("bgu", [E3 * FK, 2, P]), lb("bgT", [P, E3 * FK]), lb("buT", [P, E3 * FK])
                bd = lb("bd", [P, E3 // 2, D])
                rows = {k: lb(k, [P, D]) for k in ("L3_ffn_norm_g", "L3_ffn_norm_b", "L3_ffn_slot_g", "L3_ffn_slot_b",
                                                   "L3_attn_bo")}
                sc = lb("scale", [P, 1])
                bdr = a["L3_ffn_bd"].rearrange("(q e) o -> e q o", e=2)
                slots_in = c.load("slots_w", (se[:, :, :], a["L3_ffn_slot_embeds"].rearrange("(q e) s d -> (e s) q d", e=2)),
                                  (sc[:, :], row(a["L3_ffn_scale"])), *[(v[:, :], row(a[k])) for k, v in rows.items()],
                                  (bgu[:, 0, :], a["L3_ffn_bg"].rearrange("e (f p) -> (e f) p", p=P)),
                                  (bgu[:, 1, :], a["L3_ffn_bu"].rearrange("e (f p) -> (e f) p", p=P)),
                                  (bd[0:SL, :, :], bdr[0].partition_broadcast(SL)),
                                  (bd[SL:P, :, :], bdr[1].partition_broadcast(SL)))
                ffn_in = c.load("ffn_w", (wg[:, :, :], a["L3_ffn_Wg"].rearrange("e d f -> d e f")),
                                (wu[:, :, :], a["L3_ffn_Wu"].rearrange("e d f -> d e f")),
                                *[(wd[:, :, f, :], a["L3_ffn_Wd"].rearrange("e (f p) o -> f p e o", p=P)[f]) for f in range(FK)])
                attn_in = load_attention()
                norm_tiles(c, "norm3", x, xl, NT, xnT, biases=(rows["L3_attn_bo"][:, :],), bias_landed=slots_in)
                for l in c.lanes:
                    l.need(slots_in)
                norm_tiles(c, "norm_ffn", xl, xl, NT, xlT, affine=(per_row(rows["L3_ffn_norm_g"]), per_row(rows["L3_ffn_norm_b"])))
                norm_tiles(c, "norm_slot", se, se, ES // P, None, affine=(per_row(rows["L3_ffn_slot_g"]), per_row(rows["L3_ffn_slot_b"])), groups=2)
                s = c.dve.done(nc.vector.tensor_scalar(se[:, :, :], se[:, :, :], sc[:, 0:1], None, ALU.mult))
                c.pe.need(s)
                for k in range(ES // P):
                    mm = nc.tensor.transpose(c.banks[k // 4][:, (k % 4) * P:(k % 4 + 1) * P], se[:, k, :], c.ident)
                for k in range(2):
                    nk = E3 * FK
                    mm = nc.tensor.transpose(c.banks[2][:, k * nk:(k + 1) * nk], bgu[:, k, :], c.ident[0:nk, 0:nk])
                c.dve.need(c.pe.done(mm))
                for k in range(2):
                    nc.vector.tensor_copy(seT[:, k * BANK:(k + 1) * BANK], c.banks[k])
                nc.vector.tensor_copy(bgT[:, :], c.banks[2][:, 0:nk])
                c.dve.done(nc.vector.tensor_copy(buT[:, :], c.banks[2][:, nk:2 * nk]))
                for l in c.lanes:
                    l.need(ffn_in)
                c.stage("slots")
                slot_experts(c, "slotmoe", x, xl, xlT, seT, wg, wu, wd, bgT, buT, bd)
            for l in c.lanes:
                l.need(attn_in)
            nc.scalar.preload_act_table_set("natural_log_exp_and_others")
            iterated_attention(c, "attn3", x, xnT, {k: v[:, :] for k, v in w3.items()}, a["L3_attn_Wo"],
                               {k: v[:, :] for k, v in b3.items()}, gam[:, 0:1], bet[:, 0:1], store)
            nc.sync.wait_ge(stored, 64)


def kernel(**inputs):
    import concourse.bacc as bacc
    from concourse.bass_utils import run_bass_kernel_spmd

    nc = bacc.Bacc("TRN2", target_bir_lowering=False, num_devices=1)
    arrays = {k: np.ascontiguousarray(v) for k, v in inputs.items()}
    arrays["L0_ffn_weight_q"] = arrays["L0_ffn_weight_q"].view(np.int32)
    arrays["const"] = np.concatenate(list(all_columns().values()), axis=1)
    aps = {k: nc.dram_tensor(f"in_{k}", v.shape, mybir.dt.from_np(v.dtype), kind="ExternalInput").ap()
           for k, v in arrays.items()}
    out = nc.dram_tensor("out", (B, N, D), F32, kind="ExternalOutput").ap()
    program(nc, aps, aps["const"], out)
    r = run_bass_kernel_spmd(nc, [{f"in_{k}": v for k, v in arrays.items()}], core_ids=[0])
    return r.results[0]["out"]
```
